# Optimizing a Trainium2 kernel written in Bass

```python
import numpy as np
import jax
import jax.numpy as jnp

def _softmax(x, axis=-1):
    return jax.nn.softmax(x, axis=axis)

def _gelu(x):
    return jax.nn.gelu(x, approximate=True)

def _silu(x):
    return jax.nn.silu(x)

def _sigmoid(x):
    return jax.nn.sigmoid(x)

def _layernorm(x, axis=-1, eps=1e-05):
    m = jnp.mean(x, axis=axis, keepdims=True)
    v = jnp.var(x, axis=axis, keepdims=True)
    return (x - m) / jnp.sqrt(v + eps)

def _scatter_add(tgt, idx, src, axis=0):
    return tgt.at[idx].add(src)

def _segment_sum(src, seg, n):
    return jax.ops.segment_sum(src, seg, n)
kernel_name = 'mk_hybrid_d1_jaxref_r8_264253'

def setup_inputs(seed: int=0):
    np.random.seed(seed)
    _w = jnp.asarray

    def _L0_attn_a_setup():
        import jax, jax.numpy as jnp
        import numpy as np
        D = 128
        H = 16
        HD = D // H
        K = 4
        B = 8
        S = 256
        SIZES = [D, D // 2, D, D, D, D, H, H, D]
        OFF = np.cumsum([0] + SIZES)

        def _dwconv_silu(x, w):
            s = x.shape[1]
            xp = jnp.pad(x, ((0, 0), (K - 1, 0), (0, 0)))
            y = sum((xp[:, j:j + s, :] * w[:, j] for j in range(K)))
            return jax.nn.silu(y)

        def _rmsnorm(x, w, eps=1e-06):
            return x * jax.lax.rsqrt(jnp.mean(x * x, axis=-1, keepdims=True) + eps) * w

        def _forward(hidden, W_ctrl, b_ctrl, W_block, qconv_w, kconv_w, vconv_w, rms_m_w, rms_v_w, W_out, b_out):
            b, s, _ = hidden.shape
            ctrl = hidden @ W_ctrl + b_ctrl
            parts = [ctrl[..., OFF[i]:OFF[i + 1]] for i in range(9)]
            ug_in, ang_in, cand_in, q_in, k_in, v_in, a_in, be_in, og_in = parts

            def heads(t):
                return t.reshape(b, s, H, HD)
            q = heads(_dwconv_silu(q_in, qconv_w))
            k = heads(_dwconv_silu(k_in, kconv_w))
            v = heads(_dwconv_silu(v_in, vconv_w))
            q = q * jax.lax.rsqrt(jnp.sum(q * q, axis=-1, keepdims=True) + 1e-12)
            k = k * jax.lax.rsqrt(jnp.sum(k * k, axis=-1, keepdims=True) + 1e-12)
            upd = jax.nn.sigmoid(ug_in)
            ret = 1.0 - upd
            cand = jax.nn.silu(cand_in)
            cos_a = jnp.cos(ang_in)
            sin_a = jnp.sin(ang_in)
            alpha = jax.nn.sigmoid(a_in)
            beta = jax.nn.sigmoid(be_in)
            tm = lambda t: jnp.moveaxis(t, 1, 0)
            xs = (tm(upd), tm(ret), tm(cand), tm(cos_a), tm(sin_a), tm(q), tm(k), tm(v), tm(alpha), tm(beta))
            vec0 = jnp.zeros((b, D), dtype=hidden.dtype)
            S0 = jnp.zeros((b, H, HD, HD), dtype=hidden.dtype)

            def step(carry, x):
                vec, St = carry
                u, r, c, ca, sa, qt, kt, vt, at, bt = x
                vp = jnp.einsum('bpi,pij->bpj', vec.reshape(b, D // 2, 2), W_block)
                x1, x2 = (vp[..., 0], vp[..., 1])
                rot = jnp.stack([x1 * ca - x2 * sa, x1 * sa + x2 * ca], axis=-1).reshape(b, D)
                vec_new = u * rot + r * c
                pred = jnp.einsum('bhij,bhi->bhj', St, kt)
                delta = vt - pred
                S_new = at[..., None, None] * St + bt[..., None, None] * (kt[..., :, None] * delta[..., None, :])
                read = jnp.einsum('bhij,bhi->bhj', S_new, qt)
                return ((vec_new, S_new), (vec_new, read))
            _, (vec_states, reads) = jax.lax.scan(step, (vec0, S0), xs)
            vec_states = jnp.moveaxis(vec_states, 0, 1)
            reads = jnp.moveaxis(reads, 0, 1)
            m = _rmsnorm(reads, rms_m_w).reshape(b, s, D)
            vread = _rmsnorm(vec_states, rms_v_w)
            gate = jax.nn.sigmoid(og_in)
            return (jnp.concatenate([m, vread], axis=-1) @ W_out + b_out) * gate
        key = jax.random.key(seed)
        ks = jax.random.split(key, 10)
        tot = int(OFF[-1])
        W_ctrl = jax.random.normal(ks[0], (D, tot), dtype=jnp.float32) / np.sqrt(D)
        b = np.zeros(tot, np.float32)
        b[OFF[6]:OFF[7]] = 1.5
        b[OFF[7]:OFF[8]] = -2.0
        b[OFF[8]:OFF[9]] = -1.5
        b_ctrl = jnp.asarray(b)
        W_block = jax.random.normal(ks[1], (D // 2, 2, 2), dtype=jnp.float32) * 0.1

        def conv_w(k):
            w = jax.random.normal(k, (D, K), dtype=jnp.float32) * 0.02
            return w.at[:, -1].add(1.0)
        qconv_w = conv_w(ks[2])
        kconv_w = conv_w(ks[3])
        vconv_w = conv_w(ks[4])
        rms_m_w = jnp.ones((HD,), dtype=jnp.float32)
        rms_v_w = jnp.ones((D,), dtype=jnp.float32)
        W_out = jax.random.normal(ks[5], (2 * D, D), dtype=jnp.float32) * 0.02
        b_out = jnp.zeros((D,), dtype=jnp.float32)
        hidden = jax.random.normal(ks[6], (B, S, D), dtype=jnp.float32)
        return {'hidden': hidden, 'W_ctrl': W_ctrl, 'b_ctrl': b_ctrl, 'W_block': W_block, 'qconv_w': qconv_w, 'kconv_w': kconv_w, 'vconv_w': vconv_w, 'rms_m_w': rms_m_w, 'rms_v_w': rms_v_w, 'W_out': W_out, 'b_out': b_out}
    _L0_attn_a_in = _L0_attn_a_setup()

    def _L0_attn_b_setup():
        import jax, jax.numpy as jnp
        import numpy as np
        EPS = 1e-08
        key = jax.random.key(seed)
        k0, k1, k2, k3 = jax.random.split(key, 4)
        B, S, D = (8, 256, 128)
        scale = 1.0 / np.sqrt(D)
        x = jax.random.normal(k0, (B, S, D), dtype=jnp.float32)
        Wq = jax.random.normal(k1, (D, D), dtype=jnp.float32) * scale
        Wk = jax.random.normal(k2, (D, D), dtype=jnp.float32) * scale
        Wv = jax.random.normal(k3, (D, D), dtype=jnp.float32) * scale
        return {'x': x, 'Wq': Wq, 'Wk': Wk, 'Wv': Wv}
    _L0_attn_b_in = _L0_attn_b_setup()

    def _L0_ffn_setup():
        import jax, jax.numpy as jnp
        import numpy as np
        DIM = 128
        HEADS = 16
        HD = DIM // HEADS
        M = 32
        E = 4
        K = 2
        HID = 256
        MID = 256
        LB = 0.01
        EPS = 1.1920929e-07

        def _rms(x, w):
            return x * jax.lax.rsqrt(jnp.mean(x * x, axis=-1, keepdims=True) + EPS) * w

        def _gelu(x):
            return jax.nn.gelu(x, approximate=False)
        key = jax.random.key(seed)
        ks = jax.random.split(key, 20)
        d = DIM
        w = lambda k, s: jax.random.normal(k, s, jnp.float32) * 0.02
        return {'x': jax.random.normal(ks[0], (4, 128, d), jnp.float32), 'n1_w': jnp.ones((d,), jnp.float32), 'n2_w': jnp.ones((d,), jnp.float32), 'wq': w(ks[1], (d, d)), 'wk': w(ks[2], (d, d)), 'wv': w(ks[3], (d, d)), 'wo': w(ks[4], (d, d)), 'qn_w': jnp.ones((HD,), jnp.float32), 'kn_w': jnp.ones((HD,), jnp.float32), 'gate_w': w(ks[5], (E, d)), 'e0_up': w(ks[6], (HID, d)), 'e0_down': w(ks[7], (d, HID)), 'e1_w1': w(ks[8], (HID, d)), 'e1_w2': w(ks[9], (HID, d)), 'e1_down': w(ks[10], (d, HID)), 'e2_l1': w(ks[11], (MID, d)), 'e2_l2': w(ks[12], (HID, MID)), 'e2_l3': w(ks[13], (MID, HID)), 'e2_l4': w(ks[14], (d, MID)), 'e3_down': w(ks[15], (d, d)), 'e3_up': w(ks[16], (HID, d)), 'e3_out': w(ks[17], (d, HID))}
    _L0_ffn_in = _L0_ffn_setup()
    _d = {'L0_attn_a_hidden': _L0_attn_a_in['hidden'], 'L0_attn_a_W_ctrl': _L0_attn_a_in['W_ctrl'], 'L0_attn_a_b_ctrl': _L0_attn_a_in['b_ctrl'], 'L0_attn_a_W_block': _L0_attn_a_in['W_block'], 'L0_attn_a_qconv_w': _L0_attn_a_in['qconv_w'], 'L0_attn_a_kconv_w': _L0_attn_a_in['kconv_w'], 'L0_attn_a_vconv_w': _L0_attn_a_in['vconv_w'], 'L0_attn_a_rms_m_w': _L0_attn_a_in['rms_m_w'], 'L0_attn_a_rms_v_w': _L0_attn_a_in['rms_v_w'], 'L0_attn_a_W_out': _L0_attn_a_in['W_out'], 'L0_attn_a_b_out': _L0_attn_a_in['b_out'], 'L0_attn_b_Wq': _L0_attn_b_in['Wq'], 'L0_attn_b_Wk': _L0_attn_b_in['Wk'], 'L0_attn_b_Wv': _L0_attn_b_in['Wv'], 'L0_ffn_n1_w': _L0_ffn_in['n1_w'], 'L0_ffn_n2_w': _L0_ffn_in['n2_w'], 'L0_ffn_wq': _L0_ffn_in['wq'], 'L0_ffn_wk': _L0_ffn_in['wk'], 'L0_ffn_wv': _L0_ffn_in['wv'], 'L0_ffn_wo': _L0_ffn_in['wo'], 'L0_ffn_qn_w': _L0_ffn_in['qn_w'], 'L0_ffn_kn_w': _L0_ffn_in['kn_w'], 'L0_ffn_gate_w': _L0_ffn_in['gate_w'], 'L0_ffn_e0_up': _L0_ffn_in['e0_up'], 'L0_ffn_e0_down': _L0_ffn_in['e0_down'], 'L0_ffn_e1_w1': _L0_ffn_in['e1_w1'], 'L0_ffn_e1_w2': _L0_ffn_in['e1_w2'], 'L0_ffn_e1_down': _L0_ffn_in['e1_down'], 'L0_ffn_e2_l1': _L0_ffn_in['e2_l1'], 'L0_ffn_e2_l2': _L0_ffn_in['e2_l2'], 'L0_ffn_e2_l3': _L0_ffn_in['e2_l3'], 'L0_ffn_e2_l4': _L0_ffn_in['e2_l4'], 'L0_ffn_e3_down': _L0_ffn_in['e3_down'], 'L0_ffn_e3_up': _L0_ffn_in['e3_up'], 'L0_ffn_e3_out': _L0_ffn_in['e3_out']}
    _x0 = _d['L0_attn_a_hidden']
    _d['L0_attn_a_hidden'] = jax.random.normal(jax.random.fold_in(jax.random.key(seed), 1), (2, 1024, 128), dtype=_x0.dtype)
    del _x0
    return _d

def reference(L0_attn_a_hidden, L0_attn_a_W_ctrl, L0_attn_a_b_ctrl, L0_attn_a_W_block, L0_attn_a_qconv_w, L0_attn_a_kconv_w, L0_attn_a_vconv_w, L0_attn_a_rms_m_w, L0_attn_a_rms_v_w, L0_attn_a_W_out, L0_attn_a_b_out, L0_attn_b_Wq, L0_attn_b_Wk, L0_attn_b_Wv, L0_ffn_n1_w, L0_ffn_n2_w, L0_ffn_wq, L0_ffn_wk, L0_ffn_wv, L0_ffn_wo, L0_ffn_qn_w, L0_ffn_kn_w, L0_ffn_gate_w, L0_ffn_e0_up, L0_ffn_e0_down, L0_ffn_e1_w1, L0_ffn_e1_w2, L0_ffn_e1_down, L0_ffn_e2_l1, L0_ffn_e2_l2, L0_ffn_e2_l3, L0_ffn_e2_l4, L0_ffn_e3_down, L0_ffn_e3_up, L0_ffn_e3_out):

    def _L0_attn_a_ref(hidden, W_ctrl, b_ctrl, W_block, qconv_w, kconv_w, vconv_w, rms_m_w, rms_v_w, W_out, b_out):
        import jax, jax.numpy as jnp
        import numpy as np
        D = 128
        H = 16
        HD = D // H
        K = 4
        B = 8
        S = 256
        SIZES = [D, D // 2, D, D, D, D, H, H, D]
        OFF = np.cumsum([0] + SIZES)

        def _dwconv_silu(x, w):
            s = x.shape[1]
            xp = jnp.pad(x, ((0, 0), (K - 1, 0), (0, 0)))
            y = sum((xp[:, j:j + s, :] * w[:, j] for j in range(K)))
            return jax.nn.silu(y)

        def _rmsnorm(x, w, eps=1e-06):
            return x * jax.lax.rsqrt(jnp.mean(x * x, axis=-1, keepdims=True) + eps) * w

        def _forward(hidden, W_ctrl, b_ctrl, W_block, qconv_w, kconv_w, vconv_w, rms_m_w, rms_v_w, W_out, b_out):
            b, s, _ = hidden.shape
            ctrl = hidden @ W_ctrl + b_ctrl
            parts = [ctrl[..., OFF[i]:OFF[i + 1]] for i in range(9)]
            ug_in, ang_in, cand_in, q_in, k_in, v_in, a_in, be_in, og_in = parts

            def heads(t):
                return t.reshape(b, s, H, HD)
            q = heads(_dwconv_silu(q_in, qconv_w))
            k = heads(_dwconv_silu(k_in, kconv_w))
            v = heads(_dwconv_silu(v_in, vconv_w))
            q = q * jax.lax.rsqrt(jnp.sum(q * q, axis=-1, keepdims=True) + 1e-12)
            k = k * jax.lax.rsqrt(jnp.sum(k * k, axis=-1, keepdims=True) + 1e-12)
            upd = jax.nn.sigmoid(ug_in)
            ret = 1.0 - upd
            cand = jax.nn.silu(cand_in)
            cos_a = jnp.cos(ang_in)
            sin_a = jnp.sin(ang_in)
            alpha = jax.nn.sigmoid(a_in)
            beta = jax.nn.sigmoid(be_in)
            tm = lambda t: jnp.moveaxis(t, 1, 0)
            xs = (tm(upd), tm(ret), tm(cand), tm(cos_a), tm(sin_a), tm(q), tm(k), tm(v), tm(alpha), tm(beta))
            vec0 = jnp.zeros((b, D), dtype=hidden.dtype)
            S0 = jnp.zeros((b, H, HD, HD), dtype=hidden.dtype)

            def step(carry, x):
                vec, St = carry
                u, r, c, ca, sa, qt, kt, vt, at, bt = x
                vp = jnp.einsum('bpi,pij->bpj', vec.reshape(b, D // 2, 2), W_block)
                x1, x2 = (vp[..., 0], vp[..., 1])
                rot = jnp.stack([x1 * ca - x2 * sa, x1 * sa + x2 * ca], axis=-1).reshape(b, D)
                vec_new = u * rot + r * c
                pred = jnp.einsum('bhij,bhi->bhj', St, kt)
                delta = vt - pred
                S_new = at[..., None, None] * St + bt[..., None, None] * (kt[..., :, None] * delta[..., None, :])
                read = jnp.einsum('bhij,bhi->bhj', S_new, qt)
                return ((vec_new, S_new), (vec_new, read))
            _, (vec_states, reads) = jax.lax.scan(step, (vec0, S0), xs)
            vec_states = jnp.moveaxis(vec_states, 0, 1)
            reads = jnp.moveaxis(reads, 0, 1)
            m = _rmsnorm(reads, rms_m_w).reshape(b, s, D)
            vread = _rmsnorm(vec_states, rms_v_w)
            gate = jax.nn.sigmoid(og_in)
            return (jnp.concatenate([m, vread], axis=-1) @ W_out + b_out) * gate
        return _forward(hidden, W_ctrl, b_ctrl, W_block, qconv_w, kconv_w, vconv_w, rms_m_w, rms_v_w, W_out, b_out)

    def _L0_attn_b_ref(x, Wq, Wk, Wv):
        import jax, jax.numpy as jnp
        import numpy as np
        EPS = 1e-08
        D = x.shape[-1]
        q = jnp.einsum('bsd,ed->bse', x, Wq)
        k = jnp.einsum('bsd,ed->bse', x, Wk)
        v = jnp.einsum('bsd,ed->bse', x, Wv)
        fk = jnp.fft.rfft(k, axis=-1)
        fk = fk / (jnp.abs(fk) + EPS)
        fq = jnp.fft.rfft(q, axis=-1)
        fq = fq / (jnp.abs(fq) + EPS)
        fv = jnp.fft.rfft(v, axis=-1)
        fkv = jnp.cumsum(fk * fv, axis=-2)
        values_hat = jnp.fft.irfft(fkv * jnp.conj(fq), n=D, axis=-1)
        return x + values_hat

    def _L0_ffn_ref(x, n1_w, n2_w, wq, wk, wv, wo, qn_w, kn_w, gate_w, e0_up, e0_down, e1_w1, e1_w2, e1_down, e2_l1, e2_l2, e2_l3, e2_l4, e3_down, e3_up, e3_out):
        import jax, jax.numpy as jnp
        import numpy as np
        DIM = 128
        HEADS = 16
        HD = DIM // HEADS
        M = 32
        E = 4
        K = 2
        HID = 256
        MID = 256
        LB = 0.01
        EPS = 1.1920929e-07

        def _rms(x, w):
            return x * jax.lax.rsqrt(jnp.mean(x * x, axis=-1, keepdims=True) + EPS) * w

        def _gelu(x):
            return jax.nn.gelu(x, approximate=False)
        B, T, C = x.shape
        h = _rms(x, n1_w)
        heads = lambda w_: (h @ w_.T).reshape(B, T, HEADS, HD).transpose(0, 2, 1, 3)
        q = _rms(heads(wq), qn_w)
        k = _rms(heads(wk), kn_w)
        v = heads(wv)
        scores = jnp.einsum('bhqd,bhkd->bhqk', q, k) * HD ** (-0.5)
        causal = jnp.tril(jnp.ones((T, T), bool))
        scores = jnp.where(causal[None, None], scores, -jnp.inf)
        attn = jax.nn.softmax(scores, axis=-1)
        ao = jnp.einsum('bhqk,bhkd->bhqd', attn, v).transpose(0, 2, 1, 3).reshape(B, T, C) @ wo.T
        ao = ao.at[:, :, :M].set(0.0)
        x = x + ao
        xf = _rms(x, n2_w).reshape(-1, C)
        N = xf.shape[0]
        logits = jnp.nan_to_num(xf @ gate_w.T)
        probs = jax.nn.softmax(logits, axis=-1)
        topv, topi = jax.lax.top_k(probs, K)
        topv = topv / (topv.sum(-1, keepdims=True) + 1e-08)
        wts = jnp.zeros((N, E), x.dtype).at[jnp.arange(N)[:, None], topi].add(topv)
        o0 = _gelu(xf @ e0_up.T) @ e0_down.T
        o1 = jax.nn.silu(xf @ e1_w1.T) * (xf @ e1_w2.T) @ e1_down.T
        o2 = _gelu(_gelu(_gelu(xf @ e2_l1.T) @ e2_l2.T) @ e2_l3.T) @ e2_l4.T
        o3 = _gelu(_gelu(xf @ e3_down.T) @ e3_up.T) @ e3_out.T
        moe = wts[:, 0:1] * o0 + wts[:, 1:2] * o1 + wts[:, 2:3] * o2 + wts[:, 3:4] * o3
        moe = moe.reshape(B, T, C).at[:, :, :M].set(0.0)
        return x + moe
    x = L0_attn_a_hidden
    x = x + _L0_attn_a_ref(_layernorm(x, axis=-1), L0_attn_a_W_ctrl, L0_attn_a_b_ctrl, L0_attn_a_W_block, L0_attn_a_qconv_w, L0_attn_a_kconv_w, L0_attn_a_vconv_w, L0_attn_a_rms_m_w, L0_attn_a_rms_v_w, L0_attn_a_W_out, L0_attn_a_b_out)
    x = x + _L0_ffn_ref(_layernorm(x, axis=-1), L0_ffn_n1_w, L0_ffn_n2_w, L0_ffn_wq, L0_ffn_wk, L0_ffn_wv, L0_ffn_wo, L0_ffn_qn_w, L0_ffn_kn_w, L0_ffn_gate_w, L0_ffn_e0_up, L0_ffn_e0_down, L0_ffn_e1_w1, L0_ffn_e1_w2, L0_ffn_e1_down, L0_ffn_e2_l1, L0_ffn_e2_l2, L0_ffn_e2_l3, L0_ffn_e2_l4, L0_ffn_e3_down, L0_ffn_e3_up, L0_ffn_e3_out)
    x = x + _L0_attn_b_ref(_layernorm(x, axis=-1), L0_attn_b_Wq, L0_attn_b_Wk, L0_attn_b_Wv)
    x = x + _L0_ffn_ref(_layernorm(x, axis=-1), L0_ffn_n1_w, L0_ffn_n2_w, L0_ffn_wq, L0_ffn_wk, L0_ffn_wv, L0_ffn_wo, L0_ffn_qn_w, L0_ffn_kn_w, L0_ffn_gate_w, L0_ffn_e0_up, L0_ffn_e0_down, L0_ffn_e1_w1, L0_ffn_e1_w2, L0_ffn_e1_down, L0_ffn_e2_l1, L0_ffn_e2_l2, L0_ffn_e2_l3, L0_ffn_e2_l4, L0_ffn_e3_down, L0_ffn_e3_up, L0_ffn_e3_out)
    return x

_drawn_inputs = setup_inputs


def setup_inputs(seed=0):
    import zlib

    import numpy as np

    out = dict(_drawn_inputs(seed))
    spreads = {'L0_attn_a_rms_m_w': (1.0, 0.2),
     'L0_attn_a_rms_v_w': (1.0, 0.2),
     'L0_attn_a_b_out': (0.0, 0.1),
     'L0_ffn_n1_w': (1.0, 0.6),
     'L0_ffn_n2_w': (1.0, 0.6),
     'L0_ffn_qn_w': (1.0, 0.6),
     'L0_ffn_kn_w': (1.0, 0.6)}
    factors = {'L0_attn_a_W_block': 3.077,
     'L0_ffn_wq': 5.19,
     'L0_ffn_wk': 5.179,
     'L0_ffn_wv': 5.3,
     'L0_ffn_wo': 4.82,
     'L0_ffn_gate_w': 4.237,
     'L0_ffn_e0_up': 3.336,
     'L0_ffn_e0_down': 3.039,
     'L0_ffn_e1_w1': 8.0,
     'L0_ffn_e1_w2': 8.0,
     'L0_ffn_e1_down': 8.0,
     'L0_ffn_e2_l1': 8.0,
     'L0_ffn_e2_l2': 8.0,
     'L0_ffn_e2_l3': 8.0,
     'L0_ffn_e2_l4': 8.0,
     'L0_ffn_e3_down': 8.0,
     'L0_ffn_e3_up': 8.0,
     'L0_ffn_e3_out': 8.0}
    for name, (base, spread) in spreads.items():
        noise = np.random.default_rng([zlib.crc32(name.encode()), seed]).standard_normal(out[name].shape)
        drawn = base * np.exp(spread * noise) if base else spread * noise
        out[name] = jnp.asarray(drawn.astype(out[name].dtype))
    for name, factor in factors.items():
        out[name] = (out[name] * factor).astype(out[name].dtype)
    return out
```

```python
from contextlib import ExitStack

import concourse.bass as bass
from concourse import mybir

ALU = mybir.AluOpType
ACT = mybir.ActivationFunctionType
AX = mybir.AxisListType
F32 = mybir.dt.float32
BF16 = mybir.dt.bfloat16

P = 128
B, S, D = 2, 1024, 128
NT = B * S
TILES = NT // P
TB = TILES // B
H, HD = 16, 8
SEG, C = 4, 16
BH = B * H
ST = S // SEG
NC = ST // C
CH = 512
NCH = NT // CH
TPC = CH // P
NB = D // 2 + 1
KEEP = 32
OUTC = D - KEEP
HID = 256
E4 = 4
LN_EPS, A_EPS, L2_EPS, B_EPS, F_EPS = 1e-5, 1e-6, 1e-12, 1e-8, 1.1920929e-07
TOP_EPS = 1e-8
SHIFT = 80.0
FLT_MAX = 3.4028234663852886e38
MASKED = -1.0e30
MAGIC = 12582912.0
TWO_PI = 6.283185307179586
TWO_PI_HI = 6.28125
PI = 3.1415925

A_Q, A_K, A_V, A_UE, A_UO, A_CE, A_CO, A_ANG, A_OG, A_COLS = 0, 128, 256, 384, 448, 512, 576, 640, 704, 832
S_BQKV, S_CONV, S_BPAIR, S_WB, S_BAB, S_RMS, S_COLS = 0, 3, 15, 20, 24, 26, 29
F_QKV, F_GATE, F_E0, F_E1A, F_E1B, F_E2, F_E3, F_COLS = 0, 384, 388, 644, 900, 1156, 1412, 1540
Q_SIDE = (0, 1, 0, 1, 2, 0)
K_SIDE = (0, 0, 1, 1, 0, 2)
NSLOT = len(Q_SIDE)
QROWS = NSLOT * HD + 1
GH = 4
NG = H // GH


class Tally:

    def __init__(self, eng, sem):
        self.eng, self.sem, self.n = eng, sem, 0

    def wait(self, more=1):
        self.n = self.n + more
        self.eng.wait_ge(self.sem, self.n)


class Chain:

    def __init__(self, eng, sem):
        self.eng, self.sem, self.n = eng, sem, 0

    def __call__(self, ins):
        self.open(ins)
        self.close()

    def open(self, ins):
        ins.then_inc(self.sem, 1)
        self.n = self.n + 1

    def close(self):
        self.eng.wait_ge(self.sem, self.n)


def hybrid_kernel(nc, x, a_w, a_wab, a_small, a_bog, a_bout, a_wout, b_w, b_dft, b_idft,
                  f_w, f_n, f_qk, f_mid, f_down, f_wo, eye, causal, out):
    ctx = ExitStack()
    with ctx:
        def sem(name):
            return ctx.enter_context(nc.semaphore(name))

        def sb(name, shape, dt=F32, at=None):
            return (at or ctx).enter_context(nc.sbuf_tensor(name, shape, dt))

        def dram(name, shape, dt=F32):
            return nc.dram_tensor(name, shape, dt, kind="Internal").ap()

        X = sb("X", [P, TILES, D])
        XL = sb("XL", [P, TILES, D])
        SQ = sb("SQ", [P, TILES, D])
        HT = sb("HT", [P, NT])
        ident = sb("ident", [P, P])
        stat = sb("stat", [P, TILES])
        var = sb("var", [P, TILES])
        rstd = sb("rstd", [P, TILES])
        rrms = sb("rrms", [P, TILES])
        PS = ctx.enter_context(nc.psum_tensor("PS", [P, 8, CH], F32))

        with ExitStack() as sa:
            aw = sb("aw", [P, A_COLS], at=sa)
            awab = sb("awab", [P, 4, 32], at=sa)
            asm = sb("asm", [P, S_COLS], at=sa)
            nwb = sb("nwb", [P, 4], at=sa)
            abog = sb("abog", [P, D], at=sa)
            about = sb("about", [P, D], at=sa)
            awout = sb("awout", [P, 3, D], at=sa)
            ones = sb("ones", [P, 1], at=sa)
            ALP = sb("ALP", [P, ST], at=sa)
            BET = sb("BET", [P, ST], at=sa)
            V0 = sb("V0", [P, 2, S], at=sa)
            LQK = sb("LQK", [P, 2, HD, ST], at=sa)
            WU = sb("WU", [P, 2 * HD, ST], at=sa)
            with ExitStack() as s1:
                CQ = [sb(f"CQ{i}", [P, B, S + 3], at=s1) for i in range(2)]
                CY = [sb(f"CY{i}", [P, B, S], at=s1) for i in range(2)]
                UEO = sb("UEO", [P, 2, S], at=s1)
                ANG = sb("ANG", [P, S], at=s1)
                SIN = sb("SIN", [P, S], at=s1)
                COS = sb("COS", [P, S], at=s1)
                TRA = [sb(f"TRA{l}", [P, 2, 3, S >> l], at=s1) for l in range(11)]
                TRV = [V0] + [sb(f"TRV{l}", [P, 2, S >> l], at=s1) for l in range(1, 11)]
                TRT = sb("TRT", [P, 2, 3, S // 2], at=s1)
            with ExitStack() as s23:
                KB = sb("KB", [P, HD, ST], at=s23)
                PA = sb("PA", [P, NC, C, C], at=s23)
                AC1 = sb("AC1", [P, NC], at=s23)
                VS = sb("VS", [P, 2, S], at=s23)
                with ExitStack() as s2:
                    GAM = sb("GAM", [P, NC, C + 1, C + 1], at=s2)
                    SS = sb("SS", [P, 2, ST], at=s2)
                    RS = sb("RS", [P, 2, ST], at=s2)
                    NG0 = sb("NG0", [P, ST], at=s2)
                    LA = sb("LA", [P, NC, C, C], at=s2)
                    PRD = sb("PRD", [P, 2 * HD * ST], at=s2)
                    PRP = [sb(f"PRP{i}", [P, HD * ST], at=s2) for i in range(2)]
                with ExitStack() as s3:
                    W2 = sb("W2", [P, SEG, HD, ST], at=s3)
                    K2 = sb("K2", [P, SEG, HD, ST], at=s3)
                    U2 = sb("U2", [P, SEG, 2, ST], at=s3)
                    D2 = sb("D2", [P, SEG, 2, ST], at=s3)
                    S2 = sb("S2", [P, SEG * NC + 1, 2, HD], at=s3)
                    AC2 = sb("AC2", [P, SEG, NC], at=s3)
                    P1 = sb("P1", [P, 2, 2, C, HD + 1], at=s3)
                    P2 = sb("P2", [P, 2, HD, C + 1], at=s3)
                with ExitStack() as s4:
                    DJ = sb("DJ", [P, HD, ST], at=s4)
                    SJ = sb("SJ", [P, 4, NC, 2, HD], at=s4)
                    RO = sb("RO", [P, HD, ST], at=s4)
                    RP = sb("RP", [P, HD, ST], at=s4)
                    PRR = sb("PRR", [P, NC * C * HD], at=s4)
                    PRQ = [sb(f"PRQ{i}", [P, NC * HD * C], at=s4) for i in range(2)]
                    RT = sb("RT", [P, B, S], at=s4)
                    SS4 = sb("SS4", [P, ST], at=s4)
                    OT = sb("OT", [P, TILES, D], at=s4)
                    vss = sb("vss", [P, TILES], at=s4)
        qkv_d = dram("qkv_d", (3, B, D, S))
        w_d = dram("w_d", (SEG, BH, HD, ST))
        k_d = dram("k_d", (SEG, BH, HD, ST))
        u_d = dram("u_d", (SEG, BH, HD, ST))
        ac_d = dram("ac_d", (SEG, BH, NC))
        d_d = dram("d_d", (SEG, BH, HD, ST))
        s_d = dram("s_d", (SEG, BH, 4, NC * 2 * HD))
        r_d = dram("r_d", (BH, HD, S))

        with ExitStack() as sw:
            bw = sb("bw", [P, 3, D], at=sw)
            bdft = sb("bdft", [P, 2, NB], at=sw)
            bidft = sb("bidft", [P, 2, D], at=sw)
            bwf = sb("bwf", [P, 3, 2, NB], at=sw)
            identb = sb("identb", [P, P], BF16, at=sw)
            maskb = sb("maskb", [P, P], BF16, at=sw)
            maskf = sb("maskf", [P, P], at=sw)
            fw = sb("fw", [P, F_COLS], at=sw)
            fn = sb("fn", [P, 2], at=sw)
            fqk = sb("fqk", [P, 2, HD], at=sw)
            kwmax = sb("kwmax", [P, 1], at=sw)
            fmid = sb("fmid", [P, 5, HID], at=sw)
            fdown = sb("fdown", [P, E4, 2, OUTC], at=sw)
            fwo = sb("fwo", [P, NG, OUTC], at=sw)
            KS = [sb(f"KS{i}", [P, GH, S], BF16, at=sw) for i in range(2)]
            QS = [sb(f"QS{i}", [P, GH, S], BF16, at=sw) for i in range(2)]
            VA = [sb(f"VA{i}", [P, TB, GH, 32], at=sw) for i in range(2)]
            with ExitStack() as sB:
                QF = sb("QF", [P, 3, 2, CH], at=sB)
                QF2 = sb("QF2", [P, 2, 2, CH], at=sB)
                mag = sb("mag", [P, 2, CH], at=sB)
                PRB = sb("PRB", [P, 4, CH], at=sB)
                CUM = sb("CUM", [P, 2, B, S], at=sB)
                YF = sb("YF", [P, 2, NT], at=sB)
            with ExitStack() as sF:
                QKV = sb("QKV", [P, TILES, 3 * D], at=sF)
                PX = [sb(f"PX{i}", [P, 2, CH], at=sF) for i in range(3)]
                DEN = sb("DEN", [P, CH], at=sF)
                AO = sb("AO", [P, NG, NT], at=sF)
                with ExitStack() as f1:
                    QKS = sb("QKS", [P, TILES, 2 * D], at=f1)
                    qst = sb("qst", [P, TILES, 2 * H], at=f1)
                    qst2 = sb("qst2", [P, TILES, 2 * H], at=f1)
                    MT = sb("MT", [H, NT], BF16, at=f1)
                    QP = [sb(f"QP{i}", [P, 2, CH], BF16, at=f1) for i in range(3)]
                    QR = sb("QR", [P, 2, CH], at=f1)
                with ExitStack() as f3:
                    lg = sb("lg", [P, TILES, E4], at=f3)
                    pr = sb("pr", [P, TILES, E4], at=f3)
                    cnt = sb("cnt", [P, TILES, E4], at=f3)
                    ge = sb("ge", [P, TILES], at=f3)
                    red = sb("red", [P, TILES], at=f3)
                    wts = sb("wts", [P, TILES, E4], at=f3)
                    HG = [sb(f"HG{i}", [P, 2, CH], at=f3) for i in range(2)]
                    H0 = sb("H0", [P, 2, CH], at=f3)
                    HA = sb("HA", [P, 2, CH], at=f3)
                    HB = sb("HB", [P, 2, CH], at=f3)
                    HC = sb("HC", [P, 2, CH], at=f3)
                    HE = sb("HE", [P, CH], at=f3)
                    HF = sb("HF", [P, 2, CH], at=f3)
        qs_d = dram("qs_d", (H, QROWS, NT), BF16)
        ks_d = dram("ks_d", (H, QROWS, NT), BF16)


        psum_read = sem("psum_read")
        psum_full = sem("psum_full")
        to_act = sem("to_act")
        normed = sem("normed")
        to_dve = sem("to_dve")
        x_loaded = sem("x_loaded")
        a_loaded = sem("a_loaded")
        silu_done = sem("silu_done")
        qkv_stored = sem("qkv_stored")
        lanes_loaded = sem("lanes_loaded")
        wk_ready = sem("wk_ready")
        wk_stored = sem("wk_stored")
        u_solved = sem("u_solved")
        u_stored = sem("u_stored")
        seg_loaded = [sem(f"seg_loaded{i}") for i in range(SEG)]
        chunk_done = sem("chunk_done")
        ds_stored = sem("ds_stored")
        ds_loaded = sem("ds_loaded")
        reads_ready = sem("reads_ready")
        reads_stored = sem("reads_stored")
        rt_loaded = sem("rt_loaded")
        wout_ready = sem("wout_ready")
        vs_ready = sem("vs_ready")
        trig_in = sem("trig_in")
        trig_ready = sem("trig_ready")
        conv_done = sem("conv_done")
        pads_clear = sem("pads_clear")
        gate_ready = sem("gate_ready")
        state_clear = sem("state_clear")
        u_slot = sem("u_slot")
        s_slot = sem("s_slot")
        tree_in = sem("tree_in")
        lanes_clear = sem("lanes_clear")
        kb_ready = sem("kb_ready")
        prod_ready = sem("prod_ready")
        prod_used = sem("prod_used")
        la_ready = sem("la_ready")
        rprod_ready = sem("rprod_ready")
        rprod_used = sem("rprod_used")
        x_ready = sem("x_ready")
        w_loaded = sem("w_loaded")
        y_ready = sem("y_ready")
        stack_clear = sem("stack_clear")
        parts_ready = sem("parts_ready")
        parts_stored = sem("parts_stored")
        shift_stored = sem("shift_stored")
        stack_loaded = [sem(f"stack_loaded{i}") for i in range(B)]
        probs_used = sem("probs_used")
        v_ready = sem("v_ready")
        fw_ready = sem("fw_ready")
        qk_normed = sem("qk_normed")
        shifts_ready = sem("shifts_ready")
        probs_ready = sem("probs_ready")
        scores_ready = sem("scores_ready")
        o_read = sem("o_read")
        h1_ready = sem("h1_ready")
        up_full = sem("up_full")
        down_read = sem("down_read")
        down_full = sem("down_full")
        up_read = sem("up_read")
        part_high = sem("part_high")
        part_mid = sem("part_mid")
        den_ready = sem("den_ready")
        x_sum = sem("x_sum")
        expert_added = sem("expert_added")
        out_stored = sem("out_stored")
        act_chain = sem("act_chain")
        dve_chain = sem("dve_chain")
        pool_chain = sem("pool_chain")

        def bcast(ap, at, n):
            ap = ap.unsqueeze(at)
            shape = list(ap.shape)
            shape[at] = n
            return ap.to_broadcast(shape)

        class Banks:

            def __init__(self, pe):
                self.pe, self.n = pe, 0

            def take(self):
                if self.n >= 8:
                    self.pe.wait_ge(psum_read, self.n - 7)
                self.n += 1
                return (self.n - 1) % 8

            def all_read(self):
                self.pe.wait_ge(psum_read, self.n)

        class Reads:

            def __init__(self, eng):
                self.eng, self.n = eng, 0

            def next(self):
                self.n += 1
                self.eng.wait_ge(psum_full, self.n)
                return (self.n - 1) % 8

        def dve_norm(v, link, ans, eps, rms_eps=None):
            link(v.tensor_reduce(stat[:], X[:], AX.X, ALU.add))
            link(v.tensor_scalar(stat[:], stat[:], -1.0 / D, None, ALU.mult))
            link(v.tensor_tensor(XL[:], X[:], bcast(stat[:], 2, D), ALU.add))
            link(v.tensor_tensor(SQ[:], XL[:], XL[:], ALU.mult))
            link(v.tensor_reduce(var[:], SQ[:], AX.X, ALU.add))
            link(v.tensor_scalar(var[:], var[:], 1.0 / D, None, ALU.mult))
            v.tensor_scalar(stat[:], var[:], eps, None, ALU.add).then_inc(to_act, 1)
            ans.wait()
            link(v.reciprocal(rstd[:], stat[:]))
            ins = v.tensor_tensor(XL[:], XL[:], bcast(rstd[:], 2, D), ALU.mult)
            if rms_eps is None:
                ins.then_inc(normed, 1)
            else:
                link(ins)
                link(v.tensor_tensor(var[:], var[:], rstd[:], ALU.mult))
                link(v.tensor_tensor(var[:], var[:], rstd[:], ALU.mult))
                v.tensor_scalar(stat[:], var[:], rms_eps, None, ALU.add).then_inc(to_act, 1)
                ans.wait()
                link(v.reciprocal(rrms[:], stat[:]))
                v.tensor_tensor(SQ[:], XL[:], bcast(rrms[:], 2, D), ALU.mult).then_inc(normed, 1)

        def act_sqrt(act, ask, ap):
            ask.wait()
            act.activation(ap, ap, ACT.Sqrt).then_inc(to_dve, 1)

        def pe_transpose_in(pe, banks, src):
            for g in range(NCH):
                k = banks.take()
                for i in range(TPC):
                    last = pe.transpose(PS[:, k, i * P:(i + 1) * P], src[:, g * TPC + i, :], ident[:])
                last.then_inc(psum_full, 1)

        def act_ht(act, reads):
            for g in range(NCH):
                k = reads.next()
                act.activation(HT[:, g * CH:(g + 1) * CH], PS[:, k, :], ACT.Copy).then_inc(psum_read, 1)

        A_RES = 34

        def lanes(t):
            return t.rearrange("p d (c s) -> p c s d", s=C)

        def a_sync(sp):
            for half in range(2):
                t = slice(half * TB, (half + 1) * TB)
                sp.dma_start(X[:, t, :], x.rearrange("(t p) d -> p t d", p=P)[:, t, :]).then_inc(x_loaded, 16)
            sp.dma_start(ident[:], eye).then_inc(x_loaded, 16)
            for dst, src in ((aw, a_w), (awab, a_wab), (asm, a_small), (awout, a_wout)):
                sp.dma_start(dst[:], src).then_inc(a_loaded, 16)
            sp.dma_start(abog[:], a_bog.partition_broadcast(P)).then_inc(a_loaded, 16)
            sp.dma_start(about[:], a_bout.partition_broadcast(P)).then_inc(a_loaded, 16)
            for n in range(3):
                sp.wait_ge(silu_done, n + 1)
                sp.dma_start(qkv_d[n].rearrange("b p s -> p b s"), CY[n % 2][:]).then_inc(qkv_stored, 16)
                sp.wait_ge(qkv_stored, 16 * (n + 1))
                src = qkv_d[n].rearrange("b (h d) s -> (b h) d s", d=HD)
                for g in range(SEG):
                    rows = slice(g * BH, (g + 1) * BH)
                    dst = LQK[rows, n, :, :] if n < 2 else WU[rows, HD:2 * HD, :]
                    sp.dma_start(dst, src[:, :, g * ST:(g + 1) * ST]).then_inc(lanes_loaded, 16)
            sp.wait_ge(wk_ready, 1)
            sp.dma_start(w_d.rearrange("g h i t -> (g h) i t"), WU[:, 0:HD, :]).then_inc(wk_stored, 16)
            sp.dma_start(k_d.rearrange("g h i t -> (g h) i t"), KB[:]).then_inc(wk_stored, 16)
            sp.dma_start(ac_d.rearrange("g h c -> (g h) c"), AC1[:]).then_inc(wk_stored, 16)
            sp.wait_ge(u_solved, 1)
            sp.dma_start(u_d.rearrange("g h i t -> (g h) i t"), WU[:, HD:2 * HD, :]).then_inc(u_stored, 16)
            sp.wait_ge(wk_stored, 48)
            sp.wait_ge(u_stored, 16)
            for g in range(SEG):
                for j in range(4):
                    rows = slice(j * BH, (j + 1) * BH)
                    for dst, src in ((W2[rows, g], w_d[g]), (K2[rows, g], k_d[g]),
                                     (U2[rows, g], u_d[g][:, 2 * j:2 * j + 2, :]), (AC2[rows, g], ac_d[g])):
                        sp.dma_start(dst, src).then_inc(seg_loaded[g], 16)
            sp.wait_ge(chunk_done, SEG * NC)
            for j in range(4):
                rows = slice(j * BH, (j + 1) * BH)
                sp.dma_start(d_d[:, :, 2 * j:2 * j + 2, :].rearrange("g h j t -> h g (j t)"),
                             D2[rows].rearrange("p g j t -> p g (j t)")).then_inc(ds_stored, 16)
                sp.dma_start(s_d[:, :, j, :].rearrange("g h r -> h g r"),
                             S2[rows, 0:SEG * NC].rearrange("p (g c) j i -> p g (c j i)", g=SEG)).then_inc(ds_stored, 16)
            sp.wait_ge(ds_stored, 128)
            sp.dma_start(DJ[:], d_d.rearrange("g h j t -> (g h) j t")).then_inc(ds_loaded, 16)
            sp.dma_start(SJ[:].rearrange("p a c j i -> p a (c j i)"),
                         s_d.rearrange("g h a r -> (g h) a r")).then_inc(ds_loaded, 16)
            sp.wait_ge(reads_ready, 1)
            for g in range(SEG):
                sp.dma_start(r_d[:, :, g * ST:(g + 1) * ST], RO[g * BH:(g + 1) * BH]).then_inc(reads_stored, 16)
            sp.wait_ge(reads_stored, 64)
            sp.dma_start(RT[:], r_d.rearrange("(b h) j s -> (h j) b s", b=B)).then_inc(rt_loaded, 16)

        PAIRS = ((A_ANG, 4), (A_UE, 0), (A_UO, 1), (A_CE, 2), (A_CO, 3))

        def a_tensor(pe, banks):
            pe.wait_ge(x_loaded, 48)
            pe.wait_ge(a_loaded, 96)
            pe.wait_ge(normed, 1)
            pe_transpose_in(pe, banks, XL)
            banks.all_read()

            def pair(col):
                for c in range(S // CH):
                    k = banks.take()
                    for b in range(B):
                        t = b * S + c * CH
                        last = pe.matmul(PS[64 * b:64 * b + 64, k, :], aw[:, col:col + 64], HT[:, t:t + CH],
                                         start=True, stop=True)
                    last.then_inc(psum_full, 1)

            for col, _ in PAIRS[:3]:
                pair(col)
            k = banks.take()
            for w in range(2):
                for g in range(SEG):
                    for b in range(B):
                        t = b * S + g * ST
                        last = pe.matmul(PS[g * BH:(g + 1) * BH, k, w * ST:(w + 1) * ST], awab[:, 2 * w + b, :],
                                         HT[:, t:t + ST], start=(b == 0), stop=(b == B - 1))
            last.then_inc(psum_full, 1)
            for col, _ in PAIRS[3:]:
                pair(col)
            for col in (A_Q, A_K, A_V):
                for c in range(NCH):
                    k = banks.take()
                    pe.matmul(PS[:, k, :], aw[:, col:col + D], HT[:, c * CH:(c + 1) * CH],
                              start=True, stop=True).then_inc(psum_full, 1)
            for g in range(NCH):
                k = banks.take()
                for i in range(TPC):
                    t = (g * TPC + i) * P
                    last = pe.matmul(PS[:, k, i * P:(i + 1) * P], HT[:, t:t + P], aw[:, A_OG:A_OG + D],
                                     start=True, stop=True)
                last.then_inc(psum_full, 1)
            banks.all_read()
            pe.wait_ge(wout_ready, 3)
            pe.wait_ge(vs_ready, 1)
            for b in range(B):
                for t in range(TB):
                    last = pe.matmul(PS[:, b, t:t + 1], VS[64 * b:64 * b + 64, 0, t * P:(t + 1) * P],
                                     ones[64 * b:64 * b + 64, :], start=True, stop=True)
            last.then_inc(psum_full, 1)
            banks.n += 1
            for g in range(NCH):
                for i in range(TPC):
                    b, t = divmod(g * TPC + i, TB)
                    rows = slice(64 * b, 64 * b + 64)
                    for e in range(2):
                        last = pe.matmul(PS[:, 4 + g, i * P:(i + 1) * P], V0[rows, e, t * P:(t + 1) * P],
                                         awout[rows, 1 + e, :], start=(e == 0), stop=(e == 1))
            last.then_inc(psum_full, 1)
            banks.n += 1
            pe.wait_ge(rt_loaded, 16)
            pe.wait_ge(psum_read, 32)
            for g in range(NCH):
                for i in range(TPC):
                    b, t = divmod(g * TPC + i, TB)
                    last = pe.matmul(PS[:, g, i * P:(i + 1) * P], RT[:, b, t * P:(t + 1) * P], awout[:, 0, :],
                                     start=True, stop=True)
            last.then_inc(psum_full, 1)
            banks.n += 1

        def a_scalar(act, link, ask, reads):
            act_sqrt(act, ask, stat[:])
            act_ht(act, reads)
            act.wait_ge(a_loaded, 96)

            def bias(col):
                return asm[:, col:col + 1]

            def pair(dst, n, func):
                for c in range(S // CH):
                    k = reads.next()
                    act.activation(dst[:, c * CH:(c + 1) * CH], PS[:, k, :], func,
                                   bias=bias(S_BPAIR + n)).then_inc(psum_read, 1)

            pair(ANG[:], 4, ACT.Identity)
            pair(UEO[:, 0], 0, ACT.Sigmoid)
            pair(UEO[:, 1], 1, ACT.Sigmoid)
            k = reads.next()
            link(act.activation(ALP[:], PS[:, k, 0:ST], ACT.Sigmoid, bias=bias(S_BAB)))
            act.activation(BET[:], PS[:, k, ST:2 * ST], ACT.Sigmoid, bias=bias(S_BAB + 1)).then_inc(psum_read, 1)
            pair(TRA[0][:, 0, 2], 2, ACT.Silu)
            pair(TRA[0][:, 1, 2], 3, ACT.Silu)
            act.wait_ge(trig_in, 1)
            act.activation(SIN[:], SIN[:], ACT.Sin).then_inc(trig_ready, 1)
            act.activation(COS[:], COS[:], ACT.Sin).then_inc(trig_ready, 1)

            def take(n):
                if n >= 2:
                    act.wait_ge(conv_done, n - 1)
                else:
                    act.wait_ge(pads_clear, 3)
                for c in range(NCH):
                    k = reads.next()
                    b, h = divmod(c, S // CH)
                    act.activation(CQ[n % 2][:, b, 3 + h * CH:3 + (h + 1) * CH], PS[:, k, :], ACT.Identity,
                                   bias=bias(S_BQKV + n)).then_inc(psum_read, 1)

            def silu(n):
                act.wait_ge(conv_done, n + 1)
                act.activation(CY[n % 2][:], CY[n % 2][:], ACT.Silu).then_inc(silu_done, 1)

            take(0)
            take(1)
            silu(0)
            take(2)
            silu(1)
            silu(2)
            for g in range(NCH):
                k = reads.next()
                act.activation(SQ[:, g * TPC:(g + 1) * TPC, :].rearrange("p t d -> p (t d)"), PS[:, k, :],
                               ACT.Copy).then_inc(psum_read, 1)
            ask.wait()
            act.activation(SQ[:], SQ[:], ACT.Sigmoid).then_inc(gate_ready, 1)
            act_sqrt(act, ask, SS[:])
            act.wait_ge(state_clear, 1)

            def u_in(n):
                g, c = divmod(n, NC)
                if c == 0:
                    act.wait_ge(seg_loaded[g], 256)
                act.activation(P1[:, n % 2, :, :, HD], U2[:, g, :, c * C:(c + 1) * C], ACT.Copy).then_inc(u_slot, 1)

            u_in(0)
            for n in range(SEG * NC):
                g, c = divmod(n, NC)
                if n:
                    act.wait_ge(chunk_done, n)
                act.activation(P2[:, :, :, C], S2[:, n], ACT.Copy, scale=AC2[:, g, c:c + 1]).then_inc(s_slot, 1)
                if n + 1 < SEG * NC:
                    u_in(n + 1)
            act_sqrt(act, ask, SS4[:])
            act_sqrt(act, ask, vss[:])
            reads.n += 3

        def a_vector(v, link, ans):
            v.wait_ge(x_loaded, 48)
            dve_norm(v, link, ans, LN_EPS)
            v.wait_ge(a_loaded, 96)
            link(v.tensor_scalar(nwb[:], asm[:, S_WB:S_WB + 4], -1.0, None, ALU.mult))
            for i in range(3):
                v.tensor_scalar(awout[:, i], awout[:, i], asm[:, S_RMS + i:S_RMS + i + 1], None,
                                ALU.mult).then_inc(wout_ready, 1)
            v.wait_ge(psum_read, 6)
            link(v.tensor_scalar(SIN[:], ANG[:], 1.0 / TWO_PI, MAGIC, ALU.mult, ALU.add))
            link(v.tensor_scalar(SIN[:], SIN[:], -MAGIC, None, ALU.add))
            link(v.scalar_tensor_tensor(out=ANG[:], in0=SIN[:], scalar=-TWO_PI_HI, in1=ANG[:], op0=ALU.mult, op1=ALU.add))
            link(v.scalar_tensor_tensor(out=ANG[:], in0=SIN[:], scalar=TWO_PI_HI - TWO_PI, in1=ANG[:],
                                        op0=ALU.mult, op1=ALU.add))
            link(v.tensor_scalar(SIN[:], ANG[:], -PI, PI, ALU.max, ALU.min))
            link(v.scalar_tensor_tensor(out=COS[:], in0=SIN[:], scalar=-1.0, in1=SIN[:], op0=ALU.mult, op1=ALU.min))
            v.tensor_scalar(COS[:], COS[:], TWO_PI / 4, None, ALU.add).then_inc(trig_in, 1)
            v.wait_ge(psum_read, 15)
            v.wait_ge(trig_ready, 2)
            tmp = TRT[:].rearrange("p a b s -> p (a b s)")[:, 0:S]
            wb = [asm[:, S_WB + i:S_WB + i + 1] for i in range(4)]
            for row, u in ((0, UEO[:, 0]), (1, UEO[:, 1])):
                link.open(v.tensor_tensor(ANG[:], u, COS[:], ALU.mult))
                link(v.tensor_tensor(tmp, u, SIN[:], ALU.mult))
                for i in range(2):
                    m = TRA[0][:, row, i, :]
                    first, by, second, by2 = ((ANG[:], wb[2 * i], tmp, nwb[:, 2 * i + 1:2 * i + 2]) if row == 0 else
                                              (tmp, wb[2 * i], ANG[:], wb[2 * i + 1]))
                    link(v.tensor_scalar(m, first, by, None, ALU.mult))
                    link(v.scalar_tensor_tensor(out=m, in0=second, scalar=by2, in1=m, op0=ALU.mult, op1=ALU.add))
            link(v.tensor_tensor(UEO[:], UEO[:], TRA[0][:, :, 2, :], ALU.mult))
            v.tensor_tensor(TRA[0][:, :, 2, :], TRA[0][:, :, 2, :], UEO[:], ALU.subtract).then_inc(tree_in, 1)
            for n in range(3):
                v.wait_ge(psum_read, 15 + NCH * (n + 1))
                if n >= 2:
                    v.wait_ge(qkv_stored, 16 * (n - 1))
                y, xq = CY[n % 2], CQ[n % 2]
                link(v.tensor_scalar(y[:], xq[:, :, 0:S], asm[:, S_CONV + 4 * n:S_CONV + 4 * n + 1], None, ALU.mult))
                for j in range(1, 4):
                    w = asm[:, S_CONV + 4 * n + j:S_CONV + 4 * n + j + 1]
                    ins = v.scalar_tensor_tensor(out=y[:], in0=xq[:, :, j:j + S], scalar=w, in1=y[:],
                                                 op0=ALU.mult, op1=ALU.add)
                    if j < 3:
                        link(ins)
                    else:
                        ins.then_inc(conv_done, 1)
            v.wait_ge(psum_read, 31)
            v.tensor_tensor(SQ[:], SQ[:], bcast(abog[:], 1, TILES), ALU.add).then_inc(to_act, 1)
            v.wait_ge(lanes_loaded, 16 * 12)
            v.wait_ge(lanes_clear, 3)
            sq = PRD[:].rearrange("p (n d t) -> p n d t", n=2, d=HD)
            link(v.tensor_tensor(sq, LQK[:], LQK[:], ALU.mult))
            link(v.tensor_reduce(SS[:], sq.rearrange("p n d t -> p n t d"), AX.X, ALU.add))
            v.tensor_scalar(SS[:], SS[:], L2_EPS, None, ALU.add).then_inc(to_act, 1)
            ans.wait()
            link(v.reciprocal(RS[:], SS[:]))
            link(v.tensor_tensor(LQK[:], LQK[:], bcast(RS[:], 2, HD), ALU.mult))
            v.tensor_tensor(KB[:], LQK[:, 1], bcast(BET[:], 1, HD), ALU.mult).then_inc(kb_ready, 1)
            al = ALP[:].rearrange("p (c s) -> p c s", s=C)
            for m in range(C - 1, -1, -1):
                n = C - m
                link(v.tensor_tensor(GAM[:, :, m + 1:C + 1, m], GAM[:, :, m + 1:C + 1, m + 1],
                                     bcast(al[:, :, m], 2, n), ALU.mult))
            v.wait_ge(kb_ready, 1)
            kn = lanes(LQK[:, 1])
            kb = lanes(KB[:])
            for s in range(C):
                if s < C - 1:
                    n = C - 1 - s
                    pv = PRD[:, 0:NC * n * HD].rearrange("p (c t d) -> p c t d", c=NC, d=HD)
                    link(v.tensor_tensor(pv, kn[:, :, s + 1:C, :], bcast(kb[:, :, s, :], 2, n), ALU.mult))
                    link(v.tensor_reduce(LA[:, :, s + 1:C, s], pv, AX.X, ALU.add))
                n = C - s
                v.wait_ge(prod_ready, s + 1)
                pp = PRP[s % 2][:, 0:NC * n * HD].rearrange("p (c t d) -> p c t d", c=NC, d=HD)
                v.tensor_reduce(PA[:, :, s:C, s], pp, AX.X, ALU.add).then_inc(prod_used, 1)
            v.wait_ge(prod_used, C)
            v.tensor_tensor(LA[:], LA[:], GAM[:, :, 0:C, 1:C + 1], ALU.mult).then_inc(la_ready, 1)
            link.open(v.tensor_tensor(PA[:], PA[:], GAM[:, :, 1:C + 1, 1:C + 1], ALU.mult))
            link(v.tensor_scalar(NG0[:].rearrange("p (c s) -> p c s", s=C), GAM[:, :, 0:C, 0], -1.0, None, ALU.mult))
            link.open(v.tensor_tensor(WU[:, 0:HD, :], LQK[:, 1], bcast(NG0[:], 1, HD), ALU.mult))
            q4 = LQK[:, 0].rearrange("p d (c s) -> p d c s", s=C)
            k4 = KB[:].rearrange("p d (c s) -> p d c s", s=C)
            link.open(v.tensor_tensor(q4, q4, bcast(GAM[:, :, 1:C + 1, 0], 1, HD), ALU.mult))
            link.open(v.tensor_tensor(k4, k4, bcast(GAM[:, :, C, 1:C + 1], 1, HD), ALU.mult))
            link.open(v.tensor_copy(AC1[:], GAM[:, :, C, 0]))
            link.close()
            v.wait_ge(la_ready, 1)
            solve(v, link, 0, PRD, wk_ready)
            v.wait_ge(u_solved, 1)
            v.wait_ge(wk_stored, 48)
            v.memset(S2[:, 0], 0.0).then_inc(state_clear, 1)
            v.wait_ge(state_clear, 1)
            for n in range(SEG * NC):
                g, c = divmod(n, NC)
                cs = slice(c * C, (c + 1) * C)
                if c == 0:
                    v.wait_ge(seg_loaded[g], 256)
                if n:
                    v.wait_ge(chunk_done, n)
                link(v.tensor_tensor(P1[:, n % 2, :, :, 0:HD], bcast(W2[:, g, :, cs].rearrange("p i s -> p s i"), 1, 2),
                                     bcast(S2[:, n], 2, C), ALU.mult))
                v.wait_ge(u_slot, n + 1)
                link(v.tensor_reduce(D2[:, g, :, cs], P1[:, n % 2], AX.X, ALU.add))
                link(v.tensor_tensor(P2[:, :, :, 0:C], bcast(K2[:, g, :, cs], 1, 2), bcast(D2[:, g, :, cs], 2, HD),
                                     ALU.mult))
                v.wait_ge(s_slot, n + 1)
                v.tensor_reduce(S2[:, n + 1], P2[:], AX.X, ALU.add).then_inc(chunk_done, 1)
            v.wait_ge(ds_loaded, 32)
            qa = lanes(LQK[:, 0])
            pr3 = PRR[:].rearrange("p (c s i) -> p c s i", c=NC, i=HD)
            for j in range(HD):
                link(v.tensor_tensor(pr3, qa, bcast(SJ[:, j // 2, :, j % 2, :], 2, C), ALU.mult))
                link(v.tensor_reduce(RP[:, j].rearrange("p (c s) -> p c s", s=C), pr3, AX.X, ALU.add))
                for t in (2 * j, 2 * j + 1):
                    v.wait_ge(rprod_ready, t + 1)
                    pq = PRQ[t % 2][:, 0:NC * HD * (t + 1)].rearrange("p (c j s) -> p c j s", c=NC, j=HD)
                    v.tensor_reduce(RO[:].rearrange("p j (c s) -> p c j s", s=C)[:, :, :, t], pq, AX.X,
                                    ALU.add).then_inc(rprod_used, 1)
            v.wait_ge(rprod_used, C)
            link(v.tensor_tensor(RO[:], RO[:], RP[:], ALU.add))
            link(v.tensor_tensor(RP[:], RO[:], RO[:], ALU.mult))
            link(v.tensor_reduce(SS4[:], RP[:].rearrange("p j t -> p t j"), AX.X, ALU.add))
            v.tensor_scalar(SS4[:], SS4[:], 1.0 / HD, A_EPS, ALU.mult, ALU.add).then_inc(to_act, 1)
            ans.wait()
            link(v.reciprocal(RP[:, 0], SS4[:]))
            v.tensor_tensor(RO[:], RO[:], bcast(RP[:, 0], 1, HD), ALU.mult).then_inc(reads_ready, 1)
            v.wait_ge(psum_full, 32)
            v.tensor_copy(vss[:].rearrange("p (b t) -> p b t", b=B), PS[:, 0:B, 0:TB]).then_inc(psum_read, 1)
            v.wait_ge(psum_read, 32)
            v.tensor_scalar(vss[:], vss[:], 1.0 / D, A_EPS, ALU.mult, ALU.add).then_inc(to_act, 1)
            ans.wait()
            link(v.reciprocal(rrms[:], vss[:]))
            v.wait_ge(psum_full, 33)
            v.tensor_tensor(OT[:], PS[:, 4:8, :].rearrange("p b (t d) -> p (b t) d", d=D), bcast(rrms[:], 2, D),
                            ALU.mult).then_inc(psum_read, 1)
            v.wait_ge(psum_full, 34)
            v.wait_ge(psum_read, 33)
            v.tensor_tensor(OT[:], OT[:], PS[:, 0:4, :].rearrange("p b (t d) -> p (b t) d", d=D),
                            ALU.add).then_inc(psum_read, 1)
            v.wait_ge(psum_read, 34)
            link(v.tensor_tensor(OT[:], OT[:], bcast(about[:], 1, TILES), ALU.add))
            v.wait_ge(gate_ready, 1)
            link(v.tensor_tensor(OT[:], OT[:], SQ[:], ALU.mult))
            v.tensor_tensor(X[:], X[:], OT[:], ALU.add).then_inc(x_ready, 1)

        def solve(eng, link, col, room, done):
            z = WU[:, col:col + HD, :].rearrange("p d (c s) -> p c s d", s=C)
            for s in range(C - 1):
                n = C - 1 - s
                pv = room[:, 0:NC * n * HD].rearrange("p (c t d) -> p c t d", c=NC, d=HD)
                link(eng.tensor_tensor(pv, bcast(LA[:, :, s + 1:C, s], 3, HD), bcast(z[:, :, s, :], 2, n), ALU.mult))
                ins = eng.tensor_tensor(z[:, :, s + 1:C, :], z[:, :, s + 1:C, :], pv, ALU.subtract)
                if s < C - 2:
                    link(ins)
                else:
                    ins.then_inc(done, 1)

        def a_gpsimd(pool, link):
            for i in range(2):
                pool.memset(CQ[i][:, :, 0:3], 0.0).then_inc(pads_clear, 1)
            pool.memset(ones[:], 1.0).then_inc(pads_clear, 1)
            pool.wait_ge(tree_in, 1)
            for l in range(1, 11):
                n = S >> l
                lo, hi, to = TRA[l - 1][:, :, :, 0::2], TRA[l - 1][:, :, :, 1::2], TRA[l]
                tt = TRT[:, :, :, 0:n]
                link.open(pool.tensor_tensor(to[:], bcast(hi[:, :, 0, :], 2, 3), bcast(lo[:, 0, :, :], 1, 2), ALU.mult))
                link(pool.tensor_tensor(tt, bcast(hi[:, :, 1, :], 2, 3), bcast(lo[:, 1, :, :], 1, 2), ALU.mult))
                link(pool.tensor_tensor(to[:], to[:], tt, ALU.add))
                link(pool.tensor_tensor(to[:, :, 2, :], to[:, :, 2, :], hi[:, :, 2, :], ALU.add))
            link(pool.tensor_copy(TRV[10][:], TRA[10][:, :, 2, :]))
            for l in range(9, -1, -1):
                n = S >> (l + 1)
                a, to = TRA[l], TRV[l]
                link.open(pool.tensor_copy(to[:, :, 0:1], a[:, :, 2, 0:1]))
                link(pool.tensor_copy(to[:, :, 1::2], TRV[l + 1][:]))
                if n > 1:
                    tt = TRT[:, :, 0:2, 0:n - 1]
                    link(pool.tensor_tensor(tt, a[:, :, 0:2, 2::2], bcast(TRV[l + 1][:, :, 0:n - 1], 1, 2), ALU.mult))
                    link(pool.tensor_tensor(to[:, :, 2::2], tt[:, :, 0, :], tt[:, :, 1, :], ALU.add))
                    link(pool.tensor_tensor(to[:, :, 2::2], to[:, :, 2::2], a[:, :, 2, 2::2], ALU.add))
            pool.wait_ge(lanes_loaded, 16 * 12)
            pool.wait_ge(conv_done, 3)
            pool.memset(GAM[:], 1.0).then_inc(lanes_clear, 1)
            pool.memset(LA[:], 0.0).then_inc(lanes_clear, 1)
            pool.memset(PA[:], 0.0).then_inc(lanes_clear, 1)
            pool.wait_ge(kb_ready, 1)
            qn, kb = lanes(LQK[:, 0]), lanes(KB[:])
            for s in range(C):
                n = C - s
                if s >= 2:
                    pool.wait_ge(prod_used, s - 1)
                pp = PRP[s % 2][:, 0:NC * n * HD].rearrange("p (c t d) -> p c t d", c=NC, d=HD)
                pool.tensor_tensor(pp, qn[:, :, s:C, :], bcast(kb[:, :, s, :], 2, n), ALU.mult).then_inc(prod_ready, 1)
            pool.wait_ge(la_ready, 1)
            pool.wait_ge(prod_used, C)
            solve(pool, link, HD, PRP[0], u_solved)
            link.open(pool.tensor_tensor(VS[:, 0], V0[:, 0], V0[:, 0], ALU.mult))
            link(pool.tensor_tensor(VS[:, 1], V0[:, 1], V0[:, 1], ALU.mult))
            pool.tensor_tensor(VS[:, 0], VS[:, 0], VS[:, 1], ALU.add).then_inc(vs_ready, 1)
            pool.wait_ge(ds_loaded, 32)
            dj = DJ[:].rearrange("p j (c s) -> p c j s", s=C)
            for t in range(C):
                if t >= 2:
                    pool.wait_ge(rprod_used, t - 1)
                pq = PRQ[t % 2][:, 0:NC * HD * (t + 1)].rearrange("p (c j s) -> p c j s", c=NC, j=HD)
                pool.tensor_tensor(pq, bcast(PA[:, :, t, 0:t + 1], 2, HD), dj[:, :, :, 0:t + 1],
                                   ALU.mult).then_inc(rprod_ready, 1)

        B_RES = 3 + NCH + 3 * NCH + NCH

        def b_tensor(pe, banks, nth):
            base = banks.n
            pe.wait_ge(w_loaded, W_LOADED)
            for n in range(3):
                k = banks.take()
                pe.matmul(PS[:, k, 0:2 * NB], bw[:, n, :], bdft[:].rearrange("p r f -> p (r f)"),
                          start=True, stop=True).then_inc(psum_full, 1)
            pe.wait_ge(normed, FIRST_NORM[nth] + 1)
            pe_transpose_in(pe, banks, XL)
            banks.all_read()
            for c in range(NCH):
                for n in range(3):
                    if c:
                        pe.wait_ge(psum_read, banks.n - 2)
                    for r in range(2):
                        last = pe.matmul(PS[0:NB, 2 * n + r, :], bwf[:, n, r, :], HT[:, c * CH:(c + 1) * CH],
                                         start=True, stop=True)
                    last.then_inc(psum_full, 1)
                    banks.n += 1
            banks.all_read()
            for g in range(NCH):
                pe.wait_ge(y_ready, g + 1)
                for i in range(TPC):
                    t = (g * TPC + i) * P
                    for r in range(2):
                        last = pe.matmul(PS[:, g, i * P:(i + 1) * P], YF[0:NB, r, t:t + P], bidft[0:NB, r, :],
                                         start=(r == 0), stop=(r == 1))
                last.then_inc(psum_full, 1)
                banks.n += 1
            assert banks.n == base + B_RES

        def b_scalar(act, link, ask, reads):
            for n in range(3):
                k = reads.next()
                act.activation(bwf[:, n].rearrange("p r f -> p (r f)"), PS[:, k, 0:2 * NB],
                               ACT.Copy).then_inc(psum_read, 1)
            act_sqrt(act, ask, stat[:])
            act_ht(act, reads)
            for c in range(NCH):
                if c:
                    act.wait_ge(y_ready, c)
                for n in range(3):
                    reads.next()
                    act.activation(QF[0:NB, n], PS[0:NB, 2 * n:2 * n + 2, :], ACT.Copy).then_inc(psum_read, 1)
                act_sqrt(act, ask, mag[0:NB])
            reads.n += NCH

        def b_vector(v, link, ans, nth):
            v.wait_ge(x_ready, nth)
            dve_norm(v, link, ans, LN_EPS)
            v.wait_ge(normed, FIRST_NORM[nth] + 1)
            base = FIRST_RESULT[nth] + 3 + NCH
            R = slice(0, NB)
            q, k, w = QF[R, 0], QF[R, 1], QF[R, 2]
            for c in range(NCH):
                b, h = divmod(c, S // CH)
                cs = slice(h * CH, (h + 1) * CH)
                ts = slice(c * CH, (c + 1) * CH)
                v.wait_ge(psum_read, base + 3 * (c + 1))
                link(v.tensor_tensor(QF2[R], QF[R, 0:2], QF[R, 0:2], ALU.mult))
                v.tensor_tensor(mag[R], QF2[R, :, 0], QF2[R, :, 1], ALU.add).then_inc(to_act, 1)
                ans.wait()
                link(v.tensor_scalar(mag[R], mag[R], B_EPS, None, ALU.add))
                link(v.reciprocal(mag[R], mag[R]))
                link(v.tensor_tensor(QF[R, 0:2], QF[R, 0:2], bcast(mag[R], 2, 2), ALU.mult))
                link.open(v.tensor_tensor(PRB[R, 0:2], k, w, ALU.mult))
                link.open(v.tensor_tensor(PRB[R, 2], k[:, 0], w[:, 1], ALU.mult))
                link(v.tensor_tensor(PRB[R, 3], k[:, 1], w[:, 0], ALU.mult))
                for r, op in ((0, ALU.subtract), (1, ALU.add)):
                    init = CUM[R, r, b, h * CH - 1:h * CH] if h else 0.0
                    link.open(v.tensor_tensor_scan(CUM[R, r, b, cs], PRB[R, 2 * r], PRB[R, 2 * r + 1], init, ALU.add, op))
                link.close()
                link.open(v.tensor_tensor(PRB[R, 0:2], CUM[R, :, b, cs], q, ALU.mult))
                link.open(v.tensor_tensor(PRB[R, 2], CUM[R, 1, b, cs], q[:, 0], ALU.mult))
                link(v.tensor_tensor(PRB[R, 3], CUM[R, 0, b, cs], q[:, 1], ALU.mult))
                link.open(v.tensor_tensor(YF[R, 0, ts], PRB[R, 0], PRB[R, 1], ALU.add))
                v.tensor_tensor(YF[R, 1, ts], PRB[R, 2], PRB[R, 3], ALU.subtract).then_inc(y_ready, 1)
                link.close()
                v.wait_ge(y_ready, c + 1)
            link(v.tensor_tensor(X[:], X[:], XL[:], ALU.add))
            for g in range(NCH):
                v.wait_ge(psum_full, base + 3 * NCH + g + 1)
                t = slice(g * TPC, (g + 1) * TPC)
                v.tensor_tensor(X[:, t], X[:, t], PS[:, g, :].rearrange("p (t d) -> p t d", d=D),
                                ALU.add).then_inc(psum_read, 1)
            v.wait_ge(psum_read, base + 4 * NCH)
            v.nop().then_inc(x_ready, 1)

        def w_sync(sp):
            sp.wait_ge(x_ready, 1)
            for dst, src in ((bw, b_w), (bdft, b_dft), (bidft, b_idft), (fw, f_w), (fn, f_n), (fmid, f_mid),
                             (fdown, f_down), (fwo, f_wo)):
                sp.dma_start(dst[:], src).then_inc(w_loaded, 16)
            sp.dma_start(fqk[:].rearrange("p n d -> p (n d)"), f_qk.partition_broadcast(P)).then_inc(w_loaded, 16)
            sp.dma_start(maskf[:], causal).then_inc(w_loaded, 16)

        W_LOADED = 16 * 10
        ATT = [(b, qc, kt, hp, max(0, kt - TPC * qc) * P) for b in range(B) for qc in range(S // CH)
               for kt in range(TPC * (qc + 1)) for hp in range(GH // 2)]
        NA = len(ATT)
        NA_B = NA // B
        NA_Q0 = TPC * GH // 2
        LAG = 2
        DEPTH = 3
        OBANKS = 2
        SCORES_BANKS = 2 * DEPTH
        F_RES = NCH + TILES + 2 * NCH + NCH + NCH + NCH + 1


        def f_sync(sp, nth, rep):
            sp.wait_ge(stack_clear, 2 * B)
            for c in range(NCH):
                ts = slice(c * CH, (c + 1) * CH)
                sp.wait_ge(parts_ready, NCH * rep + c + 1)
                for n, (d, side) in enumerate(((qs_d, Q_SIDE), (ks_d, K_SIDE))):
                    for s in range(NSLOT):
                        sp.dma_start(d[:, HD * s:HD * (s + 1), ts], QP[side[s]][:, n, :]).then_inc(parts_stored, 16)
            sp.wait_ge(psum_read, FIRST_RESULT[nth] + NCH + TILES + 3 * NCH)
            sp.dma_start(qs_d[:, QROWS - 1, :], MT[:]).then_inc(shift_stored, 16)
            sp.wait_ge(shift_stored, 16 * (rep + 1))
            sp.wait_ge(parts_stored, PARTS * NCH * (rep + 1))

            def load(g, b):
                ts = slice(b * S, (b + 1) * S)
                heads = bass.ds(g * GH, GH)
                sp.dma_start(QS[b][0:QROWS], qs_d[heads, :, ts].rearrange("h r t -> r h t")).then_inc(stack_loaded[b], 16)
                sp.dma_start(KS[b][0:QROWS - 1],
                             ks_d[heads, 0:QROWS - 1, ts].rearrange("h r t -> r h t")).then_inc(stack_loaded[b], 16)

            for b in range(B):
                load(0, b)
            with sp.Fori(1, NG) as g:
                for b in range(B):
                    sp.wait_ge(probs_used, DEPTH + (rep * NG + g - 1) * NA + (b + 1) * NA_B)
                    load(g, b)

        PARTS = 16 * 2 * NSLOT

        def f_gpsimd(pool, link, nth, rep):
            if rep == 0:
                pool.wait_ge(w_loaded, W_LOADED)
                for b in range(B):
                    pool.memset(KS[b][:], 1.0).then_inc(stack_clear, 1)
                    pool.memset(QS[b][:], 0.0).then_inc(stack_clear, 1)
                    link(pool.memset(VA[b][:], 1.0))
                pool.tensor_copy(maskb[:], maskf[:]).then_inc(stack_clear, 1)
                pool.tensor_copy(identb[:], ident[:]).then_inc(stack_clear, 1)
            pool.wait_ge(psum_read, FIRST_RESULT[nth] + NCH + TILES)

            def values(g, b):
                src = QKV[:, b * TB:(b + 1) * TB, bass.ds(2 * D + g * (GH * HD), GH * HD)]
                pool.tensor_copy(VA[b][:, :, :, 0:HD], src.rearrange("p t (h d) -> p t h d", d=HD)).then_inc(v_ready, 1)

            for b in range(B):
                values(0, b)
            with pool.Fori(1, NG) as g:
                for b in range(B):
                    pool.wait_ge(probs_used, DEPTH + (rep * NG + g - 1) * NA + (b + 1) * NA_B)
                    values(g, b)

        def f_tensor(pe, banks, nth, rep):
            base = banks.n
            assert base == FIRST_RESULT[nth]
            if rep == 0:
                pe.sem_inc(probs_used, DEPTH)
            pe.wait_ge(fw_ready, 4)
            pe.wait_ge(normed, FIRST_NORM[nth] + 1)
            pe_transpose_in(pe, banks, SQ)
            banks.all_read()
            for t in range(TILES):
                k = banks.take()
                pe.matmul(PS[:, k, 0:3 * D], HT[:, t * P:(t + 1) * P], fw[:, 0:3 * D], start=True,
                          stop=True).then_inc(psum_full, 1)
            for c in range(NCH):
                pe.wait_ge(qk_normed, rep * B + c // 2 + 1)
                for n in range(2):
                    k = banks.take()
                    for i in range(TPC):
                        last = pe.transpose(PS[:, k, i * P:(i + 1) * P], QKS[:, c * TPC + i, n * D:(n + 1) * D], ident[:])
                    last.then_inc(psum_full, 1)
            for c in range(NCH):
                pe.wait_ge(shifts_ready, rep * B + c // 2 + 1)
                k = banks.take()
                for i in range(TPC):
                    last = pe.transpose(PS[0:H, k, i * P:(i + 1) * P], qst2[:, c * TPC + i, 0:H], ident[:])
                last.then_inc(psum_full, 1)
            banks.all_read()
            pe.wait_ge(stack_clear, 2 * B + 2)
            with pe.Fori(0, NG) as g:
                n = rep * NG + g
                for u in range(NA + LAG):
                    if u < NA:
                        b, qc, kt, hp, c0 = ATT[u]
                        if u % NA_B == 0:
                            pe.wait_ge(stack_loaded[b], 32 * (n + 1))
                            pe.wait_ge(v_ready, n * B + b + 1)
                        pe.wait_ge(probs_ready, n * NA + u + 1)
                        diag = kt >= TPC * qc
                        for i in range(2):
                            h, k = 2 * hp + i, 2 * (u % DEPTH) + i
                            last = pe.matmul(PS[:, k, c0:CH], KS[b][:, h, kt * P:(kt + 1) * P],
                                             QS[b][:, h, qc * CH + c0:(qc + 1) * CH], start=True, stop=True)
                            if diag:
                                last = pe.matmul(PS[:, k, c0:c0 + P], identb[:], maskb[:], start=False, stop=True,
                                                 skip_group_check=True)
                        last.then_inc(scores_ready, 1)
                    if u >= LAG:
                        w = u - LAG
                        b, qc, kt, hp, c0 = ATT[w]
                        pe.wait_ge(probs_ready, DEPTH + n * NA + w + 1)
                        if kt == 0 and hp == 0:
                            pe.wait_ge(o_read, (n * B + b) * 2 + qc + 1)
                        for i in range(2):
                            h = 2 * hp + i
                            last = pe.matmul(PS[32 * h:32 * h + 32, SCORES_BANKS + qc, c0:CH], VA[b][:, kt, h, :],
                                             PX[w % DEPTH][:, i, c0:CH], start=(kt == 0),
                                             stop=(kt >= TPC * qc), skip_group_check=True)
                        last.then_inc(probs_used, 1)
            pe.wait_ge(o_read, OBANKS + (rep + 1) * NG * B * 2)
            for c in range(NCH):
                k = banks.take()
                for i in range(TPC):
                    t = (c * TPC + i) * P
                    for g in range(NG):
                        last = pe.matmul(PS[:, k, i * OUTC:(i + 1) * OUTC], AO[:, g, t:t + P], fwo[:, g, :],
                                         start=(g == 0), stop=(g == NG - 1))
                last.then_inc(psum_full, 1)
            pe.wait_ge(normed, FIRST_NORM[nth] + 2)
            pe_transpose_in(pe, banks, SQ)
            banks.all_read()
            k = banks.take()
            for t in range(TILES):
                last = pe.matmul(PS[:, k, t * E4:(t + 1) * E4], HT[:, t * P:(t + 1) * P], fw[:, F_GATE:F_GATE + E4],
                                 start=True, stop=True)
            last.then_inc(psum_full, 1)
            banks.all_read()
            assert banks.n == base + F_RES
            with pe.Fori(0, NCH) as i:
                n = rep * NCH + i
                rhs = HT[:, bass.ds(i * CH, CH)]
                pe.wait_ge(h1_ready, n + 1)
                for w, col in ((0, F_E1A), (2, F_E1B)):
                    for m in range(2):
                        last = pe.matmul(PS[:, w + m, :], fw[:, col + m * P:col + (m + 1) * P], rhs, start=True, stop=True)
                    last.then_inc(up_full, 1)
                pe.wait_ge(h1_ready, n + 2)
                pe.wait_ge(down_read, rep * 2 * TILES + i * TPC + 1)
                for t in range(TPC):
                    for m in range(2):
                        last = pe.matmul(PS[:, 4 + t, 0:OUTC], HG[1][:, m, t * P:(t + 1) * P], fdown[:, 1, m, :],
                                         start=(m == 0), stop=(m == 1))
                    last.then_inc(down_full, 1)
            pe.wait_ge(down_read, rep * 2 * TILES + TILES + 1)
            with pe.Fori(0, NCH) as i:
                rhs = HT[:, bass.ds(i * CH, CH)]
                seen = rep * UPS + NCH + i * 6

                def up(bank, col):
                    for m in range(2):
                        last = pe.matmul(PS[:, bank + m, :], fw[:, col + m * P:col + (m + 1) * P], rhs, start=True, stop=True)
                    last.then_inc(up_full, 1)

                def mid(bank, w, h, nk):
                    for m in range(2):
                        for k in range(nk):
                            last = pe.matmul(PS[:, bank + m, :], fmid[:, w + k, m * P:(m + 1) * P],
                                             h[:, k, :] if nk == 2 else h[:], start=(k == 0), stop=(k == nk - 1))
                    last.then_inc(up_full, 1)

                pe.wait_ge(up_read, seen)
                up(0, F_E0)
                up(2, F_E2)
                pe.matmul(PS[:, 4, :], fw[:, F_E3:F_E3 + P], rhs, start=True, stop=True).then_inc(up_full, 1)
                pe.wait_ge(up_read, seen + 2)
                mid(0, 0, HA, 2)
                pe.wait_ge(up_read, seen + 3)
                mid(2, 4, HE, 1)
                pe.wait_ge(up_read, seen + 4)
                mid(4, 2, HB, 2)
                pe.wait_ge(up_read, seen + 6)
                for t in range(TPC):
                    pe.wait_ge(down_read, rep * 2 * TILES + TILES + i * TPC + t)
                    for j, (e, h) in enumerate(((0, H0), (2, HC), (3, HF))):
                        for m in range(2):
                            last = pe.matmul(PS[:, 6 + t % 2, j * OUTC:(j + 1) * OUTC], h[:, m, t * P:(t + 1) * P],
                                             fdown[:, e, m, :], start=(m == 0), stop=(m == 1))
                    last.then_inc(down_full, 1)

        UPS = NCH + 6 * NCH

        def f_scalar(act, link, ask, reads, nth, rep):
            if rep == 0:
                act.sem_inc(probs_ready, DEPTH)
            act_sqrt(act, ask, stat[:])
            act_sqrt(act, ask, stat[:])
            act_ht(act, reads)
            for t in range(TILES):
                k = reads.next()
                act.activation(QKV[:, t, :], PS[:, k, 0:3 * D], ACT.Copy).then_inc(psum_read, 1)
            for b in range(B):
                tb = slice(b * TB, (b + 1) * TB)
                act_sqrt(act, ask, qst[:, tb])
                act_sqrt(act, ask, qst[:, tb, H:2 * H])
            for c in range(NCH):
                if rep or c:
                    act.wait_ge(parts_stored, PARTS * (rep * NCH + c))
                for n in range(2):
                    k = reads.next()
                    act.activation(QP[0][:, n], PS[:, k, :], ACT.Copy).then_inc(part_high, 1)
                act.wait_ge(psum_read, reads.n)
                act.activation(QP[1][:], QR[:], ACT.Copy).then_inc(part_mid, 1)
            for c in range(NCH):
                k = reads.next()
                act.activation(MT[:, c * CH:(c + 1) * CH], PS[0:H, k, :], ACT.Copy).then_inc(psum_read, 1)
            with act.Fori(0, NG) as g:
                n = rep * NG + g
                for u in range(NA):
                    c0 = ATT[u][-1]
                    act.wait_ge(scores_ready, n * NA + u + 1)
                    act.wait_ge(probs_used, n * NA + u + 1)
                    act.activation(PX[u % DEPTH][:, :, c0:CH], PS[:, 2 * (u % DEPTH):2 * (u % DEPTH) + 2, c0:CH],
                                   ACT.Exp).then_inc(probs_ready, 1)
            reads.n += NCH
            act_sqrt(act, ask, stat[:])
            act_ht(act, reads)
            reads.n += 1
            ask.wait()
            act.activation(pr[:], lg[:], ACT.Exp).then_inc(to_dve, 1)
            with act.Fori(0, NCH) as i:
                act.wait_ge(up_full, rep * (2 * NCH + 6 * NCH) + 2 * i + 1)
                act.wait_ge(h1_ready, rep * NCH + i + 1)
                act.activation(HG[0][:], PS[:, 0:2, :], ACT.Silu).then_inc(up_read, 1)
            with act.Fori(0, NCH) as i:
                for j, (bank, w, h) in enumerate(((0, 2, H0), (2, 2, HA), (4, 1, HE), (0, 2, HB), (2, 2, HF), (4, 2, HC))):
                    act.wait_ge(up_full, rep * 8 * NCH + 2 * NCH + 6 * i + j + 1)
                    src = PS[:, bank:bank + 2, :] if w == 2 else PS[:, bank, :]
                    act.activation(h[:], src, ACT.Gelu).then_inc(up_read, 1)

        def f_vector(v, link, ans, nth, rep):
            base = FIRST_RESULT[nth]
            v.wait_ge(x_ready, nth)
            if rep == 0:
                v.sem_inc(o_read, OBANKS)
                v.sem_inc(h1_ready, 1)
                v.sem_inc(down_read, 1)
                v.wait_ge(w_loaded, W_LOADED)
                v.tensor_scalar(fw[:, 0:3 * D], fw[:, 0:3 * D], fn[:, 0:1], None, ALU.mult).then_inc(fw_ready, 1)
                v.tensor_scalar(fw[:, 3 * D:], fw[:, 3 * D:], fn[:, 1:2], None, ALU.mult).then_inc(fw_ready, 1)
                v.tensor_reduce(kwmax[:], fqk[:, 1], AX.X, ALU.max, apply_absolute_value=True).then_inc(fw_ready, 1)
                v.wait_ge(fw_ready, 3)
                link(v.tensor_scalar(kwmax[:], kwmax[:], HD ** 0.5, None, ALU.mult))
                v.tensor_scalar(fqk[:, 0], fqk[:, 0], HD ** -0.5, None, ALU.mult).then_inc(fw_ready, 1)
                v.wait_ge(fw_ready, 4)
            dve_norm(v, link, ans, LN_EPS, F_EPS)
            for b in range(B):
                tb = slice(b * TB, (b + 1) * TB)
                v.wait_ge(psum_read, base + NCH + TB * (b + 1))
                qk = QKV[:, tb, 0:2 * D].rearrange("p t (n d) -> p t n d", d=HD)
                to = QKS[:, tb].rearrange("p t (n d) -> p t n d", d=HD)
                link(v.tensor_tensor(to, qk, qk, ALU.mult))
                link(v.tensor_reduce(qst[:, tb], to, AX.X, ALU.add))
                v.tensor_scalar(qst[:, tb], qst[:, tb], 1.0 / HD, F_EPS, ALU.mult, ALU.add).then_inc(to_act, 1)
                ans.wait()
                link(v.reciprocal(qst2[:, tb], qst[:, tb]))
                link(v.tensor_tensor(to, qk, bcast(qst2[:, tb], 3, HD), ALU.mult))
                for n in range(2):
                    half = QKS[:, tb, n * D:(n + 1) * D].rearrange("p t (h d) -> p t h d", d=HD)
                    w = bcast(bcast(fqk[:, n], 1, H), 1, TB)
                    ins = v.tensor_tensor(half, half, w, ALU.mult)
                    if n == 0:
                        link(ins)
                    else:
                        ins.then_inc(qk_normed, 1)
                v.wait_ge(qk_normed, rep * B + b + 1)
                q, k = QKS[:, tb, 0:D], QKS[:, tb, D:2 * D]
                sq = SQ[:, tb]
                heads = sq.rearrange("p t (h d) -> p t h d", d=HD)
                link(v.tensor_tensor(sq, q, k, ALU.mult))
                link(v.tensor_reduce(qst[:, tb, 0:H], heads, AX.X, ALU.add))
                link(v.tensor_tensor(sq, q, q, ALU.mult))
                link(v.tensor_reduce(qst[:, tb, H:2 * H], heads, AX.X, ALU.add))
                v.tensor_scalar(qst[:, tb, H:2 * H], qst[:, tb, H:2 * H], 0.0, None, ALU.max).then_inc(to_act, 1)
                ans.wait()
                link(v.tensor_scalar(qst[:, tb, H:2 * H], qst[:, tb, H:2 * H], kwmax[:], -SHIFT, ALU.mult, ALU.add))
                link(v.tensor_tensor(qst2[:, tb, 0:H], qst[:, tb, 0:H], qst[:, tb, H:2 * H], ALU.max))
                v.tensor_scalar(qst2[:, tb, 0:H], qst2[:, tb, 0:H], -1.0, None, ALU.mult).then_inc(shifts_ready, 1)
            for c in range(NCH):
                for n in range(2):
                    r = base + NCH + TILES + 2 * c + n
                    v.wait_ge(part_high, (rep * NCH + c) * 2 + n + 1)
                    v.tensor_tensor(QR[:, n], PS[:, r % 8, :], QP[0][:, n], ALU.subtract).then_inc(psum_read, 1)
                v.wait_ge(part_mid, rep * NCH + c + 1)
                v.tensor_tensor(QP[2][:], QR[:], QP[1][:], ALU.subtract).then_inc(parts_ready, 1)
                v.wait_ge(parts_ready, rep * NCH + c + 1)
            for g in range(NG):
                n = rep * NG + g
                for b in range(B):
                    for qc in range(2):
                        done = b * NA_B + (NA_Q0 if qc == 0 else NA_B)
                        at = (n * B + b) * 2 + qc
                        o = PS[:, SCORES_BANKS + qc, :]
                        t = b * S + qc * CH
                        v.wait_ge(probs_used, DEPTH + n * NA + done)
                        v.wait_ge(o_read, OBANKS + at)
                        v.stream_shuffle(DEN[:], o, [HD] * 32).then_inc(den_ready, 1)
                        v.wait_ge(den_ready, 2 * at + 1)
                        v.reciprocal(DEN[:], DEN[:]).then_inc(den_ready, 1)
                        v.wait_ge(den_ready, 2 * at + 2)
                        v.tensor_tensor(AO[:, g, t:t + CH], o, DEN[:], ALU.mult).then_inc(o_read, 1)
            first = base + NCH + TILES + 3 * NCH
            for c in range(NCH):
                v.wait_ge(psum_full, first + c + 1)
                t = slice(c * TPC, (c + 1) * TPC)
                v.tensor_tensor(XL[:, t, KEEP:], XL[:, t, KEEP:],
                                PS[:, (first + c) % 8, 0:TPC * OUTC].rearrange("p (t d) -> p t d", d=OUTC),
                                ALU.add).then_inc(psum_read, 1)
            v.wait_ge(psum_read, first + NCH)
            link(v.tensor_tensor(SQ[:], XL[:], XL[:], ALU.mult))
            link(v.tensor_reduce(stat[:], SQ[:], AX.X, ALU.add))
            v.tensor_scalar(stat[:], stat[:], 1.0 / D, F_EPS, ALU.mult, ALU.add).then_inc(to_act, 1)
            ans.wait()
            link(v.reciprocal(rrms[:], stat[:]))
            v.tensor_tensor(SQ[:], XL[:], bcast(rrms[:], 2, D), ALU.mult).then_inc(normed, 1)
            v.tensor_tensor(X[:], X[:], XL[:], ALU.add).then_inc(x_sum, 1)
            first += 2 * NCH
            v.wait_ge(psum_full, first + 1)
            v.tensor_scalar(lg[:].rearrange("p t e -> p (t e)"), PS[:, first % 8, 0:TILES * E4], FLT_MAX, -FLT_MAX,
                            ALU.min, ALU.max).then_inc(psum_read, 1)
            v.wait_ge(psum_read, first + 1)
            link(v.tensor_reduce(red[:], lg[:], AX.X, ALU.max))
            v.tensor_tensor(lg[:], lg[:], bcast(red[:], 2, E4), ALU.subtract).then_inc(to_act, 1)
            ans.wait()
            link(v.tensor_reduce(red[:], pr[:], AX.X, ALU.add))
            link(v.reciprocal(red[:], red[:]))
            link.open(v.tensor_tensor(pr[:], pr[:], bcast(red[:], 2, E4), ALU.mult))
            link(v.memset(cnt[:], 0.0))
            for i in range(E4):
                for j in range(i):
                    link(v.tensor_tensor(ge[:], pr[:, :, j], pr[:, :, i], ALU.is_ge))
                    link.open(v.tensor_tensor(cnt[:, :, i], cnt[:, :, i], ge[:], ALU.add))
                    link(v.tensor_scalar(red[:], ge[:], -1.0, 1.0, ALU.mult, ALU.add))
                    link(v.tensor_tensor(cnt[:, :, j], cnt[:, :, j], red[:], ALU.add))
            link(v.tensor_scalar(cnt[:], cnt[:], 2.0, None, ALU.is_lt))
            link(v.tensor_tensor(wts[:], pr[:], cnt[:], ALU.mult))
            link(v.tensor_reduce(red[:], wts[:], AX.X, ALU.add))
            link(v.tensor_scalar(red[:], red[:], TOP_EPS, None, ALU.add))
            link(v.reciprocal(red[:], red[:]))
            link(v.tensor_tensor(wts[:], wts[:], bcast(red[:], 2, E4), ALU.mult))
            v.wait_ge(x_sum, rep + 1)

            def add_expert(tile, e, src):
                xt = X[:, bass.ds(tile, 1), KEEP:]
                return v.scalar_tensor_tensor(out=xt, in0=src.unsqueeze(1), scalar=wts[:, bass.ds(tile, 1), e],
                                              in1=xt, op0=ALU.mult, op1=ALU.add)

            with v.Fori(0, NCH) as i:
                v.wait_ge(up_read, rep * UPS + i + 1)
                v.wait_ge(up_full, rep * 8 * NCH + 2 * i + 2)
                v.tensor_tensor(HG[1][:], HG[0][:], PS[:, 2:4, :], ALU.mult).then_inc(h1_ready, 1)
                for t in range(TPC):
                    n = rep * 2 * TILES + i * TPC + t
                    v.wait_ge(down_full, n + 1)
                    add_expert(i * TPC + t, 1, PS[:, 4 + t, 0:OUTC]).then_inc(down_read, 1)
            v.wait_ge(down_read, rep * 2 * TILES + TILES + 1)
            with v.Fori(0, NCH) as i:
                for t in range(TPC):
                    n = rep * 2 * TILES + TILES + i * TPC + t
                    v.wait_ge(down_full, n + 1)
                    for j, e in enumerate((0, 2, 3)):
                        ins = add_expert(i * TPC + t, e, PS[:, 6 + t % 2, j * OUTC:(j + 1) * OUTC])
                        if j < 2:
                            at = ((rep * NCH + i) * TPC + t) * 2 + j + 1
                            ins.then_inc(expert_added, 1)
                            v.wait_ge(expert_added, at)
                        else:
                            ins.then_inc(down_read, 1)
            v.wait_ge(down_read, (rep + 1) * 2 * TILES + 1)
            v.nop().then_inc(x_ready, 1)

        LAYERS = 'AFBF'
        RESULTS = {"A": A_RES, "B": B_RES, "F": F_RES}
        NORMS = {"A": 1, "B": 1, "F": 2}
        FIRST_RESULT = [sum(RESULTS[l] for l in LAYERS[:n]) for n in range(len(LAYERS))]
        FIRST_NORM = [sum(NORMS[l] for l in LAYERS[:n]) for n in range(len(LAYERS))]
        block = ctx.enter_context(nc.Block())

        @block.sync
        def _(sp):
            a_sync(sp)
            w_sync(sp)
            for n, layer in enumerate(LAYERS):
                if layer == "F":
                    f_sync(sp, n, LAYERS[:n].count("F"))
            sp.wait_ge(x_ready, len(LAYERS))
            sp.dma_start(out.rearrange("(t p) d -> p t d", p=P), X[:]).then_inc(out_stored, 16)
            sp.wait_ge(out_stored, 16)

        @block.tensor
        def _(pe):
            banks = Banks(pe)
            for n, layer in enumerate(LAYERS):
                if layer == "A":
                    a_tensor(pe, banks)
                elif layer == "B":
                    b_tensor(pe, banks, n)
                else:
                    f_tensor(pe, banks, n, LAYERS[:n].count("F"))

        @block.scalar
        def _(act):
            link, ask, reads = Chain(act, act_chain), Tally(act, to_act), Reads(act)
            for n, layer in enumerate(LAYERS):
                if layer == "A":
                    a_scalar(act, link, ask, reads)
                elif layer == "B":
                    b_scalar(act, link, ask, reads)
                else:
                    f_scalar(act, link, ask, reads, n, LAYERS[:n].count("F"))

        @block.vector
        def _(v):
            link, ans = Chain(v, dve_chain), Tally(v, to_dve)
            for n, layer in enumerate(LAYERS):
                if layer == "A":
                    a_vector(v, link, ans)
                elif layer == "B":
                    b_vector(v, link, ans, n)
                else:
                    f_vector(v, link, ans, n, LAYERS[:n].count("F"))

        @block.gpsimd
        def _(pool):
            link = Chain(pool, pool_chain)
            for n, layer in enumerate(LAYERS):
                if layer == "A":
                    a_gpsimd(pool, link)
                elif layer == "F":
                    f_gpsimd(pool, link, n, LAYERS[:n].count("F"))


def dft_tables():
    import numpy as np
    n = np.arange(D)[:, None]
    f = np.arange(NB)[None, :]
    turn = (n * f) % D
    cos = np.cos(2 * np.pi * turn / D)
    sin = np.sin(2 * np.pi * turn / D)
    sin[(2 * turn) % D == 0] = 0.0
    weight = np.where((f == 0) | (f == D // 2), 1.0, 2.0) / D
    forward = np.stack([cos, -sin], 1).astype(np.float32)
    back = np.zeros((P, 2, D), np.float32)
    back[:NB, 0] = (weight * cos).T
    back[:NB, 1] = (-weight * sin).T
    return forward, back


def kernel(**inputs):
    import numpy as np
    import concourse.bacc as bacc
    from concourse.bass_utils import run_bass_kernel_spmd as run

    g = {k: np.asarray(v) for k, v in inputs.items()}
    a = lambda name: g["L0_attn_a_" + name]
    f = lambda name: g["L0_ffn_" + name]
    W, bias = a("W_ctrl"), a("b_ctrl")
    ug, ang, cand, q, k, v, al, be, og = np.split(np.arange(W.shape[1]), np.cumsum([D, D // 2, D, D, D, D, H, H]))
    pick = np.concatenate([q, k, v, ug[0::2], ug[1::2], cand[0::2], cand[1::2], ang, og])
    a_w = W[:, pick]
    a_wab = np.zeros((D, 4, BH), np.float32)
    for w, cols in enumerate((al, be)):
        for b in range(B):
            a_wab[:, 2 * w + b, b * H:(b + 1) * H] = W[:, cols]
    two = lambda t: np.concatenate([t, t])
    small = [bias[q], bias[k], bias[v]]
    small += [a(n)[:, j] for n in ("qconv_w", "kconv_w", "vconv_w") for j in range(4)]
    small += [two(bias[c]) for c in (ug[0::2], ug[1::2], cand[0::2], cand[1::2], ang)]
    small += [two(a("W_block")[:, i, j]) for i in range(2) for j in range(2)]
    small += [np.tile(bias[al], SEG * B), np.tile(bias[be], SEG * B)]
    small += [np.tile(a("rms_m_w"), H), two(a("rms_v_w")[0::2]), two(a("rms_v_w")[1::2])]
    W_out = a("W_out")
    forward, back = dft_tables()
    b_w = np.stack([g["L0_attn_b_W" + n] for n in "qkv"], 1)
    down = lambda n: f(n).T[:, KEEP:].reshape(2, P, OUTC).transpose(1, 0, 2)
    mid = lambda n: f(n).T.reshape(2, P, HID).transpose(1, 0, 2)
    wo = np.zeros((P, NG, OUTC), np.float32)
    for n in range(H):
        wo[32 * (n % GH):32 * (n % GH) + HD, n // GH] = f("wo").T[n * HD:(n + 1) * HD, KEEP:]
    arrays = {
        "x": a("hidden").reshape(NT, D), "a_w": a_w, "a_wab": a_wab, "a_small": np.stack(small, 1),
        "a_bog": bias[og], "a_bout": a("b_out"),
        "a_wout": np.stack([W_out[:D], two(W_out[D::2]), two(W_out[D + 1::2])], 1),
        "b_w": b_w, "b_dft": forward, "b_idft": back,
        "f_w": np.concatenate([f(n).T for n in ("wq", "wk", "wv", "gate_w", "e0_up", "e1_w1", "e1_w2", "e2_l1",
                                                "e3_down")], 1),
        "f_n": np.stack([f("n1_w"), f("n2_w")], 1), "f_qk": np.concatenate([f("qn_w"), f("kn_w")]),
        "f_mid": np.concatenate([mid("e2_l2"), mid("e2_l3"), f("e3_up").T[:, None]], 1),
        "f_down": np.stack([down(n) for n in ("e0_down", "e1_down", "e2_l4", "e3_out")], 1),
        "f_wo": wo, "eye": np.eye(P, dtype=np.float32),
        "causal": np.where(np.arange(P)[:, None] > np.arange(P)[None, :], MASKED, 0.0).astype(np.float32),
    }
    nc = bacc.Bacc("TRN2", target_bir_lowering=False, num_devices=1)
    arrays = {n: np.ascontiguousarray(t) for n, t in arrays.items()}
    args = {n: nc.dram_tensor(n, t.shape, F32, kind="ExternalInput").ap() for n, t in arrays.items()}
    out = nc.dram_tensor("out", (NT, D), F32, kind="ExternalOutput").ap()
    hybrid_kernel(nc, out=out, **args)
    got = run(nc, [arrays], core_ids=[0]).results[0]["out"]
    return got.reshape(B, S, D)
```

```python
from contextlib import ExitStack

import concourse.bass as bass
from concourse import mybir

ALU = mybir.AluOpType
ACT = mybir.ActivationFunctionType
AX = mybir.AxisListType
F32 = mybir.dt.float32
BF16 = mybir.dt.bfloat16

P = 128
B, S, D = 2, 1024, 128
NT = B * S
TILES = NT // P
TB = TILES // B
H, HD = 16, 8
SEG, C = 4, 16
BH = B * H
ST = S // SEG
NC = ST // C
CH = 512
NCH = NT // CH
TPC = CH // P
NB = D // 2 + 1
KEEP = 32
OUTC = D - KEEP
HID = 256
E4 = 4
LN_EPS, A_EPS, L2_EPS, B_EPS, F_EPS = 1e-5, 1e-6, 1e-12, 1e-8, 1.1920929e-07
TOP_EPS = 1e-8
SHIFT = 80.0
FLT_MAX = 3.4028234663852886e38
MASKED = -1.0e30
MAGIC = 12582912.0
TWO_PI = 6.283185307179586
TWO_PI_HI = 6.28125
PI = 3.1415925

A_Q, A_K, A_V, A_UE, A_UO, A_CE, A_CO, A_ANG, A_OG, A_COLS = 0, 128, 256, 384, 448, 512, 576, 640, 704, 832
S_BQKV, S_CONV, S_BPAIR, S_WB, S_BAB, S_RMS, S_COLS = 0, 3, 15, 20, 24, 26, 29
F_QKV, F_GATE, F_E0, F_E1A, F_E1B, F_E2, F_E3, F_COLS = 0, 384, 388, 644, 900, 1156, 1412, 1540
Q_SIDE = (0, 1, 0, 1, 2, 0)
K_SIDE = (0, 0, 1, 1, 0, 2)
NSLOT = len(Q_SIDE)
QROWS = NSLOT * HD + 1
GH = 4
NG = H // GH


class Tally:

    def __init__(self, eng, sem):
        self.eng, self.sem, self.n = eng, sem, 0

    def wait(self, more=1):
        self.n = self.n + more
        self.eng.wait_ge(self.sem, self.n)


class Chain:

    def __init__(self, eng, sem):
        self.eng, self.sem, self.n = eng, sem, 0

    def __call__(self, ins):
        self.open(ins)
        self.close()

    def open(self, ins):
        ins.then_inc(self.sem, 1)
        self.n = self.n + 1

    def close(self):
        self.eng.wait_ge(self.sem, self.n)


def hybrid_kernel(nc, x, a_w, a_wab, a_small, a_bog, a_bout, a_wout, b_w, b_dft, b_idft,
                  f_w, f_n, f_qk, f_mid, f_down, f_wo, eye, causal, out):
    ctx = ExitStack()
    with ctx:
        def sem(name):
            return ctx.enter_context(nc.semaphore(name))

        def sb(name, shape, dt=F32, at=None, side=None):
            return (at or ctx).enter_context(nc.sbuf_tensor(name, shape, dt, side=side))

        def dram(name, shape, dt=F32):
            return nc.dram_tensor(name, shape, dt, kind="Internal").ap()

        X = sb("X", [P, TILES, D])
        XL = sb("XL", [P, TILES, D])
        SQ = sb("SQ", [P, TILES, D])
        HT = sb("HT", [P, NT])
        ident = sb("ident", [P, P])
        stat = sb("stat", [P, TILES])
        var = sb("var", [P, TILES])
        bst = sb("bst", [P, TILES, 6])
        mv = sb("mv", [P, TILES, 2])
        rstd = sb("rstd", [P, TILES])
        rrms = sb("rrms", [P, TILES])
        PS = ctx.enter_context(nc.psum_tensor("PS", [P, 8, CH], F32))

        with ExitStack() as sa:
            aw = sb("aw", [P, A_COLS], at=sa)
            awab = sb("awab", [P, 4, 32], at=sa)
            asm = sb("asm", [P, S_COLS], at=sa)
            nwb = sb("nwb", [P, 4], at=sa)
            abog = sb("abog", [P, D], at=sa)
            about = sb("about", [P, D], at=sa)
            awout = sb("awout", [P, 3, D], at=sa)
            ones = sb("ones", [P, 1], at=sa)
            ALP = sb("ALP", [P, ST], at=sa)
            BET = sb("BET", [P, ST], at=sa)
            V0 = sb("V0", [P, 2, S], at=sa)
            LQK = sb("LQK", [P, 2, HD, ST], at=sa)
            WU = sb("WU", [P, 2 * HD, ST], at=sa)
            AC1 = sb("AC1", [P, NC], at=sa)
            KB = XL[:].rearrange("p t d -> p (t d)").rearrange("p (d s) -> p d s", d=HD)
            VS = HT[:].rearrange("p (e s) -> p e s", e=2)
            DJ = WU[:, HD:2 * HD, :]
            SJ = WU[:, 0:4, :].rearrange("p a (c j i) -> p a c j i", c=NC, j=2)
            with ExitStack() as s1:
                CQ = [sb(f"CQ{i}", [P, B, S + 3], at=s1) for i in range(2)]
                TRA = [sb(f"TRA{l}", [P, 2, 3, S >> l], at=s1) for l in range(11)]
                TRV = [V0] + [sb(f"TRV{l}", [P, 2, S >> l], at=s1) for l in range(1, 11)]
                TRT = sb("TRT", [P, 2, 3, S // 2], at=s1)
                CY = [sb(f"CY{i}", [P, B, S], at=s1) for i in range(2)]
                UEO = sb("UEO", [P, 2, S], at=s1)
                ANG = sb("ANG", [P, S], at=s1)
                SIN = sb("SIN", [P, S], at=s1)
                COS = sb("COS", [P, S], at=s1)
            with ExitStack() as s23:
                PA = sb("PA", [P, NC, C, C], at=s23)
                with ExitStack() as sk:
                    K2 = sb("K2", [P, SEG, HD, ST], at=sk)
                    with ExitStack() as s2:
                        PRD = sb("PRD", [P, 2 * HD * ST], at=s2)
                        PRP = [sb(f"PRP{i}", [P, HD * ST], at=s2) for i in range(2)]
                        SS = sb("SS", [P, 2, ST], at=s2)
                        RS = sb("RS", [P, 2, ST], at=s2)
                        NG0 = sb("NG0", [P, ST], at=s2)
                        GAM = sb("GAM", [P, NC, C + 1, C + 1], at=s2)
                        LA = sb("LA", [P, NC, C, C], at=s2)
                    with ExitStack() as s3:
                        W2 = sb("W2", [P, SEG, HD, ST], at=s3)
                        U2 = sb("U2", [P, SEG, 2, ST], at=s3)
                        D2 = sb("D2", [P, SEG, 2, ST], at=s3)
                        S2 = sb("S2", [P, SEG * NC + 1, 2, HD], at=s3)
                        AC2 = sb("AC2", [P, SEG, NC], at=s3)
                        P1 = sb("P1", [P, 2, 2, C, HD + 1], at=s3)
                        P2 = sb("P2", [P, 2, HD, C + 1], at=s3)
                with ExitStack() as s4:
                    RO = sb("RO", [P, HD, ST], at=s4)
                    RP = sb("RP", [P, HD, ST], at=s4)
                    PRR = sb("PRR", [P, NC * C * HD], at=s4)
                    PRQ = [sb(f"PRQ{i}", [P, NC * HD * C], at=s4) for i in range(2)]
                    RT = sb("RT", [P, B, S], at=s4)
                    SS4 = sb("SS4", [P, ST], at=s4)
                    OT = sb("OT", [P, TILES, D], at=s4)
                    vss = sb("vss", [P, TILES], at=s4)
        qkv_d = dram("qkv_d", (3, B, D, S))
        w_d = dram("w_d", (SEG, BH, HD, ST))
        k_d = dram("k_d", (SEG, BH, HD, ST))
        u_d = dram("u_d", (SEG, BH, HD, ST))
        ac_d = dram("ac_d", (BH, SEG, NC))
        d_d = dram("d_d", (SEG, BH, HD, ST))
        s_d = dram("s_d", (SEG, BH, 4, NC * 2 * HD))
        r_d = dram("r_d", (BH, HD, S))

        with ExitStack() as sw:
            bw = sb("bw", [P, 3, D], at=sw, side="right")
            bdft = sb("bdft", [P, 2, NB], at=sw, side="right")
            bidft = sb("bidft", [P, 2, D], at=sw, side="right")
            bwf = sb("bwf", [P, 3, 2, NB], at=sw, side="right")
            identb = sb("identb", [P, P], BF16, at=sw, side="right")
            maskb = sb("maskb", [P, P], BF16, at=sw, side="right")
            maskf = sb("maskf", [P, P], at=sw, side="right")
            fw = sb("fw", [P, F_COLS], at=sw, side="right")
            fn = sb("fn", [P, 2], at=sw, side="right")
            fqk = sb("fqk", [P, 2, HD], at=sw, side="right")
            fmid = sb("fmid", [P, 5, HID], at=sw, side="right")
            fdown = sb("fdown", [P, E4, 2, OUTC], at=sw, side="right")
            fwo = sb("fwo", [P, NG, OUTC], at=sw, side="right")
            KS = [sb(f"KS{i}", [P, GH, S], BF16, at=sw) for i in range(2)]
            QS = [sb(f"QS{i}", [P, GH, S], BF16, at=sw) for i in range(2)]
            VA = [sb(f"VA{i}", [P, TB, GH, 32], at=sw) for i in range(2)]
            with ExitStack() as sB:
                QF = [sb(f"QF{i}", [P, 3, 2, CH], at=sB) for i in range(3)]
                KV = [sb(f"KV{i}", [P, 4, CH], at=sB) for i in range(2)]
                SQF = sb("SQF", [P, 2, 2, CH], at=sB)
                mag = sb("mag", [P, 2, CH], at=sB)
                PRB = sb("PRB", [P, 4, CH], at=sB)
                CUM = sb("CUM", [P, 2, B, S], at=sB)
                YF = sb("YF", [P, 2, NT], at=sB)
            with ExitStack() as sF:
                QKV = sb("QKV", [P, TILES, 3 * D], at=sF)
                PX = [sb(f"PX{i}", [P, 2, CH], at=sF) for i in range(3)]
                DEN = sb("DEN", [P, CH], at=sF)
                with ExitStack() as f0:
                    QKS = sb("QKS", [P, TILES, 2 * D], at=f0)
                    qst = sb("qst", [P, TILES, 2 * H], at=f0)
                    qst2 = sb("qst2", [P, TILES, 2 * H], at=f0)
                    QR = [sb(f"QR{i}", [P, 2, CH], at=f0) for i in range(2)]
                AO = sb("AO", [P, NG, NT], at=sF)
                with ExitStack() as f1:
                    MT = sb("MT", [H, NT], BF16, at=f1)
                    QP = [sb(f"QP{i}", [P, 2, NT], BF16, at=f1) for i in range(3)]
                with ExitStack() as f3:
                    lg = sb("lg", [P, TILES, E4], at=f3)
                    pr = sb("pr", [P, TILES, E4], at=f3)
                    cnt = sb("cnt", [P, TILES, E4], at=f3)
                    ge = sb("ge", [P, TILES], at=f3)
                    red = sb("red", [P, TILES], at=f3)
                    wts = sb("wts", [P, TILES, E4], at=f3)
                    HS = [sb(f"HS{i}", [P, 2, CH], at=f3) for i in range(2)]
                    HG = [sb(f"HG{i}", [P, 2, CH], at=f3) for i in range(2)]
                    H0 = [sb(f"H0{i}", [P, 2, CH], at=f3) for i in range(2)]
                    HA = sb("HA", [P, 2, CH], at=f3)
                    HB = sb("HB", [P, 2, CH], at=f3)
                    HC = sb("HC", [P, 2, CH], at=f3)
                    HE = sb("HE", [P, CH], at=f3)
                    HF = sb("HF", [P, 2, CH], at=f3)
        qs_d = dram("qs_d", (H, QROWS, NT), BF16)
        ks_d = dram("ks_d", (H, QROWS, NT), BF16)


        psum_read = sem("psum_read")
        psum_full = sem("psum_full")
        to_act = sem("to_act")
        normed = sem("normed")
        to_dve = sem("to_dve")
        x_loaded = sem("x_loaded")
        a_loaded = sem("a_loaded")
        silu_done = sem("silu_done")
        qkv_stored = sem("qkv_stored")
        lanes_loaded = sem("lanes_loaded")
        k_decayed = sem("k_decayed")
        k_stored = sem("k_stored")
        k_loaded = sem("k_loaded")
        wk_ready = sem("wk_ready")
        wk_stored = sem("wk_stored")
        u_solved = sem("u_solved")
        u_stored = sem("u_stored")
        seg_loaded = [sem(f"seg_loaded{i}") for i in range(SEG)]
        chunk_done = sem("chunk_done")
        ds_stored = sem("ds_stored")
        ds_loaded = sem("ds_loaded")
        reads_ready = sem("reads_ready")
        reads_stored = sem("reads_stored")
        rt_loaded = sem("rt_loaded")
        wout_ready = sem("wout_ready")
        vs_ready = sem("vs_ready")
        trig_in = sem("trig_in")
        trig_ready = sem("trig_ready")
        conv_done = sem("conv_done")
        pads_clear = sem("pads_clear")
        gate_ready = sem("gate_ready")
        state_clear = sem("state_clear")
        u_slot = sem("u_slot")
        s_slot = sem("s_slot")
        tree_in = sem("tree_in")
        level_done = sem("level_done")
        lanes_clear = sem("lanes_clear")
        kb_ready = sem("kb_ready")
        prod_ready = sem("prod_ready")
        prod_used = sem("prod_used")
        la_ready = sem("la_ready")
        rprod_ready = sem("rprod_ready")
        rprod_used = sem("rprod_used")
        x_ready = sem("x_ready")
        w_loaded = sem("w_loaded")
        y_ready = sem("y_ready")
        values_added = sem("values_added")
        values_full = sem("values_full")
        squares_ready = sem("squares_ready")
        unit_ready = sem("unit_ready")
        kv_ready = sem("kv_ready")
        sums_ready = sem("sums_ready")
        stack_clear = sem("stack_clear")
        parts_stored = sem("parts_stored")
        part_high = sem("part_high")
        parts_ready = sem("parts_ready")
        probs_used = sem("probs_used")
        stack_loaded = [sem(f"stack_loaded{i}") for i in range(B)]
        v_ready = sem("v_ready")
        fw_ready = sem("fw_ready")
        shifts_ready = sem("shifts_ready")
        qk_normed = sem("qk_normed")
        probs_ready = sem("probs_ready")
        scores_ready = sem("scores_ready")
        o_read = sem("o_read")
        proj_full = sem("proj_full")
        up_full = sem("up_full")
        up_read = sem("up_read")
        h1_ready = sem("h1_ready")
        down_read = sem("down_read")
        down_full = sem("down_full")
        q_squared = sem("q_squared")
        rest_ready = sem("rest_ready")
        den_ready = sem("den_ready")
        proj_added = sem("proj_added")
        x_sum = sem("x_sum")
        out_stored = sem("out_stored")
        act_chain = sem("act_chain")
        dve_chain = sem("dve_chain")
        pool_chain = sem("pool_chain")

        def bcast(ap, at, n):
            ap = ap.unsqueeze(at)
            shape = list(ap.shape)
            shape[at] = n
            return ap.to_broadcast(shape)

        class Banks:

            def __init__(self, pe):
                self.pe, self.n = pe, 0

            def take(self):
                if self.n >= 8:
                    self.pe.wait_ge(psum_read, self.n - 7)
                self.n += 1
                return (self.n - 1) % 8

            def all_read(self):
                self.pe.wait_ge(psum_read, self.n)

        class Reads:

            def __init__(self, eng):
                self.eng, self.n = eng, 0

            def next(self):
                self.n += 1
                self.eng.wait_ge(psum_full, self.n)
                return (self.n - 1) % 8

        def dve_norm(v, link, ans, eps, dst, rms_eps=None):
            v.tensor_scalar(stat[:], mv[:, :, 1], eps, None, ALU.add).then_inc(to_act, 1)
            ans.wait()
            link(v.reciprocal(rstd[:], stat[:]))
            scale = rstd
            if rms_eps is not None:
                link(v.tensor_tensor(var[:], mv[:, :, 1], rstd[:], ALU.mult))
                link(v.tensor_tensor(var[:], var[:], rstd[:], ALU.mult))
                v.tensor_scalar(stat[:], var[:], rms_eps, None, ALU.add).then_inc(to_act, 1)
                ans.wait()
                link(v.reciprocal(rrms[:], stat[:]))
                link(v.tensor_tensor(rrms[:], rrms[:], rstd[:], ALU.mult))
                scale = rrms
            for b in range(B):
                for t in range(b * TB, (b + 1) * TB):
                    last = center_and_scale(v, dst, t, scale)
                last.then_inc(normed, 1)

        def dve_stats(v, link, tiles):
            for t in tiles:
                link.open(v.bn_stats(bst[:, t], X[:, t]))
            link.close()
            for t in tiles:
                link.open(v.bn_aggr(mv[:, t], bst[:, t]))
            link.close()

        def center_and_scale(v, dst, t, scale):
            return v.tensor_scalar(dst[:, t], X[:, t], mv[:, t, 0:1], scale[:, t:t + 1], ALU.subtract, ALU.mult)

        def act_sqrt(act, ask, ap):
            ask.wait()
            act.activation(ap, ap, ACT.Sqrt).then_inc(to_dve, 1)

        def pe_transpose_in(pe, banks, src, norm, chunks=range(NCH), at=None):
            for g in chunks:
                if g % (NCH // B) == 0:
                    pe.wait_ge(normed, norm * B + g // (NCH // B) + 1)
                k = banks.take()
                if at is not None:
                    k = at + g
                for i in range(TPC):
                    last = pe.transpose(PS[:, k, i * P:(i + 1) * P], src[:, g * TPC + i, :], ident[:])
                last.then_inc(psum_full, 1)

        def act_ht(act, reads, chunks=range(NCH), at=None):
            for g in chunks:
                k = reads.next()
                if at is not None:
                    k = at + g
                act.activation(HT[:, g * CH:(g + 1) * CH], PS[:, k, :], ACT.Copy).then_inc(psum_read, 1)

        A_RES = 34

        def lanes(t):
            return t.rearrange("p d (c s) -> p c s d", s=C)

        def a_sync(sp):
            for half in range(2):
                t = slice(half * TB, (half + 1) * TB)
                sp.dma_start(X[:, t, :], x.rearrange("(t p) d -> p t d", p=P)[:, t, :]).then_inc(x_loaded, 16)
            sp.dma_start(ident[:], eye).then_inc(x_loaded, 16)
            for dst, src in ((aw, a_w), (awab, a_wab), (asm, a_small), (awout, a_wout)):
                sp.dma_start(dst[:], src).then_inc(a_loaded, 16)
            sp.dma_start(abog[:], a_bog.partition_broadcast(P)).then_inc(a_loaded, 16)
            sp.dma_start(about[:], a_bout.partition_broadcast(P)).then_inc(a_loaded, 16)
            for n in range(3):
                sp.wait_ge(silu_done, n + 1)
                sp.dma_start(qkv_d[n].rearrange("b p s -> p b s"), CY[n % 2][:]).then_inc(qkv_stored, 16)
                sp.wait_ge(qkv_stored, 16 * (n + 1))
                src = qkv_d[n].rearrange("b (h d) s -> (b h) d s", d=HD)
                for g in range(SEG):
                    rows = slice(g * BH, (g + 1) * BH)
                    dst = LQK[rows, n, :, :] if n < 2 else WU[rows, HD:2 * HD, :]
                    sp.dma_start(dst, src[:, :, g * ST:(g + 1) * ST]).then_inc(lanes_loaded, 16)
            sp.wait_ge(k_decayed, 1)
            sp.dma_start(k_d.rearrange("g h i t -> (g h) i t"), KB).then_inc(k_stored, 16)
            sp.dma_start(ac_d.rearrange("h g c -> g h c"), AC1[:]).then_inc(k_stored, 16)
            sp.wait_ge(k_stored, 32)
            for g in range(SEG):
                sp.dma_start(K2[:, g],
                             bcast(k_d[g].rearrange("h i t -> h (i t)"), 0, 4)).then_inc(k_loaded, 16)
            sp.wait_ge(wk_ready, 1)
            sp.dma_start(w_d.rearrange("g h i t -> (g h) i t"), WU[:, 0:HD, :]).then_inc(wk_stored, 16)
            sp.wait_ge(u_solved, 2)
            sp.dma_start(u_d.rearrange("g h i t -> (g h) i t"), WU[:, HD:2 * HD, :]).then_inc(u_stored, 16)
            sp.dma_start(AC2[:],
                         bcast(ac_d.rearrange("h g c -> h (g c)"), 0, 4)).then_inc(k_loaded, 16)
            sp.wait_ge(wk_stored, 16)
            for g in range(SEG):
                sp.dma_start(W2[:, g],
                             bcast(w_d[g].rearrange("h i t -> h (i t)"), 0, 4)).then_inc(seg_loaded[g], 16)
                if g == 0:
                    sp.wait_ge(u_stored, 16)
                sp.dma_start(U2[:, g],
                             u_d[g].rearrange("h (j e) t -> j h (e t)", j=4)).then_inc(seg_loaded[g], 16)
            w_sync(sp)
            for g in range(SEG):
                rows = slice(g * BH, (g + 1) * BH)
                sp.wait_ge(chunk_done, (g + 1) * NC)
                sp.dma_start(d_d[g].rearrange("h (j e) t -> j h (e t)", j=4),
                             D2[:, g]).then_inc(ds_stored, 16)
                sp.dma_start(s_d[g].rearrange("h j r -> j h r"),
                             S2[:, g * NC:(g + 1) * NC]).then_inc(ds_stored, 16)
                sp.wait_ge(ds_stored, 32 * (g + 1))
                sp.dma_start(DJ[rows], d_d[g]).then_inc(ds_loaded, 16)
                sp.dma_start(SJ[rows].rearrange("p a c j i -> p a (c j i)"), s_d[g]).then_inc(ds_loaded, 16)
            sp.wait_ge(reads_ready, 1)
            for g in range(SEG):
                sp.dma_start(r_d[:, :, g * ST:(g + 1) * ST], RO[g * BH:(g + 1) * BH]).then_inc(reads_stored, 16)
            sp.wait_ge(reads_stored, 64)
            sp.dma_start(RT[:], r_d.rearrange("(b h) j s -> (h j) b s", b=B)).then_inc(rt_loaded, 16)

        PAIRS = ((A_ANG, 4), (A_UE, 0), (A_UO, 1), (A_CE, 2), (A_CO, 3))

        def a_tensor(pe, banks):
            pe.wait_ge(x_loaded, 48)
            pe.wait_ge(a_loaded, 96)
            pe_transpose_in(pe, banks, XL, 0)
            banks.all_read()

            def pair(col):
                for c in range(S // CH):
                    k = banks.take()
                    for b in range(B):
                        t = b * S + c * CH
                        last = pe.matmul(PS[64 * b:64 * b + 64, k, :], aw[:, col:col + 64], HT[:, t:t + CH],
                                         start=True, stop=True)
                    last.then_inc(psum_full, 1)

            for col, _ in PAIRS[:3]:
                pair(col)
            k = banks.take()
            for w in range(2):
                for g in range(SEG):
                    for b in range(B):
                        t = b * S + g * ST
                        last = pe.matmul(PS[g * BH:(g + 1) * BH, k, w * ST:(w + 1) * ST], awab[:, 2 * w + b, :],
                                         HT[:, t:t + ST], start=(b == 0), stop=(b == B - 1))
            last.then_inc(psum_full, 1)
            for col, _ in PAIRS[3:]:
                pair(col)
            for col in (A_Q, A_K, A_V):
                for c in range(NCH):
                    k = banks.take()
                    pe.matmul(PS[:, k, :], aw[:, col:col + D], HT[:, c * CH:(c + 1) * CH],
                              start=True, stop=True).then_inc(psum_full, 1)
            for g in range(NCH):
                k = banks.take()
                for i in range(TPC):
                    t = (g * TPC + i) * P
                    last = pe.matmul(PS[:, k, i * P:(i + 1) * P], HT[:, t:t + P], aw[:, A_OG:A_OG + D],
                                     start=True, stop=True)
                last.then_inc(psum_full, 1)
            banks.all_read()
            pe.wait_ge(wout_ready, 3)
            pe.wait_ge(vs_ready, 1)
            for b in range(B):
                for t in range(TB):
                    last = pe.matmul(PS[:, b, t:t + 1], VS[64 * b:64 * b + 64, 0, t * P:(t + 1) * P],
                                     ones[64 * b:64 * b + 64, :], start=True, stop=True)
            last.then_inc(psum_full, 1)
            banks.n += 1
            for g in range(NCH):
                for i in range(TPC):
                    b, t = divmod(g * TPC + i, TB)
                    rows = slice(64 * b, 64 * b + 64)
                    for e in range(2):
                        last = pe.matmul(PS[:, 4 + g, i * P:(i + 1) * P], V0[rows, e, t * P:(t + 1) * P],
                                         awout[rows, 1 + e, :], start=(e == 0), stop=(e == 1))
            last.then_inc(psum_full, 1)
            banks.n += 1
            pe.wait_ge(rt_loaded, 16)
            pe.wait_ge(psum_read, 32)
            for g in range(NCH):
                for i in range(TPC):
                    b, t = divmod(g * TPC + i, TB)
                    last = pe.matmul(PS[:, g, i * P:(i + 1) * P], RT[:, b, t * P:(t + 1) * P], awout[:, 0, :],
                                     start=True, stop=True)
            last.then_inc(psum_full, 1)
            banks.n += 1

        def a_scalar(act, link, ask, reads):
            act_sqrt(act, ask, stat[:])
            act_ht(act, reads)
            act.wait_ge(a_loaded, 96)

            def bias(col):
                return asm[:, col:col + 1]

            def pair(dst, n, func):
                for c in range(S // CH):
                    k = reads.next()
                    act.activation(dst[:, c * CH:(c + 1) * CH], PS[:, k, :], func,
                                   bias=bias(S_BPAIR + n)).then_inc(psum_read, 1)

            pair(ANG[:], 4, ACT.Identity)
            pair(UEO[:, 0], 0, ACT.Sigmoid)
            pair(UEO[:, 1], 1, ACT.Sigmoid)
            k = reads.next()
            link(act.activation(ALP[:], PS[:, k, 0:ST], ACT.Sigmoid, bias=bias(S_BAB)))
            act.activation(BET[:], PS[:, k, ST:2 * ST], ACT.Sigmoid, bias=bias(S_BAB + 1)).then_inc(psum_read, 1)
            pair(TRA[0][:, 0, 2], 2, ACT.Silu)
            pair(TRA[0][:, 1, 2], 3, ACT.Silu)
            act.wait_ge(trig_in, 1)
            act.activation(SIN[:], SIN[:], ACT.Sin).then_inc(trig_ready, 1)
            act.activation(COS[:], COS[:], ACT.Sin).then_inc(trig_ready, 1)

            def take(n):
                if n >= 2:
                    act.wait_ge(conv_done, n - 1)
                else:
                    act.wait_ge(pads_clear, 3)
                for c in range(NCH):
                    k = reads.next()
                    b, h = divmod(c, S // CH)
                    act.activation(CQ[n % 2][:, b, 3 + h * CH:3 + (h + 1) * CH], PS[:, k, :], ACT.Identity,
                                   bias=bias(S_BQKV + n)).then_inc(psum_read, 1)

            def silu(n):
                act.wait_ge(conv_done, n + 1)
                act.activation(CY[n % 2][:], CY[n % 2][:], ACT.Silu).then_inc(silu_done, 1)

            take(0)
            take(1)
            silu(0)
            take(2)
            silu(1)
            silu(2)
            for g in range(NCH):
                k = reads.next()
                act.activation(SQ[:, g * TPC:(g + 1) * TPC, :].rearrange("p t d -> p (t d)"), PS[:, k, :],
                               ACT.Copy).then_inc(psum_read, 1)
            ask.wait()
            act.activation(SQ[:], SQ[:], ACT.Sigmoid).then_inc(gate_ready, 1)
            act_sqrt(act, ask, SS[:])
            act.wait_ge(state_clear, 1)
            act.wait_ge(k_loaded, 16 * (SEG + 1))

            def u_in(n):
                g, c = divmod(n, NC)
                if c == 0:
                    act.wait_ge(seg_loaded[g], 32)
                act.activation(P1[:, n % 2, :, :, HD], U2[:, g, :, c * C:(c + 1) * C], ACT.Copy).then_inc(u_slot, 1)

            u_in(0)
            for n in range(SEG * NC):
                g, c = divmod(n, NC)
                if n:
                    act.wait_ge(chunk_done, n)
                act.activation(P2[:, :, :, C], S2[:, n], ACT.Copy, scale=AC2[:, g, c:c + 1]).then_inc(s_slot, 1)
                if n + 1 < SEG * NC:
                    u_in(n + 1)
            act_sqrt(act, ask, SS4[:])
            act_sqrt(act, ask, vss[:])
            reads.n += 3

        def a_vector(v, link, ans):
            v.wait_ge(x_loaded, 48)
            dve_stats(v, link, range(TILES))
            dve_norm(v, link, ans, LN_EPS, XL)
            v.wait_ge(a_loaded, 96)
            link(v.tensor_scalar(nwb[:], asm[:, S_WB:S_WB + 4], -1.0, None, ALU.mult))
            for i in range(3):
                v.tensor_scalar(awout[:, i], awout[:, i], asm[:, S_RMS + i:S_RMS + i + 1], None,
                                ALU.mult).then_inc(wout_ready, 1)
            v.wait_ge(psum_read, 6)
            link(v.tensor_scalar(SIN[:], ANG[:], 1.0 / TWO_PI, MAGIC, ALU.mult, ALU.add))
            link(v.tensor_scalar(SIN[:], SIN[:], -MAGIC, None, ALU.add))
            link(v.scalar_tensor_tensor(out=ANG[:], in0=SIN[:], scalar=-TWO_PI_HI, in1=ANG[:], op0=ALU.mult, op1=ALU.add))
            link(v.scalar_tensor_tensor(out=ANG[:], in0=SIN[:], scalar=TWO_PI_HI - TWO_PI, in1=ANG[:],
                                        op0=ALU.mult, op1=ALU.add))
            link(v.tensor_scalar(SIN[:], ANG[:], -PI, PI, ALU.max, ALU.min))
            link(v.scalar_tensor_tensor(out=COS[:], in0=SIN[:], scalar=-1.0, in1=SIN[:], op0=ALU.mult, op1=ALU.min))
            v.tensor_scalar(COS[:], COS[:], TWO_PI / 4, None, ALU.add).then_inc(trig_in, 1)
            v.wait_ge(psum_read, 15)
            v.wait_ge(trig_ready, 2)
            tmp = TRT[:].rearrange("p a b s -> p (a b s)")[:, 0:S]
            wb = [asm[:, S_WB + i:S_WB + i + 1] for i in range(4)]
            for row, u in ((0, UEO[:, 0]), (1, UEO[:, 1])):
                link.open(v.tensor_tensor(ANG[:], u, COS[:], ALU.mult))
                link(v.tensor_tensor(tmp, u, SIN[:], ALU.mult))
                for i in range(2):
                    m = TRA[0][:, row, i, :]
                    first, by, second, by2 = ((ANG[:], wb[2 * i], tmp, nwb[:, 2 * i + 1:2 * i + 2]) if row == 0 else
                                              (tmp, wb[2 * i], ANG[:], wb[2 * i + 1]))
                    link(v.tensor_scalar(m, first, by, None, ALU.mult))
                    link(v.scalar_tensor_tensor(out=m, in0=second, scalar=by2, in1=m, op0=ALU.mult, op1=ALU.add))
            link(v.tensor_tensor(UEO[:], UEO[:], TRA[0][:, :, 2, :], ALU.mult))
            v.tensor_tensor(TRA[0][:, :, 2, :], TRA[0][:, :, 2, :], UEO[:], ALU.subtract).then_inc(tree_in, 1)
            for n in range(3):
                v.wait_ge(psum_read, 15 + NCH * (n + 1))
                if n >= 2:
                    v.wait_ge(qkv_stored, 16 * (n - 1))
                y, xq = CY[n % 2], CQ[n % 2]
                link(v.tensor_scalar(y[:], xq[:, :, 0:S], asm[:, S_CONV + 4 * n:S_CONV + 4 * n + 1], None, ALU.mult))
                for j in range(1, 4):
                    w = asm[:, S_CONV + 4 * n + j:S_CONV + 4 * n + j + 1]
                    ins = v.scalar_tensor_tensor(out=y[:], in0=xq[:, :, j:j + S], scalar=w, in1=y[:],
                                                 op0=ALU.mult, op1=ALU.add)
                    if j < 3:
                        link(ins)
                    else:
                        ins.then_inc(conv_done, 1)
            v.wait_ge(psum_read, 31)
            v.tensor_tensor(SQ[:], SQ[:], bcast(abog[:], 1, TILES), ALU.add).then_inc(to_act, 1)
            v.wait_ge(level_done, 1)
            for l in range(2, 11):
                fold(v, link, l)
            link(v.tensor_copy(TRV[10][:], TRA[10][:, :, 2, :]))
            for l in range(9, -1, -1):
                unfold(v, link, l)
            v.wait_ge(lanes_loaded, 16 * 12)
            v.wait_ge(lanes_clear, 3)
            sq = PRD[:].rearrange("p (n d t) -> p n d t", n=2, d=HD)
            link(v.tensor_tensor(sq, LQK[:], LQK[:], ALU.mult))
            link(v.tensor_reduce(SS[:], sq.rearrange("p n d t -> p n t d"), AX.X, ALU.add))
            v.tensor_scalar(SS[:], SS[:], L2_EPS, None, ALU.add).then_inc(to_act, 1)
            ans.wait()
            link(v.reciprocal(RS[:], SS[:]))
            link(v.tensor_tensor(LQK[:], LQK[:], bcast(RS[:], 2, HD), ALU.mult))
            v.tensor_tensor(KB, LQK[:, 1], bcast(BET[:], 1, HD), ALU.mult).then_inc(kb_ready, 1)
            al = ALP[:].rearrange("p (c s) -> p c s", s=C)
            for m in range(C - 1, -1, -1):
                n = C - m
                link(v.tensor_tensor(GAM[:, :, m + 1:C + 1, m], GAM[:, :, m + 1:C + 1, m + 1],
                                     bcast(al[:, :, m], 2, n), ALU.mult))
            v.wait_ge(kb_ready, 1)
            kn = lanes(LQK[:, 1])
            kb = lanes(KB)
            for s in range(C):
                if s < C - 1:
                    n = C - 1 - s
                    pv = PRD[:, 0:NC * n * HD].rearrange("p (c t d) -> p c t d", c=NC, d=HD)
                    link(v.tensor_tensor(pv, kn[:, :, s + 1:C, :], bcast(kb[:, :, s, :], 2, n), ALU.mult))
                    link(v.tensor_reduce(LA[:, :, s + 1:C, s], pv, AX.X, ALU.add))
                n = C - s
                v.wait_ge(prod_ready, s + 1)
                pp = PRP[s % 2][:, 0:NC * n * HD].rearrange("p (c t d) -> p c t d", c=NC, d=HD)
                v.tensor_reduce(PA[:, :, s:C, s], pp, AX.X, ALU.add).then_inc(prod_used, 1)
            v.wait_ge(prod_used, C)
            v.tensor_tensor(LA[:], LA[:], GAM[:, :, 0:C, 1:C + 1], ALU.mult).then_inc(la_ready, 1)
            link.open(v.tensor_tensor(PA[:], PA[:], GAM[:, :, 1:C + 1, 1:C + 1], ALU.mult))
            link(v.tensor_scalar(NG0[:].rearrange("p (c s) -> p c s", s=C), GAM[:, :, 0:C, 0], -1.0, None, ALU.mult))
            q4 = LQK[:, 0].rearrange("p d (c s) -> p d c s", s=C)
            k4 = KB.rearrange("p d (c s) -> p d c s", s=C)
            link.open(v.tensor_copy(AC1[:], GAM[:, :, C, 0]))
            v.tensor_tensor(k4, k4, bcast(GAM[:, :, C, 1:C + 1], 1, HD), ALU.mult).then_inc(k_decayed, 1)
            link.open(v.tensor_tensor(WU[:, 0:HD, :], LQK[:, 1], bcast(NG0[:], 1, HD), ALU.mult))
            link.open(v.tensor_tensor(q4, q4, bcast(GAM[:, :, 1:C + 1, 0], 1, HD), ALU.mult))
            link.close()
            v.wait_ge(la_ready, 1)
            solve(v, link, 0, HD, PRD, wk_ready)
            v.wait_ge(wk_ready, 1)
            solve(v, link, HD, V_U, PRD, u_solved)
            v.wait_ge(u_solved, 2)
            v.memset(S2[:, 0], 0.0).then_inc(state_clear, 1)
            v.wait_ge(state_clear, 1)
            v.wait_ge(k_loaded, 16 * (SEG + 1))
            for n in range(SEG * NC):
                g, c = divmod(n, NC)
                cs = slice(c * C, (c + 1) * C)
                if c == 0:
                    v.wait_ge(seg_loaded[g], 32)
                if n:
                    v.wait_ge(chunk_done, n)
                link(v.tensor_tensor(P1[:, n % 2, :, :, 0:HD], bcast(W2[:, g, :, cs].rearrange("p i s -> p s i"), 1, 2),
                                     bcast(S2[:, n], 2, C), ALU.mult))
                v.wait_ge(u_slot, n + 1)
                link(v.tensor_reduce(D2[:, g, :, cs], P1[:, n % 2], AX.X, ALU.add))
                link(v.tensor_tensor(P2[:, :, :, 0:C], bcast(K2[:, g, :, cs], 1, 2), bcast(D2[:, g, :, cs], 2, HD),
                                     ALU.mult))
                v.wait_ge(s_slot, n + 1)
                v.tensor_reduce(S2[:, n + 1], P2[:], AX.X, ALU.add).then_inc(chunk_done, 1)
            w_vector(v, link)
            v.wait_ge(ds_loaded, 32 * SEG)
            qa = lanes(LQK[:, 0])
            pr3 = PRR[:].rearrange("p (c s i) -> p c s i", c=NC, i=HD)
            for j in range(HD):
                link(v.tensor_tensor(pr3, qa, bcast(SJ[:, j // 2, :, j % 2, :], 2, C), ALU.mult))
                link(v.tensor_reduce(RP[:, j].rearrange("p (c s) -> p c s", s=C), pr3, AX.X, ALU.add))
                for t in (2 * j, 2 * j + 1):
                    v.wait_ge(rprod_ready, t + 1)
                    pq = PRQ[t % 2][:, 0:NC * HD * (t + 1)].rearrange("p (c j s) -> p c j s", c=NC, j=HD)
                    v.tensor_reduce(RO[:].rearrange("p j (c s) -> p c j s", s=C)[:, :, :, t], pq, AX.X,
                                    ALU.add).then_inc(rprod_used, 1)
            v.wait_ge(rprod_used, C)
            link(v.tensor_tensor(RO[:], RO[:], RP[:], ALU.add))
            link(v.tensor_tensor(RP[:], RO[:], RO[:], ALU.mult))
            link(v.tensor_reduce(SS4[:], RP[:].rearrange("p j t -> p t j"), AX.X, ALU.add))
            v.tensor_scalar(SS4[:], SS4[:], 1.0 / HD, A_EPS, ALU.mult, ALU.add).then_inc(to_act, 1)
            ans.wait()
            link(v.reciprocal(RP[:, 0], SS4[:]))
            v.tensor_tensor(RO[:], RO[:], bcast(RP[:, 0], 1, HD), ALU.mult).then_inc(reads_ready, 1)
            v.wait_ge(psum_full, 32)
            v.tensor_copy(vss[:].rearrange("p (b t) -> p b t", b=B), PS[:, 0:B, 0:TB]).then_inc(psum_read, 1)
            v.wait_ge(psum_read, 32)
            v.tensor_scalar(vss[:], vss[:], 1.0 / D, A_EPS, ALU.mult, ALU.add).then_inc(to_act, 1)
            ans.wait()
            link(v.reciprocal(rrms[:], vss[:]))
            v.wait_ge(psum_full, 33)
            v.tensor_tensor(OT[:], PS[:, 4:8, :].rearrange("p b (t d) -> p (b t) d", d=D), bcast(rrms[:], 2, D),
                            ALU.mult).then_inc(psum_read, 1)
            v.wait_ge(psum_read, 33)
            link(v.tensor_tensor(OT[:], OT[:], bcast(about[:], 1, TILES), ALU.add))
            v.wait_ge(gate_ready, 1)
            link(v.tensor_tensor(OT[:], OT[:], SQ[:], ALU.mult))
            link(v.tensor_tensor(X[:], X[:], OT[:], ALU.add))
            v.wait_ge(psum_full, 34)
            v.tensor_tensor(OT[:], SQ[:], PS[:, 0:4, :].rearrange("p b (t d) -> p (b t) d", d=D),
                            ALU.mult).then_inc(psum_read, 1)
            v.wait_ge(psum_read, 34)
            v.tensor_tensor(X[:], X[:], OT[:], ALU.add).then_inc(x_ready, 1)
            v.wait_ge(x_ready, 1)
            dve_stats(v, link, range(TILES))

        V_U = 2

        def solve(eng, link, col, width, room, done):
            z = WU[:, col:col + width, :].rearrange("p d (c s) -> p c s d", s=C)
            for s in range(C - 1):
                n = C - 1 - s
                pv = room[:, 0:NC * n * width].rearrange("p (c t d) -> p c t d", c=NC, d=width)
                link(eng.tensor_tensor(pv, bcast(LA[:, :, s + 1:C, s], 3, width), bcast(z[:, :, s, :], 2, n), ALU.mult))
                ins = eng.tensor_tensor(z[:, :, s + 1:C, :], z[:, :, s + 1:C, :], pv, ALU.subtract)
                if s < C - 2:
                    link(ins)
                else:
                    ins.then_inc(done, 1)

        def fold(eng, link, l, done=None):
            lo, hi, to = TRA[l - 1][:, :, :, 0::2], TRA[l - 1][:, :, :, 1::2], TRA[l]
            tt = TRT[:, :, :, 0:S >> l]
            link.open(eng.tensor_tensor(to[:], bcast(hi[:, :, 0, :], 2, 3), bcast(lo[:, 0, :, :], 1, 2), ALU.mult))
            link(eng.tensor_tensor(tt, bcast(hi[:, :, 1, :], 2, 3), bcast(lo[:, 1, :, :], 1, 2), ALU.mult))
            link(eng.tensor_tensor(to[:], to[:], tt, ALU.add))
            ins = eng.tensor_tensor(to[:, :, 2, :], to[:, :, 2, :], hi[:, :, 2, :], ALU.add)
            if done is None:
                link(ins)
            else:
                ins.then_inc(done, 1)

        def unfold(eng, link, l):
            n = S >> (l + 1)
            a, to = TRA[l], TRV[l]
            link.open(eng.tensor_copy(to[:, :, 0:1], a[:, :, 2, 0:1]))
            link(eng.tensor_copy(to[:, :, 1::2], TRV[l + 1][:]))
            if n > 1:
                tt = TRT[:, :, 0:2, 0:n - 1]
                link(eng.tensor_tensor(tt, a[:, :, 0:2, 2::2], bcast(TRV[l + 1][:, :, 0:n - 1], 1, 2), ALU.mult))
                link(eng.tensor_tensor(to[:, :, 2::2], tt[:, :, 0, :], tt[:, :, 1, :], ALU.add))
                link(eng.tensor_tensor(to[:, :, 2::2], to[:, :, 2::2], a[:, :, 2, 2::2], ALU.add))

        def a_gpsimd(pool, link):
            for i in range(2):
                pool.memset(CQ[i][:, :, 0:3], 0.0).then_inc(pads_clear, 1)
            pool.memset(ones[:], 1.0).then_inc(pads_clear, 1)
            pool.wait_ge(tree_in, 1)
            fold(pool, link, 1, level_done)
            pool.wait_ge(qkv_stored, 16 * 3)
            pool.wait_ge(conv_done, 3)
            pool.memset(GAM[:], 1.0).then_inc(lanes_clear, 1)
            pool.memset(LA[:], 0.0).then_inc(lanes_clear, 1)
            pool.memset(PA[:], 0.0).then_inc(lanes_clear, 1)
            pool.wait_ge(kb_ready, 1)
            qn, kb = lanes(LQK[:, 0]), lanes(KB)
            for s in range(C):
                n = C - s
                if s >= 2:
                    pool.wait_ge(prod_used, s - 1)
                pp = PRP[s % 2][:, 0:NC * n * HD].rearrange("p (c t d) -> p c t d", c=NC, d=HD)
                pool.tensor_tensor(pp, qn[:, :, s:C, :], bcast(kb[:, :, s, :], 2, n), ALU.mult).then_inc(prod_ready, 1)
            pool.wait_ge(la_ready, 1)
            pool.wait_ge(prod_used, C)
            solve(pool, link, HD + V_U, HD - V_U, PRP[0], u_solved)
            link.open(pool.tensor_tensor(VS[:, 0], V0[:, 0], V0[:, 0], ALU.mult))
            link(pool.tensor_tensor(VS[:, 1], V0[:, 1], V0[:, 1], ALU.mult))
            pool.tensor_tensor(VS[:, 0], VS[:, 0], VS[:, 1], ALU.add).then_inc(vs_ready, 1)
            pool.wait_ge(ds_loaded, 32 * SEG)
            dj = DJ.rearrange("p j (c s) -> p c j s", s=C)
            for t in range(C):
                if t >= 2:
                    pool.wait_ge(rprod_used, t - 1)
                pq = PRQ[t % 2][:, 0:NC * HD * (t + 1)].rearrange("p (c j s) -> p c j s", c=NC, j=HD)
                pool.tensor_tensor(pq, bcast(PA[:, :, t, 0:t + 1], 2, HD), dj[:, :, :, 0:t + 1],
                                   ALU.mult).then_inc(rprod_ready, 1)

        B_RES = 3 + NCH + 3 * NCH
        OUT_BANKS = 6

        def b_tensor(pe, banks, nth):
            base = banks.n
            pe.wait_ge(w_loaded, W_LOADED)
            pe.wait_ge(x_ready, nth)
            for n in range(3):
                k = banks.take()
                pe.matmul(PS[:, k, 0:2 * NB], bw[:, n, :], bdft[:].rearrange("p r f -> p (r f)"),
                          start=True, stop=True).then_inc(psum_full, 1)
            pe_transpose_in(pe, banks, XL, FIRST_NORM[nth])
            banks.all_read()

            def spectra(c):
                for n in range(3):
                    if c:
                        pe.wait_ge(psum_read, banks.n - 2)
                    for r in range(2):
                        last = pe.matmul(PS[0:NB, 2 * n + r, :], bwf[:, n, r, :], HT[:, c * CH:(c + 1) * CH],
                                         start=True, stop=True)
                    last.then_inc(psum_full, 1)
                    banks.n += 1

            def output(c):
                pe.wait_ge(y_ready, c + 1)
                if c >= 2:
                    pe.wait_ge(values_added, c - 1)
                for i in range(TPC):
                    t = (c * TPC + i) * P
                    for r in range(2):
                        last = pe.matmul(PS[:, OUT_BANKS + c % 2, i * P:(i + 1) * P], YF[0:NB, r, t:t + P],
                                         bidft[0:NB, r, :], start=(r == 0), stop=(r == 1))
                last.then_inc(values_full, 1)

            for c in range(NCH):
                spectra(c)
            for c in range(NCH):
                output(c)
            assert banks.n == base + B_RES

        def b_scalar(act, link, ask, reads):
            for n in range(3):
                k = reads.next()
                act.activation(bwf[:, n].rearrange("p r f -> p (r f)"), PS[:, k, 0:2 * NB],
                               ACT.Copy).then_inc(psum_read, 1)
            act_sqrt(act, ask, stat[:])
            act_ht(act, reads)
            for c in range(NCH):
                if c >= 3:
                    act.wait_ge(y_ready, c - 2)
                for n in range(3):
                    reads.next()
                    act.activation(QF[c % 3][0:NB, n], PS[0:NB, 2 * n:2 * n + 2, :], ACT.Copy).then_inc(psum_read, 1)
                act.wait_ge(psum_read, reads.n)
                act.activation(SQF[0:NB], QF[c % 3][0:NB, 0:2], ACT.Square).then_inc(squares_ready, 1)
                act_sqrt(act, ask, mag[0:NB])

        def b_vector(v, link, ans, nth):
            v.wait_ge(x_ready, nth)
            dve_norm(v, link, ans, LN_EPS, XL)
            v.wait_ge(normed, B * (FIRST_NORM[nth] + 1))
            link(v.tensor_tensor(X[:], X[:], XL[:], ALU.add))
            R = slice(0, NB)

            def unit(c):
                qk = QF[c % 3][R, 0:2]
                v.wait_ge(squares_ready, c + 1)
                if c:
                    v.wait_ge(unit_ready, c)
                v.tensor_tensor(mag[R], SQF[R, :, 0], SQF[R, :, 1], ALU.add).then_inc(to_act, 1)
                ans.wait()
                link(v.tensor_scalar(mag[R], mag[R], B_EPS, None, ALU.add))
                link(v.reciprocal(mag[R], mag[R]))
                v.tensor_tensor(qk, qk, bcast(mag[R], 2, 2), ALU.mult).then_inc(unit_ready, 1)

            def sums(c):
                b, h = divmod(c, S // CH)
                v.wait_ge(kv_ready, c + 1)
                if h:
                    v.wait_ge(sums_ready, c)
                for r, op in ((0, ALU.subtract), (1, ALU.add)):
                    init = CUM[R, r, b, h * CH - 1:h * CH] if h else 0.0
                    last = v.tensor_tensor_scan(CUM[R, r, b, h * CH:(h + 1) * CH], KV[c % 2][R, 2 * r],
                                                KV[c % 2][R, 2 * r + 1], init, ALU.add, op)
                last.then_inc(sums_ready, 1)

            def add(c):
                v.wait_ge(values_full, c + 1)
                t = slice(c * TPC, (c + 1) * TPC)
                v.tensor_tensor(X[:, t], X[:, t], PS[:, OUT_BANKS + c % 2, :].rearrange("p (t d) -> p t d", d=D),
                                ALU.add).then_inc(values_added, 1)

            def stats(c):
                v.wait_ge(values_added, c + 1)
                dve_stats(v, link, range(c * TPC, (c + 1) * TPC))

            unit(0)
            for c in range(1, NCH):
                unit(c)
                sums(c - 1)
                if c >= 2:
                    add(c - 2)
                    stats(c - 2)
            sums(NCH - 1)
            for c in (NCH - 2, NCH - 1):
                add(c)
                stats(c)
            v.nop().then_inc(x_ready, 1)

        def b_gpsimd(pool, link):
            R = slice(0, NB)

            def times(c):
                k, w, to = QF[c % 3][R, 1], QF[c % 3][R, 2], KV[c % 2]
                pool.wait_ge(unit_ready, c + 1)
                if c >= 2:
                    pool.wait_ge(sums_ready, c - 1)
                pool.tensor_tensor(to[R, 0:2], k, w, ALU.mult)
                pool.tensor_tensor(to[R, 2], k[:, 0], w[:, 1], ALU.mult)
                pool.tensor_tensor(to[R, 3], k[:, 1], w[:, 0], ALU.mult).then_inc(kv_ready, 1)

            def unbind(c):
                b, h = divmod(c, S // CH)
                cs, ts = slice(h * CH, (h + 1) * CH), slice(c * CH, (c + 1) * CH)
                q = QF[c % 3][R, 0]
                pool.wait_ge(sums_ready, c + 1)
                if c:
                    pool.wait_ge(y_ready, c)
                link.open(pool.tensor_tensor(PRB[R, 0:2], CUM[R, :, b, cs], q, ALU.mult))
                link.open(pool.tensor_tensor(PRB[R, 2], CUM[R, 1, b, cs], q[:, 0], ALU.mult))
                link(pool.tensor_tensor(PRB[R, 3], CUM[R, 0, b, cs], q[:, 1], ALU.mult))
                link.open(pool.tensor_tensor(YF[R, 0, ts], PRB[R, 0], PRB[R, 1], ALU.add))
                pool.tensor_tensor(YF[R, 1, ts], PRB[R, 2], PRB[R, 3], ALU.subtract).then_inc(y_ready, 1)
                link.close()

            times(0)
            for c in range(1, NCH):
                times(c)
                unbind(c - 1)
            unbind(NCH - 1)

        def w_sync(sp):
            for dst, src in ((bw, b_w), (bdft, b_dft), (bidft, b_idft), (fw, f_w), (fn, f_n), (fmid, f_mid),
                             (fdown, f_down), (fwo, f_wo)):
                sp.dma_start(dst[:], src).then_inc(w_loaded, 16)
            sp.dma_start(fqk[:].rearrange("p n d -> p (n d)"), f_qk.partition_broadcast(P)).then_inc(w_loaded, 16)
            sp.dma_start(maskf[:], causal).then_inc(w_loaded, 16)

        W_LOADED = 16 * 10
        ATT = [(b, qc, kt, hp, max(0, kt - TPC * qc) * P) for b in range(B) for qc in range(S // CH)
               for kt in range(TPC * (qc + 1)) for hp in range(GH // 2)]
        NA = len(ATT)
        NA_B = NA // B
        NA_Q0 = TPC * GH // 2
        LAG = 2
        DEPTH = 3
        OBANKS = 2
        SCORES_BANKS = 2 * DEPTH
        ROUTER_BANK = 5
        HT_BANKS = 4
        F_RES = NCH + TILES + 2 * NCH + NCH + NCH + 1


        def f_sync(sp, nth, rep):
            if rep == 0:
                sp.wait_ge(stack_clear, 2 * B)
            first = FIRST_RESULT[nth] + NCH + TILES
            heads = lambda g: slice(g * GH, (g + 1) * GH)
            for b in range(B):
                ts = slice(b * S, (b + 1) * S)
                sp.wait_ge(psum_read, first + (2 if b == 0 else 8))
                sp.dma_start(qs_d[:, QROWS - 1, ts], MT[:, ts]).then_inc(parts_stored, 16)
                done = NCH * rep + NCH // B * (b + 1)
                for part in range(3):
                    if part == 0:
                        sp.wait_ge(part_high, 2 * done)
                    elif part == 1:
                        sp.wait_ge(psum_read, first + NCH + NCH * (b + 1))
                    else:
                        sp.wait_ge(parts_ready, done)
                    for n, (d, side) in enumerate(((qs_d, Q_SIDE), (ks_d, K_SIDE))):
                        for s in range(NSLOT):
                            if side[s] == part:
                                sp.dma_start(d[:, HD * s:HD * (s + 1), ts], QP[part][:, n, ts]).then_inc(parts_stored, 16)
                sp.wait_ge(parts_stored, PARTS * (rep * B + b + 1))
                for g in range(NG):
                    it = b * NG + g
                    if it >= 2:
                        sp.wait_ge(probs_used, DEPTH + (rep * B * NG + it - 1) * NA_B)
                    sp.dma_start(QS[it % 2][0:QROWS],
                                 qs_d[heads(g), :, ts].rearrange("h r t -> r h t")).then_inc(stack_loaded[it % 2], 16)
                    sp.dma_start(KS[it % 2][0:QROWS - 1],
                                 ks_d[heads(g), 0:QROWS - 1, ts].rearrange("h r t -> r h t")).then_inc(stack_loaded[it % 2], 16)

        PARTS = 16 * (2 * NSLOT + 1)

        def f_gpsimd(pool, link, nth, rep):
            if rep == 0:
                pool.wait_ge(w_loaded, W_LOADED)
                pool.wait_ge(x_ready, nth)
                for b in range(B):
                    pool.memset(KS[b][:], 1.0).then_inc(stack_clear, 1)
                    pool.memset(QS[b][:], 0.0).then_inc(stack_clear, 1)
                    link(pool.memset(VA[b][:], 1.0))
                pool.tensor_copy(maskb[:], maskf[:]).then_inc(stack_clear, 1)
                pool.tensor_copy(identb[:], ident[:]).then_inc(stack_clear, 1)
            pool.wait_ge(psum_read, FIRST_RESULT[nth] + NCH + TILES)

            for it in range(B * NG):
                b, g = divmod(it, NG)
                if it >= 2:
                    pool.wait_ge(probs_used, DEPTH + (rep * B * NG + it - 1) * NA_B)
                src = QKV[:, b * TB:(b + 1) * TB, 2 * D + g * (GH * HD):2 * D + (g + 1) * (GH * HD)]
                pool.tensor_copy(VA[it % 2][:, :, :, 0:HD], src.rearrange("p t (h d) -> p t h d", d=HD)).then_inc(v_ready, 1)

        def f_tensor(pe, banks, nth, rep):
            base = banks.n
            assert base == FIRST_RESULT[nth]
            if rep == 0:
                pe.sem_inc(probs_used, DEPTH)
            pe.wait_ge(fw_ready, 2)
            pe_transpose_in(pe, banks, SQ, FIRST_NORM[nth])
            banks.all_read()
            for t in range(TILES):
                k = banks.take()
                pe.matmul(PS[:, k, 0:3 * D], HT[:, t * P:(t + 1) * P], fw[:, 0:3 * D], start=True,
                          stop=True).then_inc(psum_full, 1)
            for b in range(B):
                chunks = range(b * (NCH // B), (b + 1) * (NCH // B))
                pe.wait_ge(shifts_ready, rep * B + b + 1)
                for c in chunks:
                    k = banks.take()
                    for i in range(TPC):
                        last = pe.transpose(PS[0:H, k, i * P:(i + 1) * P], qst2[:, c * TPC + i, 0:H], ident[:])
                    last.then_inc(psum_full, 1)
                if b:
                    banks.all_read()
                pe.wait_ge(qk_normed, rep * B + b + 1)
                for c in chunks:
                    for n in range(2):
                        k = banks.take()
                        for i in range(TPC):
                            last = pe.transpose(PS[:, k, i * P:(i + 1) * P], QKS[:, c * TPC + i, n * D:(n + 1) * D], ident[:])
                        last.then_inc(psum_full, 1)
            banks.all_read()
            pe.wait_ge(stack_clear, 2 * B + 2)
            with pe.Fori(0, NG) as g:
                n = rep * NG + g
                for u in range(NA + LAG):
                    if u < NA:
                        b, qc, kt, hp, c0 = ATT[u]
                        if u % NA_B == 0:
                            pe.wait_ge(stack_loaded[b], 32 * (n + 1))
                            pe.wait_ge(v_ready, n * B + b + 1)
                        pe.wait_ge(probs_ready, n * NA + u + 1)
                        diag = kt >= TPC * qc
                        for i in range(2):
                            h, k = 2 * hp + i, 2 * (u % DEPTH) + i
                            last = pe.matmul(PS[:, k, c0:CH], KS[b][:, h, kt * P:(kt + 1) * P],
                                             QS[b][:, h, qc * CH + c0:(qc + 1) * CH], start=True, stop=True)
                            if diag:
                                last = pe.matmul(PS[:, k, c0:c0 + P], identb[:], maskb[:], start=False, stop=True,
                                                 skip_group_check=True)
                        last.then_inc(scores_ready, 1)
                    if u >= LAG:
                        w = u - LAG
                        b, qc, kt, hp, c0 = ATT[w]
                        pe.wait_ge(probs_ready, DEPTH + n * NA + w + 1)
                        if kt == 0 and hp == 0:
                            pe.wait_ge(o_read, (n * B + b) * 2 + qc + 1)
                        for i in range(2):
                            h = 2 * hp + i
                            last = pe.matmul(PS[32 * h:32 * h + 32, SCORES_BANKS + qc, c0:CH], VA[b][:, kt, h, :],
                                             PX[w % DEPTH][:, i, c0:CH], start=(kt == 0),
                                             stop=(kt >= TPC * qc), skip_group_check=True)
                        last.then_inc(probs_used, 1)
            for c in range(NCH):
                if c % (NCH // B) == 0:
                    pe.wait_ge(o_read, OBANKS + (rep * B + c // (NCH // B) + 1) * NG * 2)
                for i in range(TPC):
                    t = (c * TPC + i) * P
                    for g in range(NG):
                        last = pe.matmul(PS[:, c, i * OUTC:(i + 1) * OUTC], AO[:, g, t:t + P], fwo[:, g, :],
                                         start=(g == 0), stop=(g == NG - 1))
                last.then_inc(proj_full, 1)
            pe_transpose_in(pe, banks, SQ, FIRST_NORM[nth] + 1, range(NCH // B), HT_BANKS)
            banks.all_read()
            rhs = lambda c: HT[:, c * CH:(c + 1) * CH]

            def up(c, bank, col, halves=2):
                for m in range(halves):
                    last = pe.matmul(PS[:, bank + m, :], fw[:, col + m * P:col + (m + 1) * P], rhs(c), start=True, stop=True)
                last.then_inc(up_full, 1)

            up(0, 0, F_E1A)
            pe_transpose_in(pe, banks, SQ, FIRST_NORM[nth] + 1, range(NCH // B, NCH), HT_BANKS)
            up(0, 2, F_E1B)
            banks.all_read()
            banks.n += 1
            for t in range(TILES):
                last = pe.matmul(PS[:, ROUTER_BANK, t * E4:(t + 1) * E4], HT[:, t * P:(t + 1) * P], fw[:, F_GATE:F_GATE + E4],
                                 start=True, stop=True)
            last.then_inc(psum_full, 1)
            assert banks.n == base + F_RES
            hidden = rep * UPS
            gated = rep * NCH
            tiles = rep * 2 * TILES

            def mid(bank, w, parts):
                for m in range(2):
                    for k, h in enumerate(parts):
                        last = pe.matmul(PS[:, bank + m, :], fmid[:, w + k, m * P:(m + 1) * P], h,
                                         start=(k == 0), stop=(k == len(parts) - 1))
                last.then_inc(up_full, 1)

            def down1(c):
                pe.wait_ge(h1_ready, gated + c + 1)
                if c >= 2:
                    pe.wait_ge(down_read, tiles + (c - 1) * TPC)
                for t in range(TPC):
                    for m in range(2):
                        last = pe.matmul(PS[:, 6 + c % 2, t * OUTC:(t + 1) * OUTC], HG[c % 2][:, m, t * P:(t + 1) * P],
                                         fdown[:, 1, m, :], start=(m == 0), stop=(m == 1))
                last.then_inc(down_full, 1)

            def down(c):
                pe.wait_ge(up_read, hidden + NCH + 6 * (c + 1))
                for t in range(TPC):
                    pe.wait_ge(down_read, tiles + TILES + c * TPC + t - (1 if c or t else 0))
                    for j, (e, h) in enumerate(((0, H0[c % 2]), (2, HC), (3, HF))):
                        for m in range(2):
                            last = pe.matmul(PS[:, 6 + t % 2, j * OUTC:(j + 1) * OUTC], h[:, m, t * P:(t + 1) * P],
                                             fdown[:, e, m, :], start=(m == 0), stop=(m == 1))
                    last.then_inc(down_full, 1)

            for c in range(NCH):
                if c:
                    pe.wait_ge(up_read, hidden + c)
                    up(c, 0, F_E1A)
                    pe.wait_ge(h1_ready, gated + c)
                    up(c, 2, F_E1B)
                    down1(c - 1)
            pe.wait_ge(up_read, hidden + NCH)
            pe.wait_ge(h1_ready, gated + NCH)
            banks.all_read()
            for c in range(NCH):
                seen = hidden + NCH + 6 * c
                up(c, 0, F_E2)
                up(c, 2, F_E0)
                if c:
                    pe.wait_ge(up_read, seen)
                up(c, 4, F_E3, 1)
                if c == 0:
                    down1(NCH - 1)
                else:
                    down(c - 1)
                pe.wait_ge(up_read, seen + 1)
                mid(0, 0, [HA[:, k, :] for k in range(2)])
                pe.wait_ge(up_read, seen + 3)
                mid(2, 4, [HE[:]])
                pe.wait_ge(up_read, seen + 4)
                mid(4, 2, [HB[:, k, :] for k in range(2)])
                pe.wait_ge(up_read, seen + 5)
            down(NCH - 1)

        UPS = NCH + 6 * NCH

        def f_scalar(act, link, ask, reads, nth, rep):
            if rep == 0:
                act.sem_inc(probs_ready, DEPTH)
            act_sqrt(act, ask, stat[:])
            act_sqrt(act, ask, stat[:])
            act_ht(act, reads)
            for t in range(TILES):
                k = reads.next()
                act.activation(QKS[:, t, :], PS[:, k, 0:2 * D], ACT.Square)
                act.activation(QKV[:, t, :], PS[:, k, 0:3 * D], ACT.Copy).then_inc(psum_read, 1)

            def qk_roots(b):
                tb = slice(b * TB, (b + 1) * TB)
                act_sqrt(act, ask, qst[:, tb])
                act.wait_ge(qk_normed, rep * B + b + 1)
                act.activation(QR[b][:].rearrange("p n (t d) -> p (n t) d", d=D), QKS[:, tb, 0:D],
                               ACT.Square).then_inc(q_squared, 1)
                act_sqrt(act, ask, qst[:, tb, H:2 * H])

            def high(c):
                for n in range(2):
                    k = reads.next()
                    act.activation(QP[0][:, n, c * CH:(c + 1) * CH], PS[:, k, :], ACT.Copy).then_inc(part_high, 1)

            def mid(c):
                act.wait_ge(rest_ready, 2 * (rep * NCH + c + 1))
                act.activation(QP[1][:, :, c * CH:(c + 1) * CH], QR[c % 2][:], ACT.Copy).then_inc(psum_read, 2)

            def shifts(c):
                k = reads.next()
                act.activation(MT[:, c * CH:(c + 1) * CH], PS[0:H, k, :], ACT.Copy).then_inc(psum_read, 1)

            qk_roots(0)
            shifts(0)
            shifts(1)
            high(0)
            high(1)
            qk_roots(1)
            shifts(2)
            shifts(3)
            mid(0)
            mid(1)
            high(2)
            high(3)
            mid(2)
            mid(3)
            with act.Fori(0, NG) as g:
                n = rep * NG + g
                for u in range(NA):
                    c0 = ATT[u][-1]
                    act.wait_ge(scores_ready, n * NA + u + 1)
                    act.wait_ge(probs_used, n * NA + u + 1)
                    act.activation(PX[u % DEPTH][:, :, c0:CH], PS[:, 2 * (u % DEPTH):2 * (u % DEPTH) + 2, c0:CH],
                                   ACT.Exp).then_inc(probs_ready, 1)
            for b in range(B):
                act_sqrt(act, ask, stat[:, b * TB:(b + 1) * TB])
                act_ht(act, reads, range(b * (NCH // B), (b + 1) * (NCH // B)), HT_BANKS)
            reads.n += 1
            ask.wait()
            act.activation(pr[:], lg[:], ACT.Exp).then_inc(to_dve, 1)
            hidden = rep * 8 * NCH
            for c in range(NCH):
                act.wait_ge(up_full, hidden + 2 * c + 1)
                if c >= 2:
                    act.wait_ge(h1_ready, rep * NCH + c - 1)
                act.activation(HS[c % 2][:], PS[:, 0:2, :], ACT.Silu).then_inc(up_read, 1)
            for c in range(NCH):
                for j, (bank, w, h) in enumerate(((0, 2, HA), (2, 2, H0[c % 2]), (4, 1, HE), (0, 2, HB), (2, 2, HF), (4, 2, HC))):
                    act.wait_ge(up_full, hidden + 2 * NCH + 6 * c + j + 1)
                    src = PS[:, bank:bank + 2, :] if w == 2 else PS[:, bank, :]
                    act.activation(h[:], src, ACT.Gelu).then_inc(up_read, 1)

        def w_vector(v, link):
            v.wait_ge(w_loaded, W_LOADED)
            v.tensor_scalar(fw[:, 0:3 * D], fw[:, 0:3 * D], fn[:, 0:1], None, ALU.mult).then_inc(fw_ready, 1)
            v.tensor_scalar(fw[:, 3 * D:], fw[:, 3 * D:], fn[:, 1:2], None, ALU.mult).then_inc(fw_ready, 1)
            link(v.tensor_tensor(fqk[:, 0], fqk[:, 0], fqk[:, 1], ALU.mult))
            link(v.tensor_scalar(fqk[:, 0], fqk[:, 0], HD ** -0.5, None, ALU.mult))

        def f_vector(v, link, ans, nth, rep):
            base = FIRST_RESULT[nth]
            v.wait_ge(x_ready, nth)
            if rep == 0:
                v.sem_inc(o_read, OBANKS)
            dve_norm(v, link, ans, LN_EPS, SQ, F_EPS)
            for b in range(B):
                tb = slice(b * TB, (b + 1) * TB)
                v.wait_ge(psum_read, base + NCH + TB * (b + 1))
                qk = QKV[:, tb, 0:2 * D].rearrange("p t (n d) -> p t n d", d=HD)
                to = QKS[:, tb].rearrange("p t (n d) -> p t n d", d=HD)
                link(v.tensor_reduce(qst[:, tb], to, AX.X, ALU.add))
                v.tensor_scalar(qst[:, tb], qst[:, tb], 1.0 / HD, F_EPS, ALU.mult, ALU.add).then_inc(to_act, 1)
                ans.wait()
                link(v.reciprocal(qst2[:, tb], qst[:, tb]))
                link(v.tensor_tensor(to, qk, bcast(qst2[:, tb], 3, HD), ALU.mult))
                q = QKS[:, tb, 0:D].rearrange("p t (h d) -> p t h d", d=HD)
                v.tensor_tensor(q, q, bcast(bcast(fqk[:, 0], 1, H), 1, TB), ALU.mult).then_inc(qk_normed, 1)
                v.wait_ge(qk_normed, rep * B + b + 1)
                q, k = QKS[:, tb, 0:D], QKS[:, tb, D:2 * D]
                sq = SQ[:, tb]
                heads = sq.rearrange("p t (h d) -> p t h d", d=HD)
                link(v.tensor_tensor(sq, q, k, ALU.mult))
                link(v.tensor_reduce(qst[:, tb, 0:H], heads, AX.X, ALU.add))
                v.wait_ge(q_squared, rep * B + b + 1)
                link(v.tensor_reduce(qst[:, tb, H:2 * H], QR[b][:].rearrange("p n (t h d) -> p (n t) h d", h=H, d=HD),
                                     AX.X, ALU.add))
                v.tensor_scalar(qst[:, tb, H:2 * H], qst[:, tb, H:2 * H], 0.0, None, ALU.max).then_inc(to_act, 1)
                ans.wait()
                link(v.tensor_scalar(qst[:, tb, H:2 * H], qst[:, tb, H:2 * H], HD ** 0.5, -SHIFT, ALU.mult, ALU.add))
                link(v.tensor_tensor(qst2[:, tb, 0:H], qst[:, tb, 0:H], qst[:, tb, H:2 * H], ALU.max))
                v.tensor_scalar(qst2[:, tb, 0:H], qst2[:, tb, 0:H], -1.0, None, ALU.mult).then_inc(shifts_ready, 1)
            for b in range(B):
                chunks = range(b * (NCH // B), (b + 1) * (NCH // B))
                for c in chunks:
                    for n in range(2):
                        r = base + NCH + TILES + 2 * (b + 1) + 2 * c + n
                        v.wait_ge(part_high, (rep * NCH + c) * 2 + n + 1)
                        v.tensor_tensor(QR[c % 2][:, n], PS[:, r % 8, :], QP[0][:, n, c * CH:(c + 1) * CH],
                                        ALU.subtract).then_inc(rest_ready, 1)
                for c in chunks:
                    v.wait_ge(psum_read, base + NCH + TILES + NCH + 2 * (c + 1))
                    v.tensor_tensor(QP[2][:, :, c * CH:(c + 1) * CH], QR[c % 2][:], QP[1][:, :, c * CH:(c + 1) * CH],
                                    ALU.subtract).then_inc(parts_ready, 1)
                v.wait_ge(parts_ready, rep * NCH + chunks[-1] + 1)
            for t in range(TILES):
                link.open(center_and_scale(v, XL, t, rstd))
            link.close()
            for it in range(B * NG):
                b, g = divmod(it, NG)
                if True:
                    for qc in range(2):
                        at = (rep * B * NG + it) * 2 + qc
                        o = PS[:, SCORES_BANKS + qc, :]
                        t = b * S + qc * CH
                        v.wait_ge(probs_used, DEPTH + (rep * B * NG + it) * NA_B + (NA_Q0 if qc == 0 else NA_B))
                        v.wait_ge(o_read, OBANKS + at)
                        v.stream_shuffle(DEN[:], o, [HD] * 32).then_inc(den_ready, 1)
                        v.wait_ge(den_ready, 2 * at + 1)
                        v.reciprocal(DEN[:], DEN[:]).then_inc(den_ready, 1)
                        v.wait_ge(den_ready, 2 * at + 2)
                        v.tensor_tensor(AO[:, g, t:t + CH], o, DEN[:], ALU.mult).then_inc(o_read, 1)
            first = base + NCH + TILES + 3 * NCH
            for b in range(B):
                for c in range(b * (NCH // B), (b + 1) * (NCH // B)):
                    v.wait_ge(proj_full, rep * NCH + c + 1)
                    t = slice(c * TPC, (c + 1) * TPC)
                    v.tensor_tensor(XL[:, t, KEEP:], XL[:, t, KEEP:],
                                    PS[:, c, 0:TPC * OUTC].rearrange("p (t d) -> p t d", d=OUTC),
                                    ALU.add).then_inc(proj_added, 1)
                v.wait_ge(proj_added, rep * NCH + NCH // B * (b + 1))
                tb = slice(b * TB, (b + 1) * TB)
                link(v.tensor_tensor(SQ[:, tb], XL[:, tb], XL[:, tb], ALU.mult))
                link(v.tensor_reduce(stat[:, tb], SQ[:, tb], AX.X, ALU.add))
                v.tensor_scalar(stat[:, tb], stat[:, tb], 1.0 / D, F_EPS, ALU.mult, ALU.add).then_inc(to_act, 1)
                ans.wait()
                link(v.reciprocal(rrms[:, tb], stat[:, tb]))
                v.tensor_tensor(SQ[:, tb], XL[:, tb], bcast(rrms[:, tb], 2, D), ALU.mult).then_inc(normed, 1)
            v.tensor_tensor(X[:], X[:], XL[:], ALU.add).then_inc(x_sum, 1)
            first += NCH
            v.wait_ge(psum_full, first + 1)
            v.tensor_scalar(lg[:].rearrange("p t e -> p (t e)"), PS[:, ROUTER_BANK, 0:TILES * E4], FLT_MAX, -FLT_MAX,
                            ALU.min, ALU.max).then_inc(psum_read, 1)
            v.wait_ge(psum_read, first + 1)
            link(v.tensor_reduce(red[:], lg[:], AX.X, ALU.max))
            v.tensor_tensor(lg[:], lg[:], bcast(red[:], 2, E4), ALU.subtract).then_inc(to_act, 1)
            ans.wait()
            link(v.tensor_reduce(red[:], pr[:], AX.X, ALU.add))
            link(v.reciprocal(red[:], red[:]))
            link.open(v.tensor_tensor(pr[:], pr[:], bcast(red[:], 2, E4), ALU.mult))
            link(v.memset(cnt[:], 0.0))
            for i in range(E4):
                for j in range(i):
                    link(v.tensor_tensor(ge[:], pr[:, :, j], pr[:, :, i], ALU.is_ge))
                    link.open(v.tensor_tensor(cnt[:, :, i], cnt[:, :, i], ge[:], ALU.add))
                    link(v.tensor_scalar(red[:], ge[:], -1.0, 1.0, ALU.mult, ALU.add))
                    link(v.tensor_tensor(cnt[:, :, j], cnt[:, :, j], red[:], ALU.add))
            link(v.tensor_scalar(cnt[:], cnt[:], 2.0, None, ALU.is_lt))
            link(v.tensor_tensor(wts[:], pr[:], cnt[:], ALU.mult))
            link(v.tensor_reduce(red[:], wts[:], AX.X, ALU.add))
            link(v.tensor_scalar(red[:], red[:], TOP_EPS, None, ALU.add))
            link(v.reciprocal(red[:], red[:]))
            link(v.tensor_tensor(wts[:], wts[:], bcast(red[:], 2, E4), ALU.mult))
            v.wait_ge(x_sum, rep + 1)

            def add_expert(tile, e, src):
                xt = X[:, tile, KEEP:]
                return v.scalar_tensor_tensor(out=xt, in0=src, scalar=wts[:, tile, e:e + 1], in1=xt,
                                              op0=ALU.mult, op1=ALU.add)

            chunks = rep * (NCH + TILES)

            def gate(c):
                v.wait_ge(up_read, rep * UPS + c + 1)
                v.wait_ge(up_full, rep * 8 * NCH + 2 * c + 2)
                v.tensor_tensor(HG[c % 2][:], HS[c % 2][:], PS[:, 2:4, :], ALU.mult).then_inc(h1_ready, 1)

            def add1(c):
                v.wait_ge(down_full, chunks + c + 1)
                for t in range(TPC):
                    add_expert(c * TPC + t, 1, PS[:, 6 + c % 2, t * OUTC:(t + 1) * OUTC]).then_inc(down_read, 1)

            gate(0)
            for c in range(1, NCH):
                gate(c)
                add1(c - 1)
            add1(NCH - 1)
            v.wait_ge(down_read, rep * 2 * TILES + TILES)
            for t in range(TILES):
                v.wait_ge(down_full, chunks + NCH + t + 1)
                for j, e in enumerate((0, 2, 3)):
                    ins = add_expert(t, e, PS[:, 6 + t % 2, j * OUTC:(j + 1) * OUTC])
                    if j < 2:
                        link(ins)
                    else:
                        ins.then_inc(down_read, 1)
                if nth + 1 < len(LAYERS) and t % TPC == TPC - 1:
                    v.wait_ge(down_read, rep * 2 * TILES + TILES + t + 1)
                    dve_stats(v, link, range(t + 1 - TPC, t + 1))
            v.wait_ge(down_read, (rep + 1) * 2 * TILES)
            v.nop().then_inc(x_ready, 1)

        LAYERS = 'AFBF'
        RESULTS = {"A": A_RES, "B": B_RES, "F": F_RES}
        NORMS = {"A": 1, "B": 1, "F": 2}
        FIRST_RESULT = [sum(RESULTS[l] for l in LAYERS[:n]) for n in range(len(LAYERS))]
        FIRST_NORM = [sum(NORMS[l] for l in LAYERS[:n]) for n in range(len(LAYERS))]
        block = ctx.enter_context(nc.Block())

        @block.sync
        def _(sp):
            a_sync(sp)
            for n, layer in enumerate(LAYERS):
                if layer == "F":
                    f_sync(sp, n, LAYERS[:n].count("F"))
            sp.wait_ge(x_ready, len(LAYERS))
            sp.dma_start(out.rearrange("(t p) d -> p t d", p=P), X[:]).then_inc(out_stored, 16)
            sp.wait_ge(out_stored, 16)

        @block.tensor
        def _(pe):
            banks = Banks(pe)
            for n, layer in enumerate(LAYERS):
                if layer == "A":
                    a_tensor(pe, banks)
                elif layer == "B":
                    b_tensor(pe, banks, n)
                else:
                    f_tensor(pe, banks, n, LAYERS[:n].count("F"))

        @block.scalar
        def _(act):
            link, ask, reads = Chain(act, act_chain), Tally(act, to_act), Reads(act)
            for n, layer in enumerate(LAYERS):
                if layer == "A":
                    a_scalar(act, link, ask, reads)
                elif layer == "B":
                    b_scalar(act, link, ask, reads)
                else:
                    f_scalar(act, link, ask, reads, n, LAYERS[:n].count("F"))

        @block.vector
        def _(v):
            link, ans = Chain(v, dve_chain), Tally(v, to_dve)
            for n, layer in enumerate(LAYERS):
                if layer == "A":
                    a_vector(v, link, ans)
                elif layer == "B":
                    b_vector(v, link, ans, n)
                else:
                    f_vector(v, link, ans, n, LAYERS[:n].count("F"))

        @block.gpsimd
        def _(pool):
            link = Chain(pool, pool_chain)
            for n, layer in enumerate(LAYERS):
                if layer == "A":
                    a_gpsimd(pool, link)
                elif layer == "B":
                    b_gpsimd(pool, link)
                else:
                    f_gpsimd(pool, link, n, LAYERS[:n].count("F"))


def dft_tables():
    import numpy as np
    n = np.arange(D)[:, None]
    f = np.arange(NB)[None, :]
    turn = (n * f) % D
    cos = np.cos(2 * np.pi * turn / D)
    sin = np.sin(2 * np.pi * turn / D)
    sin[(2 * turn) % D == 0] = 0.0
    weight = np.where((f == 0) | (f == D // 2), 1.0, 2.0) / D
    forward = np.stack([cos, -sin], 1).astype(np.float32)
    back = np.zeros((P, 2, D), np.float32)
    back[:NB, 0] = (weight * cos).T
    back[:NB, 1] = (-weight * sin).T
    return forward, back


def kernel(**inputs):
    import numpy as np
    import concourse.bacc as bacc
    from concourse.bass_utils import run_bass_kernel_spmd as run

    g = {k: np.asarray(v) for k, v in inputs.items()}
    a = lambda name: g["L0_attn_a_" + name]
    f = lambda name: g["L0_ffn_" + name]
    W, bias = a("W_ctrl"), a("b_ctrl")
    ug, ang, cand, q, k, v, al, be, og = np.split(np.arange(W.shape[1]), np.cumsum([D, D // 2, D, D, D, D, H, H]))
    pick = np.concatenate([q, k, v, ug[0::2], ug[1::2], cand[0::2], cand[1::2], ang, og])
    a_w = W[:, pick]
    a_wab = np.zeros((D, 4, BH), np.float32)
    for w, cols in enumerate((al, be)):
        for b in range(B):
            a_wab[:, 2 * w + b, b * H:(b + 1) * H] = W[:, cols]
    two = lambda t: np.concatenate([t, t])
    small = [bias[q], bias[k], bias[v]]
    small += [a(n)[:, j] for n in ("qconv_w", "kconv_w", "vconv_w") for j in range(4)]
    small += [two(bias[c]) for c in (ug[0::2], ug[1::2], cand[0::2], cand[1::2], ang)]
    small += [two(a("W_block")[:, i, j]) for i in range(2) for j in range(2)]
    small += [np.tile(bias[al], SEG * B), np.tile(bias[be], SEG * B)]
    small += [np.tile(a("rms_m_w"), H), two(a("rms_v_w")[0::2]), two(a("rms_v_w")[1::2])]
    W_out = a("W_out")
    forward, back = dft_tables()
    b_w = np.stack([g["L0_attn_b_W" + n] for n in "qkv"], 1)
    down = lambda n: f(n).T[:, KEEP:].reshape(2, P, OUTC).transpose(1, 0, 2)
    mid = lambda n: f(n).T.reshape(2, P, HID).transpose(1, 0, 2)
    wo = np.zeros((P, NG, OUTC), np.float32)
    for n in range(H):
        wo[32 * (n % GH):32 * (n % GH) + HD, n // GH] = f("wo").T[n * HD:(n + 1) * HD, KEEP:]
    arrays = {
        "x": a("hidden").reshape(NT, D), "a_w": a_w, "a_wab": a_wab, "a_small": np.stack(small, 1),
        "a_bog": bias[og], "a_bout": a("b_out"),
        "a_wout": np.stack([W_out[:D], two(W_out[D::2]), two(W_out[D + 1::2])], 1),
        "b_w": b_w, "b_dft": forward, "b_idft": back,
        "f_w": np.concatenate([f(n).T for n in ("wq", "wk", "wv", "gate_w", "e0_up", "e1_w1", "e1_w2", "e2_l1",
                                                "e3_down")], 1),
        "f_n": np.stack([f("n1_w"), f("n2_w")], 1), "f_qk": np.concatenate([f("qn_w"), f("kn_w")]),
        "f_mid": np.concatenate([mid("e2_l2"), mid("e2_l3"), f("e3_up").T[:, None]], 1),
        "f_down": np.stack([down(n) for n in ("e0_down", "e1_down", "e2_l4", "e3_out")], 1),
        "f_wo": wo, "eye": np.eye(P, dtype=np.float32),
        "causal": np.where(np.arange(P)[:, None] > np.arange(P)[None, :], MASKED, 0.0).astype(np.float32),
    }
    nc = bacc.Bacc("TRN2", target_bir_lowering=False, num_devices=1)
    arrays = {n: np.ascontiguousarray(t) for n, t in arrays.items()}
    args = {n: nc.dram_tensor(n, t.shape, F32, kind="ExternalInput").ap() for n, t in arrays.items()}
    out = nc.dram_tensor("out", (NT, D), F32, kind="ExternalOutput").ap()
    hybrid_kernel(nc, out=out, **args)
    got = run(nc, [arrays], core_ids=[0]).results[0]["out"]
    return got.reshape(B, S, D)
```

```python
from contextlib import ExitStack

import concourse.bass as bass
from concourse import mybir

ALU = mybir.AluOpType
ACT = mybir.ActivationFunctionType
AX = mybir.AxisListType
F32 = mybir.dt.float32
BF16 = mybir.dt.bfloat16

P = 128
B, S, D = 2, 1024, 128
NT = B * S
TILES = NT // P
TB = TILES // B
H, HD = 16, 8
SEG, C = 4, 16
BH = B * H
ST = S // SEG
NC = ST // C
CH = 512
NCH = NT // CH
TPC = CH // P
NB = D // 2 + 1
KEEP = 32
OUTC = D - KEEP
HID = 256
E4 = 4
LN_EPS, A_EPS, L2_EPS, B_EPS, F_EPS = 1e-5, 1e-6, 1e-12, 1e-8, 1.1920929e-07
TOP_EPS = 1e-8
SHIFT = 64.0
FLT_MAX = 3.4028234663852886e38
MASKED = -1.0e30
MAGIC = 12582912.0
TWO_PI = 6.283185307179586
TWO_PI_HI = 6.28125
PI = 3.1415925

A_Q, A_K, A_V, A_UE, A_UO, A_CE, A_CO, A_ANG, A_OG, A_COLS = 0, 128, 256, 384, 448, 512, 576, 640, 704, 832
S_BQKV, S_CONV, S_BPAIR, S_WB, S_BAB, S_RMS, S_COLS = 0, 3, 15, 20, 24, 26, 29
F_QKV, F_GATE, F_E0, F_E1A, F_E1B, F_E2, F_E3, F_COLS = 0, 384, 388, 644, 900, 1156, 1412, 1540
Q_SIDE = (0, 1, 0, 1, 2, 0)
K_SIDE = (0, 0, 1, 1, 0, 2)
NSLOT = len(Q_SIDE)
QROWS = NSLOT * HD + 1
GH = 4
NG = H // GH


class Tally:

    def __init__(self, eng, sem):
        self.eng, self.sem, self.n = eng, sem, 0

    def wait(self, more=1):
        self.n = self.n + more
        self.eng.wait_ge(self.sem, self.n)


class Chain:

    def __init__(self, eng, sem):
        self.eng, self.sem, self.n = eng, sem, 0

    def __call__(self, ins):
        self.open(ins)
        self.close()

    def open(self, ins):
        ins.then_inc(self.sem, 1)
        self.n = self.n + 1

    def close(self):
        self.eng.wait_ge(self.sem, self.n)


def hybrid_kernel(nc, x, a_w, a_wab, a_small, a_conv, a_bog, a_bout, a_wout, b_w, b_dft, b_idft,
                  f_w, f_n, f_qk, f_mid, f_down, f_wo, f_rows, eye, causal, out):
    ctx = ExitStack()
    with ctx:
        def sem(name):
            return ctx.enter_context(nc.semaphore(name))

        def sb(name, shape, dt=F32, at=None, side=None):
            return (at or ctx).enter_context(nc.sbuf_tensor(name, shape, dt, side=side))

        def dram(name, shape, dt=F32):
            return nc.dram_tensor(name, shape, dt, kind="Internal").ap()

        X = sb("X", [P, TILES, D])
        XL = sb("XL", [P, TILES, D])
        SQ = sb("SQ", [P, TILES, D])
        HT = sb("HT", [P, NT])
        ident = sb("ident", [P, P])
        stat = sb("stat", [P, TILES])
        var = sb("var", [P, TILES])
        bst = sb("bst", [P, TILES, 6])
        mv = sb("mv", [P, TILES, 2])
        rstd = sb("rstd", [P, TILES])
        rrms = sb("rrms", [P, TILES])
        PS = ctx.enter_context(nc.psum_tensor("PS", [P, 8, CH], F32))

        with ExitStack() as sa:
            aw = sb("aw", [P, A_COLS], at=sa)
            awab = sb("awab", [P, 4, 32], at=sa)
            asm = sb("asm", [P, S_COLS], at=sa)
            nwb = sb("nwb", [P, 4], at=sa)
            tapb = sb("tapb", [P, 3, 4], at=sa)
            cb = sb("cb", [P, 3, 4], at=sa)
            abog = sb("abog", [P, D], at=sa)
            about = sb("about", [P, D], at=sa)
            awout = sb("awout", [P, 3, D], at=sa)
            ones = sb("ones", [P, 1], at=sa)
            ALP = sb("ALP", [P, ST], at=sa)
            BET = sb("BET", [P, ST], at=sa)
            V0 = sb("V0", [P, 2, S], at=sa)
            LQK = sb("LQK", [P, 2, HD, ST], at=sa)
            WU = sb("WU", [P, 2 * HD, ST], at=sa)
            AC1 = sb("AC1", [P, NC], at=sa)
            KB = XL[:].rearrange("p t d -> p (t d)").rearrange("p (d s) -> p d s", d=HD)
            VS = HT[:].rearrange("p (e s) -> p e s", e=2)
            DJ = WU[:, HD:2 * HD, :]
            SJ = WU[:, 0:4, :].rearrange("p a (c j i) -> p a c j i", c=NC, j=2)
            with ExitStack() as s1:
                CBC = sb("CBC", [P, 3 * 4, D], at=s1)
                CWT = sb("CWT", [P, 3 * 4, D], at=s1)
                ANG = sb("ANG", [P, S], at=s1)
                TRA = [sb(f"TRA{l}", [P, 2, 3, S >> l], at=s1) for l in range(11)]
                TRV = [V0] + [sb(f"TRV{l}", [P, 2, S >> l], at=s1) for l in range(1, 11)]
                TRT = sb("TRT", [P, 2, 3, S // 2], at=s1)
                CY = [sb(f"CY{i}", [P, B, S], at=s1) for i in range(2)]
                LSQ = [t[:].rearrange("p b s -> p (b s)").rearrange("p (d t) -> p d t", d=HD) for t in CY]
                UEO = sb("UEO", [P, 2, S], at=s1)
                SIN = sb("SIN", [P, S], at=s1)
                COS = sb("COS", [P, S], at=s1)
            with ExitStack() as s23:
                PA = sb("PA", [P, NC, C, C], at=s23)
                with ExitStack() as sk:
                    K2 = sb("K2", [P, SEG, HD, ST], at=sk)
                    with ExitStack() as s2:
                        PRD = sb("PRD", [P, 2 * HD * ST], at=s2)
                        PRP = [sb(f"PRP{i}", [P, HD * ST], at=s2) for i in range(2)]
                        SS = sb("SS", [P, 2, ST], at=s2)
                        RS = sb("RS", [P, 2, ST], at=s2)
                        NG0 = sb("NG0", [P, ST], at=s2)
                        GAM = sb("GAM", [P, NC, C + 1, C + 1], at=s2)
                        LA = sb("LA", [P, NC, C, C], at=s2)
                    with ExitStack() as s3:
                        W2 = sb("W2", [P, SEG, HD, ST], at=s3)
                        U2 = sb("U2", [P, SEG, 2, ST], at=s3)
                        D2 = sb("D2", [P, SEG, 2, ST], at=s3)
                        S2 = sb("S2", [P, SEG * NC + 1, 2, HD], at=s3)
                        AC2 = sb("AC2", [P, SEG, NC], at=s3)
                        P1 = sb("P1", [P, 2, 2, C, HD + 1], at=s3)
                        P2 = sb("P2", [P, 2, HD, C + 1], at=s3)
                with ExitStack() as s4:
                    RO = sb("RO", [P, HD, ST], at=s4)
                    RP = sb("RP", [P, HD, ST], at=s4)
                    PRR = sb("PRR", [P, NC * C * HD], at=s4)
                    PRQ = [sb(f"PRQ{i}", [P, NC * HD * C], at=s4) for i in range(2)]
                    RT = sb("RT", [P, B, S], at=s4)
                    SS4 = sb("SS4", [P, ST], at=s4)
                    OT = sb("OT", [P, TILES, D], at=s4)
                    vss = sb("vss", [P, TILES], at=s4)
        qkv_d = dram("qkv_d", (3, B, D, S))
        w_d = dram("w_d", (SEG, BH, HD, ST))
        k_d = dram("k_d", (SEG, BH, HD, ST))
        u_d = dram("u_d", (SEG, BH, HD, ST))
        ac_d = dram("ac_d", (BH, SEG, NC))
        d_d = dram("d_d", (SEG, BH, HD, ST))
        s_d = dram("s_d", (SEG, BH, 4, NC * 2 * HD))
        r_d = dram("r_d", (BH, HD, S))

        with ExitStack() as sw:
            bw = sb("bw", [P, 3, D], at=sw, side="right")
            bdft = sb("bdft", [P, 2, NB], at=sw, side="right")
            bidft = sb("bidft", [P, 2, D], at=sw, side="right")
            bwf = sb("bwf", [P, 3, 2, NB], at=sw, side="right")
            identb = sb("identb", [P, P], BF16, at=sw, side="right")
            maskb = sb("maskb", [P, P], BF16, at=sw, side="right")
            maskf = sb("maskf", [P, P], at=sw, side="right")
            fw = sb("fw", [P, F_COLS], at=sw, side="right")
            fn = sb("fn", [P, 2], at=sw, side="right")
            fqk = sb("fqk", [P, 2, HD], at=sw, side="right")
            fmid = sb("fmid", [P, 5, HID], at=sw, side="right")
            fdown = sb("fdown", [P, E4, 2, OUTC], at=sw, side="right")
            fwo = sb("fwo", [P, OUTC], at=sw, side="right")
            frows = sb("frows", [P, NG], at=sw, side="right")
            KS = [sb(f"KS{i}", [P, GH, S], BF16, at=sw) for i in range(2)]
            QS = [sb(f"QS{i}", [P, GH, S], BF16, at=sw) for i in range(2)]
            VA = [sb(f"VA{i}", [P, TB, GH, 32], at=sw) for i in range(2)]
            with ExitStack() as sB:
                QF = [sb(f"QF{i}", [P, 3, 2, CH], at=sB) for i in range(3)]
                KV = [sb(f"KV{i}", [P, 4, CH], at=sB) for i in range(2)]
                SQF = sb("SQF", [P, 2, 2, CH], at=sB)
                mag = [sb(f"mag{i}", [P, 2, CH], at=sB) for i in range(2)]
                PRB = sb("PRB", [P, 4, CH], at=sB)
                CUM = sb("CUM", [P, 2, B, S], at=sB)
                YF = sb("YF", [P, 2, NT], at=sB)
            with ExitStack() as sF:
                QKV = sb("QKV", [P, TILES, 3 * D], at=sF)
                PX = [sb(f"PX{i}", [P, 2, CH], at=sF) for i in range(3)]
                QQ = [PX[b][:].rearrange("p n (t d) -> p (n t) d", d=D) for b in range(B)]
                DEN = sb("DEN", [P, CH], at=sF)
                AO = sb("AO", [P, NT], at=sF)
                with ExitStack() as f0:
                    QKS = sb("QKS", [P, TILES, 2 * D], at=f0)
                    qst = sb("qst", [P, TILES, 2 * H], at=f0)
                    qst2 = sb("qst2", [P, TILES, 2 * H], at=f0)
                    QR = [sb(f"QR{i}", [P, 2, CH], at=f0) for i in range(2)]
                    MT = sb("MT", [H, NT], BF16, at=f0)
                    QP = [sb(f"QP{i}", [P, 2, NT], BF16, at=f0) for i in range(3)]
                with ExitStack() as f3:
                    lg = sb("lg", [P, TILES, E4], at=f3)
                    pr = sb("pr", [P, TILES, E4], at=f3)
                    cnt = sb("cnt", [P, TILES, E4], at=f3)
                    ge = sb("ge", [P, TILES], at=f3)
                    red = sb("red", [P, TILES], at=f3)
                    wts = sb("wts", [P, TILES, E4], at=f3)
                    HS = [sb(f"HS{i}", [P, 2, CH], at=f3) for i in range(2)]
                    HG = [sb(f"HG{i}", [P, 2, CH], at=f3) for i in range(2)]
                    H0 = [sb(f"H0{i}", [P, 2, CH], at=f3) for i in range(2)]
                    HA = sb("HA", [P, 2, CH], at=f3)
                    HB = sb("HB", [P, 2, CH], at=f3)
                    HC = sb("HC", [P, 2, CH], at=f3)
                    HE = sb("HE", [P, CH], at=f3)
                    HF = sb("HF", [P, 2, CH], at=f3)
        qs_d = dram("qs_d", (H, QROWS, NT), BF16)
        ks_d = dram("ks_d", (H, QROWS, NT), BF16)


        psum_read = sem("psum_read")
        psum_full = sem("psum_full")
        to_act = sem("to_act")
        normed = sem("normed")
        to_dve = sem("to_dve")
        x_loaded = sem("x_loaded")
        a_loaded = sem("a_loaded")
        qkv_stored = sem("qkv_stored")
        lanes_loaded = sem("lanes_loaded")
        k_decayed = sem("k_decayed")
        k_stored = sem("k_stored")
        k_loaded = sem("k_loaded")
        wk_ready = sem("wk_ready")
        wk_stored = sem("wk_stored")
        u_solved = sem("u_solved")
        u_stored = sem("u_stored")
        seg_loaded = [sem(f"seg_loaded{i}") for i in range(SEG)]
        chunk_done = sem("chunk_done")
        ds_stored = sem("ds_stored")
        ds_loaded = sem("ds_loaded")
        reads_ready = sem("reads_ready")
        reads_stored = sem("reads_stored")
        rt_loaded = sem("rt_loaded")
        taps_ready = sem("taps_ready")
        wout_ready = sem("wout_ready")
        ones_set = sem("ones_set")
        vs_ready = sem("vs_ready")
        trig_in = sem("trig_in")
        trig_ready = sem("trig_ready")
        lanes_squared = sem("lanes_squared")
        gate_in = sem("gate_in")
        gate_ready = sem("gate_ready")
        state_clear = sem("state_clear")
        u_slot = sem("u_slot")
        s_slot = sem("s_slot")
        tree_in = sem("tree_in")
        level_done = sem("level_done")
        kb_ready = sem("kb_ready")
        lanes_clear = sem("lanes_clear")
        prod_ready = sem("prod_ready")
        prod_used = sem("prod_used")
        decays_ready = sem("decays_ready")
        la_ready = sem("la_ready")
        rprod_ready = sem("rprod_ready")
        rprod_used = sem("rprod_used")
        x_ready = sem("x_ready")
        w_loaded = sem("w_loaded")
        y_ready = sem("y_ready")
        values_added = sem("values_added")
        values_full = sem("values_full")
        squares_ready = sem("squares_ready")
        unit_ready = sem("unit_ready")
        kv_ready = sem("kv_ready")
        sums_ready = sem("sums_ready")
        stack_clear = sem("stack_clear")
        parts_stored = sem("parts_stored")
        part_high = sem("part_high")
        parts_ready = sem("parts_ready")
        third_parts = sem("third_parts")
        probs_used = sem("probs_used")
        stack_loaded = [sem(f"stack_loaded{i}") for i in range(B)]
        v_ready = sem("v_ready")
        fw_ready = sem("fw_ready")
        qk_normed = sem("qk_normed")
        shifts_ready = sem("shifts_ready")
        probs_ready = sem("probs_ready")
        scores_ready = sem("scores_ready")
        o_read = sem("o_read")
        heads_added = sem("heads_added")
        proj_full = sem("proj_full")
        up_full = sem("up_full")
        up_read = sem("up_read")
        h1_ready = sem("h1_ready")
        down_read = sem("down_read")
        down_full = sem("down_full")
        q_squared = sem("q_squared")
        rest_ready = sem("rest_ready")
        den_ready = sem("den_ready")
        proj_added = sem("proj_added")
        x_sum = sem("x_sum")
        out_stored = sem("out_stored")
        act_chain = sem("act_chain")
        dve_chain = sem("dve_chain")
        pool_chain = sem("pool_chain")

        def bcast(ap, at, n):
            ap = ap.unsqueeze(at)
            shape = list(ap.shape)
            shape[at] = n
            return ap.to_broadcast(shape)

        class Banks:

            def __init__(self, pe):
                self.pe, self.n = pe, 0

            def take(self):
                if self.n >= 8:
                    self.pe.wait_ge(psum_read, self.n - 7)
                self.n += 1
                return (self.n - 1) % 8

            def all_read(self):
                self.pe.wait_ge(psum_read, self.n)

        class Reads:

            def __init__(self, eng):
                self.eng, self.n = eng, 0

            def next(self):
                self.n += 1
                self.eng.wait_ge(psum_full, self.n)
                return (self.n - 1) % 8

        def dve_norm(v, link, ans, eps, dst, rms_eps=None):
            v.tensor_scalar(stat[:], mv[:, :, 1], eps, None, ALU.add).then_inc(to_act, 1)
            ans.wait()
            link(v.reciprocal(rstd[:], stat[:]))
            scale = rstd
            if rms_eps is not None:
                link(v.tensor_tensor(var[:], mv[:, :, 1], rstd[:], ALU.mult))
                link(v.tensor_tensor(var[:], var[:], rstd[:], ALU.mult))
                v.tensor_scalar(stat[:], var[:], rms_eps, None, ALU.add).then_inc(to_act, 1)
                ans.wait()
                link(v.reciprocal(rrms[:], stat[:]))
                link(v.tensor_tensor(rrms[:], rrms[:], rstd[:], ALU.mult))
                scale = rrms
            for b in range(B):
                for t in range(b * TB, (b + 1) * TB):
                    last = center_and_scale(v, dst, t, scale)
                last.then_inc(normed, 1)

        def dve_stats(v, link, tiles):
            for t in tiles:
                link.open(v.bn_stats(bst[:, t], X[:, t]))
            link.close()
            for t in tiles:
                link.open(v.bn_aggr(mv[:, t], bst[:, t]))
            link.close()

        def center_and_scale(v, dst, t, scale):
            return v.tensor_scalar(dst[:, t], X[:, t], mv[:, t, 0:1], scale[:, t:t + 1], ALU.subtract, ALU.mult)

        def act_sqrt(act, ask, ap):
            ask.wait()
            act.activation(ap, ap, ACT.Sqrt).then_inc(to_dve, 1)

        def pe_transpose_in(pe, banks, src, norm, chunks=range(NCH), at=None):
            for g in chunks:
                if g % (NCH // B) == 0:
                    pe.wait_ge(normed, norm * B + g // (NCH // B) + 1)
                k = banks.take()
                if at is not None:
                    k = at + g
                for i in range(TPC):
                    last = pe.transpose(PS[:, k, i * P:(i + 1) * P], src[:, g * TPC + i, :], ident[:])
                last.then_inc(psum_full, 1)

        def act_ht(act, reads, chunks=range(NCH), at=None):
            for g in chunks:
                k = reads.next()
                if at is not None:
                    k = at + g
                act.activation(HT[:, g * CH:(g + 1) * CH], PS[:, k, :], ACT.Copy).then_inc(psum_read, 1)

        A_RES = 34

        def lanes(t):
            return t.rearrange("p d (c s) -> p c s d", s=C)

        def a_sync(sp):
            for half in range(2):
                t = slice(half * TB, (half + 1) * TB)
                sp.dma_start(X[:, t, :], x.rearrange("(t p) d -> p t d", p=P)[:, t, :]).then_inc(x_loaded, 16)
            sp.dma_start(ident[:], eye).then_inc(x_loaded, 16)
            for dst, src in ((aw, a_w), (awab, a_wab), (asm, a_small), (awout, a_wout)):
                sp.dma_start(dst[:], src).then_inc(a_loaded, 16)
            sp.dma_start(CBC[:].rearrange("p n d -> p (n d)"), a_conv.partition_broadcast(P)).then_inc(a_loaded, 16)
            sp.dma_start(abog[:], a_bog.partition_broadcast(P)).then_inc(a_loaded, 16)
            sp.dma_start(about[:], a_bout.partition_broadcast(P)).then_inc(a_loaded, 16)
            for n in range(3):
                sp.wait_ge(psum_read, 15 + NCH * (n + 1))
                sp.dma_start(qkv_d[n].rearrange("b p s -> p b s"), CY[n % 2][:]).then_inc(qkv_stored, 16)
                sp.wait_ge(qkv_stored, 16 * (n + 1))
                src = qkv_d[n].rearrange("b (h d) s -> (b h) d s", d=HD)
                for g in range(SEG):
                    rows = slice(g * BH, (g + 1) * BH)
                    dst = LQK[rows, n, :, :] if n < 2 else WU[rows, HD:2 * HD, :]
                    sp.dma_start(dst, src[:, :, g * ST:(g + 1) * ST]).then_inc(lanes_loaded, 16)
            sp.wait_ge(k_decayed, 1)
            sp.dma_start(k_d.rearrange("g h i t -> (g h) i t"), KB).then_inc(k_stored, 16)
            sp.dma_start(ac_d.rearrange("h g c -> g h c"), AC1[:]).then_inc(k_stored, 16)
            sp.wait_ge(k_stored, 32)
            for g in range(SEG):
                sp.dma_start(K2[:, g],
                             bcast(k_d[g].rearrange("h i t -> h (i t)"), 0, 4)).then_inc(k_loaded, 16)
            sp.wait_ge(wk_ready, 1)
            sp.dma_start(w_d.rearrange("g h i t -> (g h) i t"), WU[:, 0:HD, :]).then_inc(wk_stored, 16)
            sp.wait_ge(u_solved, 2)
            sp.dma_start(u_d.rearrange("g h i t -> (g h) i t"), WU[:, HD:2 * HD, :]).then_inc(u_stored, 16)
            sp.dma_start(AC2[:],
                         bcast(ac_d.rearrange("h g c -> h (g c)"), 0, 4)).then_inc(k_loaded, 16)
            sp.wait_ge(wk_stored, 16)
            for g in range(SEG):
                sp.dma_start(W2[:, g],
                             bcast(w_d[g].rearrange("h i t -> h (i t)"), 0, 4)).then_inc(seg_loaded[g], 16)
                if g == 0:
                    sp.wait_ge(u_stored, 16)
                sp.dma_start(U2[:, g],
                             u_d[g].rearrange("h (j e) t -> j h (e t)", j=4)).then_inc(seg_loaded[g], 16)
            w_sync(sp)
            for g in range(SEG):
                rows = slice(g * BH, (g + 1) * BH)
                sp.wait_ge(chunk_done, (g + 1) * NC)
                sp.dma_start(d_d[g].rearrange("h (j e) t -> j h (e t)", j=4),
                             D2[:, g]).then_inc(ds_stored, 16)
                sp.dma_start(s_d[g].rearrange("h j r -> j h r"),
                             S2[:, g * NC:(g + 1) * NC]).then_inc(ds_stored, 16)
                sp.wait_ge(ds_stored, 32 * (g + 1))
                sp.dma_start(DJ[rows], d_d[g]).then_inc(ds_loaded, 16)
                sp.dma_start(SJ[rows].rearrange("p a c j i -> p a (c j i)"), s_d[g]).then_inc(ds_loaded, 16)
            sp.wait_ge(reads_ready, 1)
            for g in range(SEG):
                sp.dma_start(r_d[:, :, g * ST:(g + 1) * ST], RO[g * BH:(g + 1) * BH]).then_inc(reads_stored, 16)
            sp.wait_ge(reads_stored, 64)
            sp.dma_start(RT[:], r_d.rearrange("(b h) j s -> (h j) b s", b=B)).then_inc(rt_loaded, 16)

        PAIRS = ((A_ANG, 4), (A_UE, 0), (A_UO, 1), (A_CE, 2), (A_CO, 3))

        def a_tensor(pe, banks):
            pe.wait_ge(x_loaded, 48)
            pe.wait_ge(a_loaded, 112)
            pe_transpose_in(pe, banks, XL, 0)
            banks.all_read()

            def pair(col):
                for c in range(S // CH):
                    k = banks.take()
                    for b in range(B):
                        t = b * S + c * CH
                        last = pe.matmul(PS[64 * b:64 * b + 64, k, :], aw[:, col:col + 64], HT[:, t:t + CH],
                                         start=True, stop=True)
                    last.then_inc(psum_full, 1)

            for col, _ in PAIRS[:3]:
                pair(col)
            k = banks.take()
            for w in range(2):
                for g in range(SEG):
                    for b in range(B):
                        t = b * S + g * ST
                        last = pe.matmul(PS[g * BH:(g + 1) * BH, k, w * ST:(w + 1) * ST], awab[:, 2 * w + b, :],
                                         HT[:, t:t + ST], start=(b == 0), stop=(b == B - 1))
            last.then_inc(psum_full, 1)
            for col, _ in PAIRS[3:]:
                pair(col)
            pe.wait_ge(taps_ready, 2)
            for n in range(3):
                for c in range(NCH):
                    k = banks.take()
                    for j in (3, 2, 1, 0):
                        back = 3 - j
                        skip = back if c % (S // CH) == 0 else 0
                        t = c * CH
                        last = pe.matmul(PS[:, k, skip:CH], CWT[:, 4 * n + j, :], HT[:, t + skip - back:t + CH - back],
                                         start=(j == 3), stop=True, skip_group_check=True)
                    last.then_inc(psum_full, 1)
            for g in range(NCH):
                k = banks.take()
                for i in range(TPC):
                    t = (g * TPC + i) * P
                    last = pe.matmul(PS[:, k, i * P:(i + 1) * P], HT[:, t:t + P], aw[:, A_OG:A_OG + D],
                                     start=True, stop=True)
                last.then_inc(psum_full, 1)
            banks.all_read()
            pe.wait_ge(wout_ready, 3)
            pe.wait_ge(ones_set, 1)
            pe.wait_ge(vs_ready, 1)
            for b in range(B):
                for t in range(TB):
                    last = pe.matmul(PS[:, b, t:t + 1], VS[64 * b:64 * b + 64, 0, t * P:(t + 1) * P],
                                     ones[64 * b:64 * b + 64, :], start=True, stop=True)
            last.then_inc(psum_full, 1)
            banks.n += 1
            for g in range(NCH):
                for i in range(TPC):
                    b, t = divmod(g * TPC + i, TB)
                    rows = slice(64 * b, 64 * b + 64)
                    for e in range(2):
                        last = pe.matmul(PS[:, 4 + g, i * P:(i + 1) * P], V0[rows, e, t * P:(t + 1) * P],
                                         awout[rows, 1 + e, :], start=(e == 0), stop=(e == 1))
            last.then_inc(psum_full, 1)
            banks.n += 1
            pe.wait_ge(rt_loaded, 16)
            pe.wait_ge(psum_read, 32)
            for g in range(NCH):
                for i in range(TPC):
                    b, t = divmod(g * TPC + i, TB)
                    last = pe.matmul(PS[:, g, i * P:(i + 1) * P], RT[:, b, t * P:(t + 1) * P], awout[:, 0, :],
                                     start=True, stop=True)
            last.then_inc(psum_full, 1)
            banks.n += 1

        def a_scalar(act, link, ask, reads):
            act_sqrt(act, ask, stat[:])
            act_ht(act, reads)
            act.wait_ge(a_loaded, 112)

            def bias(col):
                return asm[:, col:col + 1]

            def pair(dst, n, func):
                for c in range(S // CH):
                    k = reads.next()
                    act.activation(dst[:, c * CH:(c + 1) * CH], PS[:, k, :], func,
                                   bias=bias(S_BPAIR + n)).then_inc(psum_read, 1)

            pair(ANG[:], 4, ACT.Identity)
            pair(UEO[:, 0], 0, ACT.Sigmoid)
            pair(UEO[:, 1], 1, ACT.Sigmoid)
            k = reads.next()
            link(act.activation(ALP[:], PS[:, k, 0:ST], ACT.Sigmoid, bias=bias(S_BAB)))
            act.activation(BET[:], PS[:, k, ST:2 * ST], ACT.Sigmoid, bias=bias(S_BAB + 1)).then_inc(psum_read, 1)
            pair(TRA[0][:, 0, 2], 2, ACT.Silu)
            pair(TRA[0][:, 1, 2], 3, ACT.Silu)
            act.wait_ge(trig_in, 1)
            act.activation(SIN[:], SIN[:], ACT.Sin).then_inc(trig_ready, 1)
            act.activation(COS[:], COS[:], ACT.Sin).then_inc(trig_ready, 1)

            act.wait_ge(taps_ready, 2)
            for n in range(3):
                if n >= 2:
                    act.wait_ge(qkv_stored, 16 * (n - 1))
                for c in range(NCH):
                    k = reads.next()
                    b, h = divmod(c, S // CH)
                    first = 0
                    if h == 0:
                        first = 3
                        for t in range(first):
                            act.activation(CY[n % 2][:, b, t:t + 1], PS[:, k, t:t + 1], ACT.Silu,
                                           bias=cb[:, n, t:t + 1])
                    act.activation(CY[n % 2][:, b, h * CH + first:(h + 1) * CH], PS[:, k, first:CH], ACT.Silu,
                                   bias=cb[:, n, 3:4]).then_inc(psum_read, 1)
            for g in range(NCH):
                k = reads.next()
                act.activation(SQ[:, g * TPC:(g + 1) * TPC, :].rearrange("p t d -> p (t d)"), PS[:, k, :],
                               ACT.Copy).then_inc(psum_read, 1)
            act.wait_ge(lanes_loaded, 16 * 12)
            for n in range(2):
                act.activation(LSQ[n], LQK[:, n], ACT.Square).then_inc(lanes_squared, 1)
            act.wait_ge(gate_in, 1)
            act.activation(SQ[:], SQ[:], ACT.Sigmoid).then_inc(gate_ready, 1)
            act_sqrt(act, ask, SS[:])
            act.wait_ge(state_clear, 1)
            act.wait_ge(k_loaded, 16 * (SEG + 1))

            def u_in(n):
                g, c = divmod(n, NC)
                if c == 0:
                    act.wait_ge(seg_loaded[g], 32)
                act.activation(P1[:, n % 2, :, :, HD], U2[:, g, :, c * C:(c + 1) * C], ACT.Copy).then_inc(u_slot, 1)

            u_in(0)
            for n in range(SEG * NC):
                g, c = divmod(n, NC)
                if n:
                    act.wait_ge(chunk_done, n)
                act.activation(P2[:, :, :, C], S2[:, n], ACT.Copy, scale=AC2[:, g, c:c + 1]).then_inc(s_slot, 1)
                if n + 1 < SEG * NC:
                    u_in(n + 1)
            act_sqrt(act, ask, SS4[:])
            act_sqrt(act, ask, vss[:])
            reads.n += 3

        def a_vector(v, link, ans):
            v.wait_ge(x_loaded, 48)
            dve_stats(v, link, range(TILES))
            dve_norm(v, link, ans, LN_EPS, XL)
            v.wait_ge(a_loaded, 112)
            link(v.tensor_scalar(nwb[:], asm[:, S_WB:S_WB + 4], -1.0, None, ALU.mult))
            for i in range(3):
                v.tensor_scalar(awout[:, i], awout[:, i], asm[:, S_RMS + i:S_RMS + i + 1], None,
                                ALU.mult).then_inc(wout_ready, 1)
            v.wait_ge(psum_read, 6)
            link(v.tensor_scalar(SIN[:], ANG[:], 1.0 / TWO_PI, MAGIC, ALU.mult, ALU.add))
            link(v.tensor_scalar(SIN[:], SIN[:], -MAGIC, None, ALU.add))
            link(v.scalar_tensor_tensor(out=ANG[:], in0=SIN[:], scalar=-TWO_PI_HI, in1=ANG[:],
                                        op0=ALU.mult, op1=ALU.add))
            link(v.scalar_tensor_tensor(out=ANG[:], in0=SIN[:], scalar=TWO_PI_HI - TWO_PI, in1=ANG[:],
                                        op0=ALU.mult, op1=ALU.add))
            link(v.tensor_scalar(SIN[:], ANG[:], -PI, PI, ALU.max, ALU.min))
            link(v.scalar_tensor_tensor(out=COS[:], in0=SIN[:], scalar=-1.0, in1=SIN[:], op0=ALU.mult, op1=ALU.min))
            v.tensor_scalar(COS[:], COS[:], TWO_PI / 4, None, ALU.add).then_inc(trig_in, 1)
            v.wait_ge(psum_read, 15)
            v.wait_ge(trig_ready, 2)
            tmp = TRT[:].rearrange("p a b s -> p (a b s)")[:, 0:S]
            wb = [asm[:, S_WB + i:S_WB + i + 1] for i in range(4)]
            for row, u in ((0, UEO[:, 0]), (1, UEO[:, 1])):
                link.open(v.tensor_tensor(ANG[:], u, COS[:], ALU.mult))
                link(v.tensor_tensor(tmp, u, SIN[:], ALU.mult))
                for i in range(2):
                    m = TRA[0][:, row, i, :]
                    first, by, second, by2 = ((ANG[:], wb[2 * i], tmp, nwb[:, 2 * i + 1:2 * i + 2]) if row == 0 else
                                              (tmp, wb[2 * i], ANG[:], wb[2 * i + 1]))
                    link(v.tensor_scalar(m, first, by, None, ALU.mult))
                    link(v.scalar_tensor_tensor(out=m, in0=second, scalar=by2, in1=m, op0=ALU.mult, op1=ALU.add))
            link(v.tensor_tensor(UEO[:], UEO[:], TRA[0][:, :, 2, :], ALU.mult))
            v.tensor_tensor(TRA[0][:, :, 2, :], TRA[0][:, :, 2, :], UEO[:], ALU.subtract).then_inc(tree_in, 1)
            v.wait_ge(tree_in, 1)
            fold(v, link, 1, slice(POOL_FOLDS, S // 2))
            v.wait_ge(level_done, 1)
            for l in range(2, 11):
                fold(v, link, l, slice(0, S >> l))
            link(v.tensor_copy(TRV[10][:], TRA[10][:, :, 2, :]))
            for l in range(9, -1, -1):
                unfold(v, link, l)
            v.wait_ge(lanes_loaded, 16 * 12)
            for n in range(2):
                v.wait_ge(lanes_squared, n + 1)
                link(v.tensor_reduce(SS[:, n], LSQ[n].rearrange("p d t -> p t d"), AX.X, ALU.add))
            v.tensor_scalar(SS[:], SS[:], L2_EPS, None, ALU.add).then_inc(to_act, 1)
            ans.wait()
            link(v.reciprocal(RS[:], SS[:]))
            link(v.tensor_tensor(LQK[:], LQK[:], bcast(RS[:], 2, HD), ALU.mult))
            v.tensor_tensor(KB, LQK[:, 1], bcast(BET[:], 1, HD), ALU.mult).then_inc(kb_ready, 1)
            v.wait_ge(kb_ready, 1)
            v.wait_ge(lanes_clear, 2)
            kn = lanes(LQK[:, 1])
            kb = lanes(KB)
            for s in range(C + 1):
                if s < C - 1:
                    n = C - 1 - s
                    pv = PRD[:, 0:NC * n * HD].rearrange("p (c t d) -> p c t d", c=NC, d=HD)
                    link(v.tensor_tensor(pv, kn[:, :, s + 1:C, :], bcast(kb[:, :, s, :], 2, n), ALU.mult))
                    link(v.tensor_reduce(LA[:, :, s + 1:C, s], pv, AX.X, ALU.add))
                if s == 0:
                    link(v.tensor_tensor(PRP[0][:].rearrange("p (c t d) -> p c t d", c=NC, d=HD), lanes(LQK[:, 0]),
                                         bcast(kb[:, :, 0, :], 2, C), ALU.mult))
                else:
                    n = C - s + 1
                    if s > 1:
                        v.wait_ge(prod_ready, s - 1)
                    pp = PRP[(s - 1) % 2][:, 0:NC * n * HD].rearrange("p (c t d) -> p c t d", c=NC, d=HD)
                    v.tensor_reduce(PA[:, :, s - 1:C, s - 1], pp, AX.X, ALU.add).then_inc(prod_used, 1)
            v.wait_ge(prod_used, C)
            v.wait_ge(decays_ready, 1)
            v.tensor_tensor(LA[:], LA[:], GAM[:, :, 0:C, 1:C + 1], ALU.mult).then_inc(la_ready, 1)
            link.open(v.tensor_tensor(PA[:], PA[:], GAM[:, :, 1:C + 1, 1:C + 1], ALU.mult))
            link(v.tensor_scalar(NG0[:].rearrange("p (c s) -> p c s", s=C), GAM[:, :, 0:C, 0], -1.0, None, ALU.mult))
            q4 = LQK[:, 0].rearrange("p d (c s) -> p d c s", s=C)
            k4 = KB.rearrange("p d (c s) -> p d c s", s=C)
            link.open(v.tensor_copy(AC1[:], GAM[:, :, C, 0]))
            v.tensor_tensor(k4, k4, bcast(GAM[:, :, C, 1:C + 1], 1, HD), ALU.mult).then_inc(k_decayed, 1)
            link.open(v.tensor_tensor(WU[:, 0:HD, :], LQK[:, 1], bcast(NG0[:], 1, HD), ALU.mult))
            link.open(v.tensor_tensor(q4, q4, bcast(GAM[:, :, 1:C + 1, 0], 1, HD), ALU.mult))
            link.close()
            v.wait_ge(la_ready, 1)
            solve(v, link, 0, HD, PRD, wk_ready)
            v.wait_ge(wk_ready, 1)
            solve(v, link, HD, V_U, PRD, u_solved)
            v.wait_ge(u_solved, 2)
            v.memset(S2[:, 0], 0.0).then_inc(state_clear, 1)
            v.wait_ge(state_clear, 1)
            v.wait_ge(k_loaded, 16 * (SEG + 1))
            for n in range(SEG * NC):
                g, c = divmod(n, NC)
                cs = slice(c * C, (c + 1) * C)
                if c == 0:
                    v.wait_ge(seg_loaded[g], 32)
                if n:
                    v.wait_ge(chunk_done, n)
                link(v.tensor_tensor(P1[:, n % 2, :, :, 0:HD], bcast(W2[:, g, :, cs].rearrange("p i s -> p s i"), 1, 2),
                                     bcast(S2[:, n], 2, C), ALU.mult))
                v.wait_ge(u_slot, n + 1)
                link(v.tensor_reduce(D2[:, g, :, cs], P1[:, n % 2], AX.X, ALU.add))
                link(v.tensor_tensor(P2[:, :, :, 0:C], bcast(K2[:, g, :, cs], 1, 2), bcast(D2[:, g, :, cs], 2, HD),
                                     ALU.mult))
                v.wait_ge(s_slot, n + 1)
                v.tensor_reduce(S2[:, n + 1], P2[:], AX.X, ALU.add).then_inc(chunk_done, 1)
            w_vector(v, link)
            v.wait_ge(ds_loaded, 32 * SEG)
            qa = lanes(LQK[:, 0])
            pr3 = PRR[:].rearrange("p (c s i) -> p c s i", c=NC, i=HD)
            for j in range(HD):
                link(v.tensor_tensor(pr3, qa, bcast(SJ[:, j // 2, :, j % 2, :], 2, C), ALU.mult))
                link(v.tensor_reduce(RP[:, j].rearrange("p (c s) -> p c s", s=C), pr3, AX.X, ALU.add))
                for t in (2 * j, 2 * j + 1):
                    v.wait_ge(rprod_ready, t + 1)
                    pq = PRQ[t % 2][:, 0:NC * HD * (t + 1)].rearrange("p (c j s) -> p c j s", c=NC, j=HD)
                    v.tensor_reduce(RO[:].rearrange("p j (c s) -> p c j s", s=C)[:, :, :, t], pq, AX.X,
                                    ALU.add).then_inc(rprod_used, 1)
            v.wait_ge(rprod_used, C)
            link(v.tensor_tensor(RO[:], RO[:], RP[:], ALU.add))
            link(v.tensor_tensor(RP[:], RO[:], RO[:], ALU.mult))
            link(v.tensor_reduce(SS4[:], RP[:].rearrange("p j t -> p t j"), AX.X, ALU.add))
            v.tensor_scalar(SS4[:], SS4[:], 1.0 / HD, A_EPS, ALU.mult, ALU.add).then_inc(to_act, 1)
            ans.wait()
            link(v.reciprocal(RP[:, 0], SS4[:]))
            v.tensor_tensor(RO[:], RO[:], bcast(RP[:, 0], 1, HD), ALU.mult).then_inc(reads_ready, 1)
            v.wait_ge(psum_full, 32)
            v.tensor_copy(vss[:].rearrange("p (b t) -> p b t", b=B), PS[:, 0:B, 0:TB]).then_inc(psum_read, 1)
            v.wait_ge(psum_read, 32)
            v.tensor_scalar(vss[:], vss[:], 1.0 / D, A_EPS, ALU.mult, ALU.add).then_inc(to_act, 1)
            ans.wait()
            link(v.reciprocal(rrms[:], vss[:]))
            v.wait_ge(psum_full, 33)
            v.tensor_tensor(OT[:], PS[:, 4:8, :].rearrange("p b (t d) -> p (b t) d", d=D), bcast(rrms[:], 2, D),
                            ALU.mult).then_inc(psum_read, 1)
            v.wait_ge(psum_read, 33)
            link(v.tensor_tensor(OT[:], OT[:], bcast(about[:], 1, TILES), ALU.add))
            v.wait_ge(gate_ready, 1)
            link(v.tensor_tensor(OT[:], OT[:], SQ[:], ALU.mult))
            link(v.tensor_tensor(X[:], X[:], OT[:], ALU.add))
            v.wait_ge(psum_full, 34)
            v.tensor_tensor(OT[:], SQ[:], PS[:, 0:4, :].rearrange("p b (t d) -> p (b t) d", d=D),
                            ALU.mult).then_inc(psum_read, 1)
            v.wait_ge(psum_read, 34)
            v.tensor_tensor(X[:], X[:], OT[:], ALU.add).then_inc(x_ready, 1)
            v.wait_ge(x_ready, 1)
            dve_stats(v, link, range(TILES))

        V_U = 2

        def solve(eng, link, col, width, room, done):
            z = WU[:, col:col + width, :].rearrange("p d (c s) -> p c s d", s=C)
            for s in range(C - 1):
                n = C - 1 - s
                pv = room[:, 0:NC * n * width].rearrange("p (c t d) -> p c t d", c=NC, d=width)
                link(eng.tensor_tensor(pv, bcast(LA[:, :, s + 1:C, s], 3, width), bcast(z[:, :, s, :], 2, n), ALU.mult))
                ins = eng.tensor_tensor(z[:, :, s + 1:C, :], z[:, :, s + 1:C, :], pv, ALU.subtract)
                if s < C - 2:
                    link(ins)
                else:
                    ins.then_inc(done, 1)

        POOL_FOLDS = S // 6

        def fold(eng, link, l, pairs, done=None):
            steps = TRA[l - 1][:].rearrange("p a b (n two) -> p a b n two", two=2)[:, :, :, pairs]
            lo, hi, to = steps[:, :, :, :, 0], steps[:, :, :, :, 1], TRA[l][:, :, :, pairs]
            tt = TRT[:, :, :, pairs]
            link.open(eng.tensor_tensor(to, bcast(hi[:, :, 0, :], 2, 3), bcast(lo[:, 0, :, :], 1, 2), ALU.mult))
            link(eng.tensor_tensor(tt, bcast(hi[:, :, 1, :], 2, 3), bcast(lo[:, 1, :, :], 1, 2), ALU.mult))
            link(eng.tensor_tensor(to, to, tt, ALU.add))
            ins = eng.tensor_tensor(to[:, :, 2, :], to[:, :, 2, :], hi[:, :, 2, :], ALU.add)
            if done is None:
                link(ins)
            else:
                ins.then_inc(done, 1)

        def unfold(eng, link, l):
            n = S >> (l + 1)
            a, to = TRA[l], TRV[l]
            link.open(eng.tensor_copy(to[:, :, 0:1], a[:, :, 2, 0:1]))
            link(eng.tensor_copy(to[:, :, 1::2], TRV[l + 1][:]))
            if n > 1:
                tt = TRT[:, :, 0:2, 0:n - 1]
                link(eng.tensor_tensor(tt, a[:, :, 0:2, 2::2], bcast(TRV[l + 1][:, :, 0:n - 1], 1, 2), ALU.mult))
                link(eng.tensor_tensor(to[:, :, 2::2], tt[:, :, 0, :], tt[:, :, 1, :], ALU.add))
                link(eng.tensor_tensor(to[:, :, 2::2], to[:, :, 2::2], a[:, :, 2, 2::2], ALU.add))

        def a_gpsimd(pool, link):
            pool.memset(ones[:], 1.0).then_inc(ones_set, 1)
            pool.wait_ge(a_loaded, 112)
            for n in range(3):
                col = (A_Q, A_K, A_V)[n]
                link.open(pool.tensor_tensor(CWT[:, 4 * n:4 * n + 4], CBC[:, 4 * n:4 * n + 4],
                                             bcast(aw[:, col:col + D], 1, 4), ALU.mult))
            taps = asm[:, S_CONV:S_CONV + 12].rearrange("p (n j) -> p n j", j=4)
            link(pool.tensor_tensor(tapb[:], taps, bcast(asm[:, S_BQKV:S_BQKV + 3], 2, 4), ALU.mult))
            pool.tensor_copy(cb[:, :, 0], tapb[:, :, 3]).then_inc(taps_ready, 1)
            pool.wait_ge(taps_ready, 1)
            for t in range(1, 4):
                ins = pool.tensor_tensor(cb[:, :, t], cb[:, :, t - 1], tapb[:, :, 3 - t], ALU.add)
                if t < 3:
                    link(ins)
                else:
                    ins.then_inc(taps_ready, 1)
            pool.wait_ge(tree_in, 1)
            fold(pool, link, 1, slice(0, POOL_FOLDS), level_done)
            pool.wait_ge(qkv_stored, 16 * 3)
            pool.memset(LA[:], 0.0).then_inc(lanes_clear, 1)
            pool.memset(PA[:], 0.0).then_inc(lanes_clear, 1)
            pool.wait_ge(psum_read, 31)
            pool.tensor_tensor(SQ[:], SQ[:], bcast(abog[:], 1, TILES), ALU.add).then_inc(gate_in, 1)
            pool.wait_ge(to_act, 2)
            link(pool.memset(GAM[:], 1.0))
            al = ALP[:].rearrange("p (c s) -> p c s", s=C)
            for m in range(C - 1, -1, -1):
                ins = pool.tensor_tensor(GAM[:, :, m + 1:C + 1, m], GAM[:, :, m + 1:C + 1, m + 1],
                                         bcast(al[:, :, m], 2, C - m), ALU.mult)
                if m:
                    link(ins)
                else:
                    ins.then_inc(decays_ready, 1)
            pool.wait_ge(kb_ready, 1)
            qn, kb = lanes(LQK[:, 0]), lanes(KB)
            for s in range(1, C):
                n = C - s
                if s >= 2:
                    pool.wait_ge(prod_used, s - 1)
                pp = PRP[s % 2][:, 0:NC * n * HD].rearrange("p (c t d) -> p c t d", c=NC, d=HD)
                pool.tensor_tensor(pp, qn[:, :, s:C, :], bcast(kb[:, :, s, :], 2, n), ALU.mult).then_inc(prod_ready, 1)
            pool.wait_ge(la_ready, 1)
            pool.wait_ge(prod_used, C)
            solve(pool, link, HD + V_U, HD - V_U, PRP[0], u_solved)
            link.open(pool.tensor_tensor(VS[:, 0], V0[:, 0], V0[:, 0], ALU.mult))
            link(pool.tensor_tensor(VS[:, 1], V0[:, 1], V0[:, 1], ALU.mult))
            pool.tensor_tensor(VS[:, 0], VS[:, 0], VS[:, 1], ALU.add).then_inc(vs_ready, 1)
            pool.wait_ge(ds_loaded, 32 * SEG)
            dj = DJ.rearrange("p j (c s) -> p c j s", s=C)
            for t in range(C):
                if t >= 2:
                    pool.wait_ge(rprod_used, t - 1)
                pq = PRQ[t % 2][:, 0:NC * HD * (t + 1)].rearrange("p (c j s) -> p c j s", c=NC, j=HD)
                pool.tensor_tensor(pq, bcast(PA[:, :, t, 0:t + 1], 2, HD), dj[:, :, :, 0:t + 1],
                                   ALU.mult).then_inc(rprod_ready, 1)

        B_RES = 3 + NCH + 3 * NCH
        OUT_BANKS = 6

        def b_tensor(pe, banks, nth):
            base = banks.n
            pe.wait_ge(w_loaded, W_LOADED)
            pe.wait_ge(x_ready, nth)
            for n in range(3):
                k = banks.take()
                pe.matmul(PS[:, k, 0:2 * NB], bw[:, n, :], bdft[:].rearrange("p r f -> p (r f)"),
                          start=True, stop=True).then_inc(psum_full, 1)
            pe_transpose_in(pe, banks, XL, FIRST_NORM[nth])
            banks.all_read()

            def spectra(c):
                for n in range(3):
                    if c:
                        pe.wait_ge(psum_read, banks.n - 2)
                    for r in range(2):
                        last = pe.matmul(PS[0:NB, 2 * n + r, :], bwf[:, n, r, :], HT[:, c * CH:(c + 1) * CH],
                                         start=True, stop=True)
                    last.then_inc(psum_full, 1)
                    banks.n += 1

            def output(c):
                pe.wait_ge(y_ready, c + 1)
                if c >= 2:
                    pe.wait_ge(values_added, c - 1)
                for i in range(TPC):
                    t = (c * TPC + i) * P
                    for r in range(2):
                        last = pe.matmul(PS[:, OUT_BANKS + c % 2, i * P:(i + 1) * P], YF[0:NB, r, t:t + P],
                                         bidft[0:NB, r, :], start=(r == 0), stop=(r == 1))
                last.then_inc(values_full, 1)

            for c in range(NCH):
                spectra(c)
            for c in range(NCH):
                output(c)
            assert banks.n == base + B_RES

        def b_scalar(act, link, ask, reads):
            for n in range(3):
                k = reads.next()
                act.activation(bwf[:, n].rearrange("p r f -> p (r f)"), PS[:, k, 0:2 * NB],
                               ACT.Copy).then_inc(psum_read, 1)
            act_sqrt(act, ask, stat[:])
            act_ht(act, reads)
            for c in range(NCH):
                act.wait_ge(psum_full, reads.n + 2)
                act.activation(SQF[0:NB], PS[0:NB, 0:4, :].rearrange("p (n r) t -> p n r t", n=2),
                               ACT.Square).then_inc(squares_ready, 1)
                if c >= 3:
                    act_sqrt(act, ask, mag[c % 2][0:NB])
                    act.wait_ge(y_ready, c - 2)
                for n in range(3):
                    reads.next()
                    act.activation(QF[c % 3][0:NB, n], PS[0:NB, 2 * n:2 * n + 2, :], ACT.Copy).then_inc(psum_read, 1)
                if c < 3:
                    act_sqrt(act, ask, mag[c % 2][0:NB])

        def b_vector(v, link, ans, nth):
            v.wait_ge(x_ready, nth)
            dve_norm(v, link, ans, LN_EPS, XL)
            v.wait_ge(normed, B * (FIRST_NORM[nth] + 1))
            link(v.tensor_tensor(X[:], X[:], XL[:], ALU.add))
            R = slice(0, NB)

            def sum_squares(c):
                v.wait_ge(squares_ready, c + 1)
                if c >= 2:
                    v.wait_ge(unit_ready, c - 1)
                v.tensor_tensor(mag[c % 2][R], SQF[R, :, 0], SQF[R, :, 1], ALU.add).then_inc(to_act, 1)

            def unit(c):
                qk, m = QF[c % 3][R, 0:2], mag[c % 2][R]
                ans.wait()
                link(v.tensor_scalar(m, m, B_EPS, None, ALU.add))
                link(v.reciprocal(m, m))
                if c + 1 < NCH:
                    sum_squares(c + 1)
                v.wait_ge(psum_read, FIRST_RESULT[nth] + 3 + NCH + 3 * (c + 1))
                v.tensor_tensor(qk, qk, bcast(m, 2, 2), ALU.mult).then_inc(unit_ready, 1)

            def sums(c):
                b, h = divmod(c, S // CH)
                if c < NCH - 1:
                    v.wait_ge(kv_ready, c + 1)
                if h:
                    v.wait_ge(sums_ready, c)
                for r, op in ((0, ALU.subtract), (1, ALU.add)):
                    init = CUM[R, r, b, h * CH - 1:h * CH] if h else 0.0
                    last = v.tensor_tensor_scan(CUM[R, r, b, h * CH:(h + 1) * CH], KV[c % 2][R, 2 * r],
                                                KV[c % 2][R, 2 * r + 1], init, ALU.add, op)
                last.then_inc(sums_ready, 1)

            def add(c):
                v.wait_ge(values_full, c + 1)
                t = slice(c * TPC, (c + 1) * TPC)
                v.tensor_tensor(X[:, t], X[:, t], PS[:, OUT_BANKS + c % 2, :].rearrange("p (t d) -> p t d", d=D),
                                ALU.add).then_inc(values_added, 1)

            def stats(c):
                v.wait_ge(values_added, c + 1)
                dve_stats(v, link, range(c * TPC, (c + 1) * TPC))

            sum_squares(0)
            unit(0)
            for c in range(1, NCH):
                unit(c)
                sums(c - 1)
                if c >= 3:
                    add(c - 3)
                    stats(c - 3)
            v.wait_ge(unit_ready, NCH)
            v.wait_ge(sums_ready, NCH - 2)
            link(b_times(v, NCH - 1))
            sums(NCH - 1)
            add(NCH - 3)
            stats(NCH - 3)
            b_unbind(v, link, NCH - 1)
            for c in (NCH - 2, NCH - 1):
                add(c)
                stats(c)
            v.nop().then_inc(x_ready, 1)

        def b_times(eng, c):
            R = slice(0, NB)
            k, w, to = QF[c % 3][R, 1], QF[c % 3][R, 2], KV[c % 2]
            eng.tensor_tensor(to[R, 0:2], k, w, ALU.mult)
            eng.tensor_tensor(to[R, 2], k[:, 0], w[:, 1], ALU.mult)
            return eng.tensor_tensor(to[R, 3], k[:, 1], w[:, 0], ALU.mult)

        def b_unbind(eng, link, c):
            R = slice(0, NB)
            b, h = divmod(c, S // CH)
            cs, ts = slice(h * CH, (h + 1) * CH), slice(c * CH, (c + 1) * CH)
            q = QF[c % 3][R, 0]
            eng.wait_ge(sums_ready, c + 1)
            if c:
                eng.wait_ge(y_ready, c)
            link.open(eng.tensor_tensor(PRB[R, 0:2], CUM[R, :, b, cs], q, ALU.mult))
            link.open(eng.tensor_tensor(PRB[R, 2], CUM[R, 1, b, cs], q[:, 0], ALU.mult))
            link(eng.tensor_tensor(PRB[R, 3], CUM[R, 0, b, cs], q[:, 1], ALU.mult))
            link.open(eng.tensor_tensor(YF[R, 0, ts], PRB[R, 0], PRB[R, 1], ALU.add))
            eng.tensor_tensor(YF[R, 1, ts], PRB[R, 2], PRB[R, 3], ALU.subtract).then_inc(y_ready, 1)
            link.close()

        def b_gpsimd(pool, link):
            def times(c):
                pool.wait_ge(unit_ready, c + 1)
                if c >= 2:
                    pool.wait_ge(sums_ready, c - 1)
                b_times(pool, c).then_inc(kv_ready, 1)

            times(0)
            for c in range(1, NCH - 1):
                times(c)
                b_unbind(pool, link, c - 1)
            b_unbind(pool, link, NCH - 2)

        def w_sync(sp):
            for dst, src in ((bw, b_w), (bdft, b_dft), (bidft, b_idft), (fw, f_w), (fn, f_n), (fmid, f_mid),
                             (fdown, f_down), (fwo, f_wo), (frows, f_rows)):
                sp.dma_start(dst[:], src).then_inc(w_loaded, 16)
            sp.dma_start(fqk[:].rearrange("p n d -> p (n d)"), f_qk.partition_broadcast(P)).then_inc(w_loaded, 16)
            sp.dma_start(maskf[:], causal).then_inc(w_loaded, 16)

        W_LOADED = 16 * 11
        ATT = [(buf, qc, kt, heads, c0) for buf in range(2) for qc in range(S // CH) for kt in range(TPC * (qc + 1))
               for c0 in [max(0, kt - TPC * qc) * P]
               for heads in (((0, 1), (2, 3)) if c0 < CH // 2 else ((0, 1, 2, 3),))]
        NA = len(ATT)
        NA_B = NA // 2
        NA_Q0 = len([a for a in ATT if a[0] == 0 and a[1] == 0])
        LAG = 2
        DEPTH = 3
        OBANKS = 2
        SCORES_BANKS = 2 * DEPTH
        ROUTER_BANK = 5
        HT_BANKS = 4
        F_RES = NCH + TILES + 2 * NCH + NCH + NCH + 1

        def f_sync(sp, nth, rep):
            if rep == 0:
                sp.wait_ge(stack_clear, 2 * B)
            first = FIRST_RESULT[nth] + NCH + TILES
            heads = lambda g: slice(g * GH, (g + 1) * GH)
            for b in range(B):
                ts = slice(b * S, (b + 1) * S)
                sp.wait_ge(psum_read, first + (2 if b == 0 else 8))
                sp.dma_start(qs_d[:, QROWS - 1, ts], MT[:, ts]).then_inc(parts_stored, 16)
                done = NCH * rep + NCH // B * (b + 1)
                for part in range(3):
                    if part == 0:
                        sp.wait_ge(part_high, 2 * done)
                    elif part == 1:
                        sp.wait_ge(psum_read, first + (2 + NCH) * (b + 1))
                    else:
                        sp.wait_ge(parts_ready if b else third_parts, (rep + 1) * (NCH // B))
                    for n, (d, side) in enumerate(((qs_d, Q_SIDE), (ks_d, K_SIDE))):
                        for s in range(NSLOT):
                            if side[s] == part:
                                sp.dma_start(d[:, HD * s:HD * (s + 1), ts],
                                             QP[part][:, n, ts]).then_inc(parts_stored, 16)
                sp.wait_ge(parts_stored, PARTS * (rep * B + b + 1))
                for g in range(NG):
                    it = b * NG + g
                    if it >= 2:
                        sp.wait_ge(probs_used, DEPTH + (rep * B * NG + it - 1) * NA_B)
                    sp.dma_start(QS[it % 2][0:QROWS],
                                 qs_d[heads(g), :, ts].rearrange("h r t -> r h t")).then_inc(stack_loaded[it % 2], 16)
                    sp.dma_start(KS[it % 2][0:QROWS - 1],
                                 ks_d[heads(g), 0:QROWS - 1, ts].rearrange("h r t -> r h t")
                                 ).then_inc(stack_loaded[it % 2], 16)

        def third(eng, c):
            return eng.tensor_tensor(QP[2][:, :, c * CH:(c + 1) * CH], QR[c % 2][:], QP[1][:, :, c * CH:(c + 1) * CH],
                                     ALU.subtract)

        PARTS = 16 * (2 * NSLOT + 1)

        def f_gpsimd(pool, link, nth, rep):
            if rep == 0:
                pool.wait_ge(w_loaded, W_LOADED)
                pool.wait_ge(x_ready, nth)
                for b in range(B):
                    pool.memset(KS[b][:], 1.0).then_inc(stack_clear, 1)
                    pool.memset(QS[b][:], 0.0).then_inc(stack_clear, 1)
                    link(pool.memset(VA[b][:], 1.0))
                pool.tensor_copy(maskb[:], maskf[:]).then_inc(stack_clear, 1)
                pool.tensor_copy(identb[:], ident[:]).then_inc(stack_clear, 1)
            pool.wait_ge(psum_read, FIRST_RESULT[nth] + NCH + TILES)

            for c in range(NCH // B):
                pool.wait_ge(psum_read, FIRST_RESULT[nth] + NCH + TILES + 2 + 2 * (c + 1))
                third(pool, c).then_inc(third_parts, 1)

            for it in range(B * NG):
                b, g = divmod(it, NG)
                if it >= 2:
                    pool.wait_ge(probs_used, DEPTH + (rep * B * NG + it - 1) * NA_B)
                src = QKV[:, b * TB:(b + 1) * TB, 2 * D + g * (GH * HD):2 * D + (g + 1) * (GH * HD)]
                pool.tensor_copy(VA[it % 2][:, :, :, HD * g:HD * (g + 1)],
                                 src.rearrange("p t (h d) -> p t h d", d=HD)).then_inc(v_ready, 1)

        def f_tensor(pe, banks, nth, rep):
            base = banks.n
            assert base == FIRST_RESULT[nth]
            if rep == 0:
                pe.sem_inc(probs_used, DEPTH)
            pe.wait_ge(fw_ready, 2)
            pe_transpose_in(pe, banks, SQ, FIRST_NORM[nth])
            banks.all_read()
            for t in range(TILES):
                k = banks.take()
                pe.matmul(PS[:, k, 0:3 * D], HT[:, t * P:(t + 1) * P], fw[:, 0:3 * D], start=True,
                          stop=True).then_inc(psum_full, 1)
            for b in range(B):
                chunks = range(b * (NCH // B), (b + 1) * (NCH // B))
                if b:
                    banks.all_read()
                pe.wait_ge(qk_normed, rep * B + b + 1)
                for c in chunks:
                    for n in range(2):
                        k = banks.take()
                        for i in range(TPC):
                            last = pe.transpose(PS[:, k, i * P:(i + 1) * P], QKS[:, c * TPC + i, n * D:(n + 1) * D],
                                                ident[:])
                        last.then_inc(psum_full, 1)
                pe.wait_ge(shifts_ready, rep * B + b + 1)
                for c in chunks:
                    k = banks.take()
                    for i in range(TPC):
                        last = pe.transpose(PS[0:H, k, i * P:(i + 1) * P], qst2[:, c * TPC + i, 0:H], ident[:])
                    last.then_inc(psum_full, 1)
            banks.all_read()
            pe.wait_ge(stack_clear, 2 * B + 2)
            with pe.Fori(0, NG) as g:
                n = rep * NG + g
                for u in range(NA + LAG):
                    if u < NA:
                        b, qc, kt, heads, c0 = ATT[u]
                        if u % NA_B == 0:
                            pe.wait_ge(stack_loaded[b], 32 * (n + 1))
                            pe.wait_ge(v_ready, n * B + b + 1)
                        pe.wait_ge(probs_ready, n * NA + u + 1)
                        diag = kt >= TPC * qc
                        for i, h in enumerate(heads):
                            k, at = 2 * (u % DEPTH) + i % 2, i // 2 * (CH // 2)
                            last = pe.matmul(PS[:, k, at:at + CH - c0], KS[b][:, h, kt * P:(kt + 1) * P],
                                             QS[b][:, h, qc * CH + c0:(qc + 1) * CH], start=True, stop=True)
                            if diag:
                                last = pe.matmul(PS[:, k, at:at + P], identb[:], maskb[:], start=False, stop=True,
                                                 skip_group_check=True)
                        last.then_inc(scores_ready, 1)
                    if u >= LAG:
                        w = u - LAG
                        b, qc, kt, heads, c0 = ATT[w]
                        pe.wait_ge(probs_ready, DEPTH + n * NA + w + 1)
                        if kt == 0 and heads[0] == 0:
                            pe.wait_ge(o_read, (n * B + b) * 2 + qc + 1)
                        for i, h in enumerate(heads):
                            at = i // 2 * (CH // 2)
                            last = pe.matmul(PS[32 * h:32 * h + 32, SCORES_BANKS + qc, c0:CH], VA[b][:, kt, h, :],
                                             PX[w % DEPTH][:, i % 2, at:at + CH - c0], start=(kt == 0),
                                             stop=(kt >= TPC * qc), skip_group_check=True)
                        last.then_inc(probs_used, 1)
            for c in range(NCH):
                if c % (NCH // B) == 0:
                    pe.wait_ge(heads_added, (rep * B + c // (NCH // B) + 1) * (NG - 1) * 2)
                for i in range(TPC):
                    t = (c * TPC + i) * P
                    last = pe.matmul(PS[:, c, i * OUTC:(i + 1) * OUTC], AO[:, t:t + P], fwo[:], start=True, stop=True)
                last.then_inc(proj_full, 1)
            pe_transpose_in(pe, banks, SQ, FIRST_NORM[nth] + 1, range(NCH // B), HT_BANKS)
            banks.all_read()
            rhs = lambda c: HT[:, c * CH:(c + 1) * CH]

            def up(c, bank, col, halves=2):
                for m in range(halves):
                    last = pe.matmul(PS[:, bank + m, :], fw[:, col + m * P:col + (m + 1) * P], rhs(c),
                                     start=True, stop=True)
                last.then_inc(up_full, 1)

            up(0, 0, F_E1A)
            pe_transpose_in(pe, banks, SQ, FIRST_NORM[nth] + 1, range(NCH // B, NCH), HT_BANKS)
            up(0, 2, F_E1B)
            banks.all_read()
            banks.n += 1
            for t in range(TILES):
                last = pe.matmul(PS[:, ROUTER_BANK, t * E4:(t + 1) * E4], HT[:, t * P:(t + 1) * P],
                                 fw[:, F_GATE:F_GATE + E4], start=True, stop=True)
            last.then_inc(psum_full, 1)
            assert banks.n == base + F_RES
            hidden = rep * UPS
            gated = rep * NCH
            tiles = rep * 2 * TILES

            def mid(bank, w, parts):
                for m in range(2):
                    for k, h in enumerate(parts):
                        last = pe.matmul(PS[:, bank + m, :], fmid[:, w + k, m * P:(m + 1) * P], h,
                                         start=(k == 0), stop=(k == len(parts) - 1))
                last.then_inc(up_full, 1)

            def down1(c):
                pe.wait_ge(h1_ready, gated + c + 1)
                if c >= 2:
                    pe.wait_ge(down_read, tiles + (c - 1) * TPC)
                for t in range(TPC):
                    for m in range(2):
                        last = pe.matmul(PS[:, 6 + c % 2, t * OUTC:(t + 1) * OUTC], HG[c % 2][:, m, t * P:(t + 1) * P],
                                         fdown[:, 1, m, :], start=(m == 0), stop=(m == 1))
                last.then_inc(down_full, 1)

            def down(c):
                pe.wait_ge(up_read, hidden + NCH + 6 * (c + 1))
                for t in range(TPC):
                    pe.wait_ge(down_read, tiles + TILES + c * TPC + t - (1 if c or t else 0))
                    for j, (e, h) in enumerate(((0, H0[c % 2]), (2, HC), (3, HF))):
                        for m in range(2):
                            last = pe.matmul(PS[:, 6 + t % 2, j * OUTC:(j + 1) * OUTC], h[:, m, t * P:(t + 1) * P],
                                             fdown[:, e, m, :], start=(m == 0), stop=(m == 1))
                    last.then_inc(down_full, 1)

            for c in range(NCH):
                if c:
                    pe.wait_ge(up_read, hidden + c)
                    up(c, 0, F_E1A)
                    pe.wait_ge(h1_ready, gated + c)
                    up(c, 2, F_E1B)
                    down1(c - 1)
            pe.wait_ge(up_read, hidden + NCH)
            pe.wait_ge(h1_ready, gated + NCH)
            banks.all_read()
            for c in range(NCH):
                seen = hidden + NCH + 6 * c
                up(c, 0, F_E2)
                up(c, 2, F_E0)
                if c:
                    pe.wait_ge(up_read, seen)
                up(c, 4, F_E3, 1)
                if c == 0:
                    down1(NCH - 1)
                else:
                    down(c - 1)
                pe.wait_ge(up_read, seen + 1)
                mid(0, 0, [HA[:, k, :] for k in range(2)])
                pe.wait_ge(up_read, seen + 3)
                mid(2, 4, [HE[:]])
                pe.wait_ge(up_read, seen + 4)
                mid(4, 2, [HB[:, k, :] for k in range(2)])
                pe.wait_ge(up_read, seen + 5)
            down(NCH - 1)

        UPS = NCH + 6 * NCH

        def f_scalar(act, link, ask, reads, nth, rep):
            if rep == 0:
                act.sem_inc(probs_ready, DEPTH)
            act_sqrt(act, ask, stat[:])
            act_sqrt(act, ask, stat[:])
            act_ht(act, reads)
            for t in range(TILES):
                k = reads.next()
                act.activation(QKS[:, t, :], PS[:, k, 0:2 * D], ACT.Square)
                act.activation(QKV[:, t, :], PS[:, k, 0:3 * D], ACT.Copy).then_inc(psum_read, 1)
                if t == TB + TPC - 1:
                    act_sqrt(act, ask, qst[:, 0:TB])

            def q_squares(b):
                act.wait_ge(qk_normed, rep * B + b + 1)
                act.activation(QQ[b], QKS[:, b * TB:(b + 1) * TB, 0:D], ACT.Square).then_inc(q_squared, 1)

            def q_root(b):
                act_sqrt(act, ask, qst[:, b * TB:(b + 1) * TB, H:2 * H])

            def high(c):
                for n in range(2):
                    k = reads.next()
                    act.activation(QP[0][:, n, c * CH:(c + 1) * CH], PS[:, k, :], ACT.Copy).then_inc(part_high, 1)

            def mid(c):
                act.wait_ge(rest_ready, 2 * (rep * NCH + c + 1))
                act.activation(QP[1][:, :, c * CH:(c + 1) * CH], QR[c % 2][:], ACT.Copy).then_inc(psum_read, 2)

            def shifts(c):
                k = reads.next()
                act.activation(MT[:, c * CH:(c + 1) * CH], PS[0:H, k, :], ACT.Copy).then_inc(psum_read, 1)

            q_squares(0)
            high(0)
            q_root(0)
            high(1)
            act_sqrt(act, ask, qst[:, TB:2 * TB])
            shifts(0)
            shifts(1)
            mid(0)
            mid(1)
            q_squares(1)
            high(2)
            q_root(1)
            high(3)
            shifts(2)
            shifts(3)
            mid(2)
            mid(3)
            with act.Fori(0, NG) as g:
                n = rep * NG + g
                for u in range(NA):
                    heads, c0 = ATT[u][3:]
                    halves = len(heads) // 2
                    tile = lambda t: t.rearrange("p k (n q) -> p k n q", n=halves)[:, :, :, 0:CH - c0]
                    k = 2 * (u % DEPTH)
                    act.wait_ge(scores_ready, n * NA + u + 1)
                    act.wait_ge(probs_used, n * NA + u + 1)
                    act.activation(tile(PX[u % DEPTH][:]), tile(PS[:, k:k + 2, :]), ACT.Exp).then_inc(probs_ready, 1)
            for b in range(B):
                act_sqrt(act, ask, stat[:, b * TB:(b + 1) * TB])
                act_ht(act, reads, range(b * (NCH // B), (b + 1) * (NCH // B)), HT_BANKS)
            hidden = rep * 8 * NCH
            for c in range(NCH):
                if c == 1:
                    reads.n += 1
                    ask.wait()
                    act.activation(pr[:], lg[:], ACT.Exp).then_inc(to_dve, 1)
                act.wait_ge(up_full, hidden + 2 * c + 1)
                if c >= 2:
                    act.wait_ge(h1_ready, rep * NCH + c - 1)
                act.activation(HS[c % 2][:], PS[:, 0:2, :], ACT.Silu).then_inc(up_read, 1)
            for c in range(NCH):
                for j, (bank, w, h) in enumerate(((0, 2, HA), (2, 2, H0[c % 2]), (4, 1, HE),
                                                  (0, 2, HB), (2, 2, HF), (4, 2, HC))):
                    act.wait_ge(up_full, hidden + 2 * NCH + 6 * c + j + 1)
                    src = PS[:, bank:bank + 2, :] if w == 2 else PS[:, bank, :]
                    act.activation(h[:], src, ACT.Gelu).then_inc(up_read, 1)

        def w_vector(v, link):
            v.wait_ge(w_loaded, W_LOADED)
            v.tensor_scalar(fw[:, 0:3 * D], fw[:, 0:3 * D], fn[:, 0:1], None, ALU.mult).then_inc(fw_ready, 1)
            v.tensor_scalar(fw[:, 3 * D:], fw[:, 3 * D:], fn[:, 1:2], None, ALU.mult).then_inc(fw_ready, 1)
            link(v.tensor_tensor(fqk[:, 0], fqk[:, 0], fqk[:, 1], ALU.mult))
            link(v.tensor_scalar(fqk[:, 0], fqk[:, 0], HD ** -0.5, None, ALU.mult))

        def f_vector(v, link, ans, nth, rep):
            base = FIRST_RESULT[nth]
            v.wait_ge(x_ready, nth)
            if rep == 0:
                v.sem_inc(o_read, OBANKS)
            dve_norm(v, link, ans, LN_EPS, SQ, F_EPS)
            def q_k_squares(b):
                tb = slice(b * TB, (b + 1) * TB)
                v.wait_ge(psum_read, base + NCH + TB * (b + 1))
                to = QKS[:, tb].rearrange("p t (n d) -> p t n d", d=HD)
                link(v.tensor_reduce(qst[:, tb], to, AX.X, ALU.add))
                v.tensor_scalar(qst[:, tb], qst[:, tb], 1.0 / HD, F_EPS, ALU.mult, ALU.add).then_inc(to_act, 1)

            def q_k_normed(b):
                tb = slice(b * TB, (b + 1) * TB)
                qk = QKV[:, tb, 0:2 * D].rearrange("p t (n d) -> p t n d", d=HD)
                to = QKS[:, tb].rearrange("p t (n d) -> p t n d", d=HD)
                ans.wait()
                link(v.reciprocal(qst2[:, tb], qst[:, tb]))
                link(v.tensor_tensor(to, qk, bcast(qst2[:, tb], 3, HD), ALU.mult))
                q = QKS[:, tb, 0:D].rearrange("p t (h d) -> p t h d", d=HD)
                v.tensor_tensor(q, q, bcast(bcast(fqk[:, 0], 1, H), 1, TB), ALU.mult).then_inc(qk_normed, 1)
                v.wait_ge(qk_normed, rep * B + b + 1)
                q, k = QKS[:, tb, 0:D], QKS[:, tb, D:2 * D]
                sq = SQ[:, tb]
                heads = sq.rearrange("p t (h d) -> p t h d", d=HD)
                link(v.tensor_tensor(sq, q, k, ALU.mult))
                link(v.tensor_reduce(qst[:, tb, 0:H], heads, AX.X, ALU.add))
                v.wait_ge(q_squared, rep * B + b + 1)
                v.tensor_reduce(qst[:, tb, H:2 * H], QQ[b].rearrange("p t (h d) -> p t h d", d=HD),
                                AX.X, ALU.add).then_inc(to_act, 1)
                ans.wait()
                link(v.tensor_scalar(qst[:, tb, H:2 * H], qst[:, tb, H:2 * H], HD ** 0.5, -SHIFT, ALU.mult, ALU.add))
                link(v.tensor_tensor(qst2[:, tb, 0:H], qst[:, tb, 0:H], qst[:, tb, H:2 * H], ALU.max))
                v.tensor_scalar(qst2[:, tb, 0:H], qst2[:, tb, 0:H], -1.0, None, ALU.mult).then_inc(shifts_ready, 1)

            def q_k_parts(b):
                if b:
                    v.wait_ge(third_parts, (rep + 1) * (NCH // B))
                chunks = range(b * (NCH // B), (b + 1) * (NCH // B))
                for c in chunks:
                    for n in range(2):
                        r = base + NCH + TILES + 2 * b + 2 * c + n
                        v.wait_ge(part_high, (rep * NCH + c) * 2 + n + 1)
                        v.tensor_tensor(QR[c % 2][:, n], PS[:, r % 8, :], QP[0][:, n, c * CH:(c + 1) * CH],
                                        ALU.subtract).then_inc(rest_ready, 1)
                if b:
                    for c in chunks:
                        v.wait_ge(psum_read, base + NCH + TILES + 2 * (b + 1) + 2 * (c + 1))
                        third(v, c).then_inc(parts_ready, 1)

            q_k_squares(0)
            q_k_normed(0)
            q_k_squares(1)
            q_k_parts(0)
            q_k_normed(1)
            q_k_parts(1)
            for t in range(TILES):
                link.open(center_and_scale(v, XL, t, rstd))
            link.close()
            added = 2 * (NG - 1) * B * rep
            for it in range(B * NG):
                b, g = divmod(it, NG)
                for qc in range(2):
                    at = (rep * B * NG + it) * 2 + qc
                    o = PS[:, SCORES_BANKS + qc, :]
                    t = b * S + qc * CH
                    v.wait_ge(probs_used, DEPTH + (rep * B * NG + it) * NA_B + (NA_Q0 if qc == 0 else NA_B))
                    v.wait_ge(o_read, OBANKS + at)
                    if added:
                        v.wait_ge(heads_added, added)
                    v.stream_shuffle(DEN[:], o, [HD * (g + 1) % 32] * 32).then_inc(den_ready, 1)
                    v.wait_ge(den_ready, 2 * at + 1)
                    v.reciprocal(DEN[:], DEN[:]).then_inc(den_ready, 1)
                    v.wait_ge(den_ready, 2 * at + 2)
                    v.scalar_tensor_tensor(out=DEN[:] if g else AO[:, t:t + CH], in0=o, scalar=frows[:, g:g + 1],
                                           in1=DEN[:], op0=ALU.mult, op1=ALU.mult).then_inc(o_read, 1)
                    if g:
                        v.wait_ge(o_read, OBANKS + at + 1)
                        v.tensor_tensor(AO[:, t:t + CH], AO[:, t:t + CH], DEN[:], ALU.add).then_inc(heads_added, 1)
                        added += 1
            first = base + NCH + TILES + 3 * NCH
            for b in range(B):
                for c in range(b * (NCH // B), (b + 1) * (NCH // B)):
                    v.wait_ge(proj_full, rep * NCH + c + 1)
                    t = slice(c * TPC, (c + 1) * TPC)
                    v.tensor_tensor(XL[:, t, KEEP:], XL[:, t, KEEP:],
                                    PS[:, c, 0:TPC * OUTC].rearrange("p (t d) -> p t d", d=OUTC),
                                    ALU.add).then_inc(proj_added, 1)
                v.wait_ge(proj_added, rep * NCH + NCH // B * (b + 1))
                tb = slice(b * TB, (b + 1) * TB)
                link(v.tensor_tensor(SQ[:, tb], XL[:, tb], XL[:, tb], ALU.mult))
                link(v.tensor_reduce(stat[:, tb], SQ[:, tb], AX.X, ALU.add))
                v.tensor_scalar(stat[:, tb], stat[:, tb], 1.0 / D, F_EPS, ALU.mult, ALU.add).then_inc(to_act, 1)
                ans.wait()
                link(v.reciprocal(rrms[:, tb], stat[:, tb]))
                v.tensor_tensor(SQ[:, tb], XL[:, tb], bcast(rrms[:, tb], 2, D), ALU.mult).then_inc(normed, 1)
            v.tensor_tensor(X[:], X[:], XL[:], ALU.add).then_inc(x_sum, 1)

            def gate(c):
                v.wait_ge(up_read, rep * UPS + c + 1)
                v.wait_ge(up_full, rep * 8 * NCH + 2 * c + 2)
                v.tensor_tensor(HG[c % 2][:], HS[c % 2][:], PS[:, 2:4, :], ALU.mult).then_inc(h1_ready, 1)

            gate(0)
            first += NCH
            v.wait_ge(psum_full, first + 1)
            v.tensor_scalar(lg[:].rearrange("p t e -> p (t e)"), PS[:, ROUTER_BANK, 0:TILES * E4], FLT_MAX, -FLT_MAX,
                            ALU.min, ALU.max).then_inc(psum_read, 1)
            v.wait_ge(psum_read, first + 1)
            link(v.tensor_reduce(red[:], lg[:], AX.X, ALU.max))
            v.tensor_tensor(lg[:], lg[:], bcast(red[:], 2, E4), ALU.subtract).then_inc(to_act, 1)
            ans.wait()
            link(v.tensor_reduce(red[:], pr[:], AX.X, ALU.add))
            link(v.reciprocal(red[:], red[:]))
            link.open(v.tensor_tensor(pr[:], pr[:], bcast(red[:], 2, E4), ALU.mult))
            link(v.memset(cnt[:], 0.0))
            for i in range(E4):
                for j in range(i):
                    link(v.tensor_tensor(ge[:], pr[:, :, j], pr[:, :, i], ALU.is_ge))
                    link.open(v.tensor_tensor(cnt[:, :, i], cnt[:, :, i], ge[:], ALU.add))
                    link(v.tensor_scalar(red[:], ge[:], -1.0, 1.0, ALU.mult, ALU.add))
                    link(v.tensor_tensor(cnt[:, :, j], cnt[:, :, j], red[:], ALU.add))
            link(v.tensor_scalar(cnt[:], cnt[:], 2.0, None, ALU.is_lt))
            link(v.tensor_tensor(wts[:], pr[:], cnt[:], ALU.mult))
            link(v.tensor_reduce(red[:], wts[:], AX.X, ALU.add))
            link(v.tensor_scalar(red[:], red[:], TOP_EPS, None, ALU.add))
            link(v.reciprocal(red[:], red[:]))
            link(v.tensor_tensor(wts[:], wts[:], bcast(red[:], 2, E4), ALU.mult))
            v.wait_ge(x_sum, rep + 1)

            def add_expert(tile, e, src):
                xt = X[:, tile, KEEP:]
                return v.scalar_tensor_tensor(out=xt, in0=src, scalar=wts[:, tile, e:e + 1], in1=xt,
                                              op0=ALU.mult, op1=ALU.add)

            chunks = rep * (NCH + TILES)

            def add1(c):
                v.wait_ge(down_full, chunks + c + 1)
                for t in range(TPC):
                    add_expert(c * TPC + t, 1, PS[:, 6 + c % 2, t * OUTC:(t + 1) * OUTC]).then_inc(down_read, 1)

            for c in range(1, NCH):
                gate(c)
                add1(c - 1)
            add1(NCH - 1)
            v.wait_ge(down_read, rep * 2 * TILES + TILES)
            for t in range(TILES):
                v.wait_ge(down_full, chunks + NCH + t + 1)
                for j, e in enumerate((0, 2, 3)):
                    ins = add_expert(t, e, PS[:, 6 + t % 2, j * OUTC:(j + 1) * OUTC])
                    if j < 2:
                        link(ins)
                    else:
                        ins.then_inc(down_read, 1)
                if nth + 1 < len(LAYERS) and t % TPC == TPC - 1:
                    v.wait_ge(down_read, rep * 2 * TILES + TILES + t + 1)
                    dve_stats(v, link, range(t + 1 - TPC, t + 1))
            v.wait_ge(down_read, (rep + 1) * 2 * TILES)
            v.nop().then_inc(x_ready, 1)

        LAYERS = 'AFBF'
        RESULTS = {"A": A_RES, "B": B_RES, "F": F_RES}
        NORMS = {"A": 1, "B": 1, "F": 2}
        FIRST_RESULT = [sum(RESULTS[l] for l in LAYERS[:n]) for n in range(len(LAYERS))]
        FIRST_NORM = [sum(NORMS[l] for l in LAYERS[:n]) for n in range(len(LAYERS))]
        block = ctx.enter_context(nc.Block())

        @block.sync
        def _(sp):
            a_sync(sp)
            for n, layer in enumerate(LAYERS):
                if layer == "F":
                    f_sync(sp, n, LAYERS[:n].count("F"))
            sp.wait_ge(x_ready, len(LAYERS))
            sp.dma_start(out.rearrange("(t p) d -> p t d", p=P), X[:]).then_inc(out_stored, 16)
            sp.wait_ge(out_stored, 16)

        @block.tensor
        def _(pe):
            banks = Banks(pe)
            for n, layer in enumerate(LAYERS):
                if layer == "A":
                    a_tensor(pe, banks)
                elif layer == "B":
                    b_tensor(pe, banks, n)
                else:
                    f_tensor(pe, banks, n, LAYERS[:n].count("F"))

        @block.scalar
        def _(act):
            link, ask, reads = Chain(act, act_chain), Tally(act, to_act), Reads(act)
            for n, layer in enumerate(LAYERS):
                if layer == "A":
                    a_scalar(act, link, ask, reads)
                elif layer == "B":
                    b_scalar(act, link, ask, reads)
                else:
                    f_scalar(act, link, ask, reads, n, LAYERS[:n].count("F"))

        @block.vector
        def _(v):
            link, ans = Chain(v, dve_chain), Tally(v, to_dve)
            for n, layer in enumerate(LAYERS):
                if layer == "A":
                    a_vector(v, link, ans)
                elif layer == "B":
                    b_vector(v, link, ans, n)
                else:
                    f_vector(v, link, ans, n, LAYERS[:n].count("F"))

        @block.gpsimd
        def _(pool):
            link = Chain(pool, pool_chain)
            for n, layer in enumerate(LAYERS):
                if layer == "A":
                    a_gpsimd(pool, link)
                elif layer == "B":
                    b_gpsimd(pool, link)
                else:
                    f_gpsimd(pool, link, n, LAYERS[:n].count("F"))


def dft_tables():
    import numpy as np
    n = np.arange(D)[:, None]
    f = np.arange(NB)[None, :]
    turn = (n * f) % D
    cos = np.cos(2 * np.pi * turn / D)
    sin = np.sin(2 * np.pi * turn / D)
    sin[(2 * turn) % D == 0] = 0.0
    weight = np.where((f == 0) | (f == D // 2), 1.0, 2.0) / D
    forward = np.stack([cos, -sin], 1).astype(np.float32)
    back = np.zeros((P, 2, D), np.float32)
    back[:NB, 0] = (weight * cos).T
    back[:NB, 1] = (-weight * sin).T
    return forward, back


def kernel(**inputs):
    import numpy as np
    import concourse.bacc as bacc
    from concourse.bass_utils import run_bass_kernel_spmd as run

    g = {k: np.asarray(v) for k, v in inputs.items()}
    a = lambda name: g["L0_attn_a_" + name]
    f = lambda name: g["L0_ffn_" + name]
    W, bias = a("W_ctrl"), a("b_ctrl")
    ug, ang, cand, q, k, v, al, be, og = np.split(np.arange(W.shape[1]), np.cumsum([D, D // 2, D, D, D, D, H, H]))
    pick = np.concatenate([q, k, v, ug[0::2], ug[1::2], cand[0::2], cand[1::2], ang, og])
    a_w = W[:, pick]
    a_wab = np.zeros((D, 4, BH), np.float32)
    for w, cols in enumerate((al, be)):
        for b in range(B):
            a_wab[:, 2 * w + b, b * H:(b + 1) * H] = W[:, cols]
    two = lambda t: np.concatenate([t, t])
    small = [bias[q], bias[k], bias[v]]
    small += [a(n)[:, j] for n in ("qconv_w", "kconv_w", "vconv_w") for j in range(4)]
    small += [two(bias[c]) for c in (ug[0::2], ug[1::2], cand[0::2], cand[1::2], ang)]
    small += [two(a("W_block")[:, i, j]) for i in range(2) for j in range(2)]
    small += [np.tile(bias[al], SEG * B), np.tile(bias[be], SEG * B)]
    small += [np.tile(a("rms_m_w"), H), two(a("rms_v_w")[0::2]), two(a("rms_v_w")[1::2])]
    W_out = a("W_out")
    forward, back = dft_tables()
    b_w = np.stack([g["L0_attn_b_W" + n] for n in "qkv"], 1)
    down = lambda n: f(n).T[:, KEEP:].reshape(2, P, OUTC).transpose(1, 0, 2)
    mid = lambda n: f(n).T.reshape(2, P, HID).transpose(1, 0, 2)
    wo = f("wo").T[:, KEEP:].reshape(NG, GH, HD, OUTC).transpose(1, 0, 2, 3).reshape(P, OUTC)
    rows = np.tile(np.repeat(np.eye(NG, dtype=np.float32), HD, 0), (GH, 1))
    arrays = {
        "x": a("hidden").reshape(NT, D), "a_w": a_w, "a_wab": a_wab, "a_small": np.stack(small, 1),
        "a_conv": np.concatenate([a(n).T.reshape(-1) for n in ("qconv_w", "kconv_w", "vconv_w")]),
        "a_bog": bias[og], "a_bout": a("b_out"),
        "a_wout": np.stack([W_out[:D], two(W_out[D::2]), two(W_out[D + 1::2])], 1),
        "b_w": b_w, "b_dft": forward, "b_idft": back,
        "f_w": np.concatenate([f(n).T for n in ("wq", "wk", "wv", "gate_w", "e0_up", "e1_w1", "e1_w2", "e2_l1",
                                                "e3_down")], 1),
        "f_n": np.stack([f("n1_w"), f("n2_w")], 1), "f_qk": np.concatenate([f("qn_w"), f("kn_w")]),
        "f_mid": np.concatenate([mid("e2_l2"), mid("e2_l3"), f("e3_up").T[:, None]], 1),
        "f_down": np.stack([down(n) for n in ("e0_down", "e1_down", "e2_l4", "e3_out")], 1),
        "f_wo": wo, "f_rows": rows, "eye": np.eye(P, dtype=np.float32),
        "causal": np.where(np.arange(P)[:, None] > np.arange(P)[None, :], MASKED, 0.0).astype(np.float32),
    }
    nc = bacc.Bacc("TRN2", target_bir_lowering=False, num_devices=1)
    arrays = {n: np.ascontiguousarray(t) for n, t in arrays.items()}
    args = {n: nc.dram_tensor(n, t.shape, F32, kind="ExternalInput").ap() for n, t in arrays.items()}
    out = nc.dram_tensor("out", (NT, D), F32, kind="ExternalOutput").ap()
    hybrid_kernel(nc, out=out, **args)
    got = run(nc, [arrays], core_ids=[0]).results[0]["out"]
    return got.reshape(B, S, D)
```
